# Optimizing a Trainium2 kernel written in Bass

```python
import numpy as np
import jax
import jax.numpy as jnp

def _softmax(x, axis=-1):
    return jax.nn.softmax(x, axis=axis)

def _gelu(x):
    return jax.nn.gelu(x, approximate=True)

def _silu(x):
    return jax.nn.silu(x)

def _sigmoid(x):
    return jax.nn.sigmoid(x)

def _layernorm(x, axis=-1, eps=1e-05):
    m = jnp.mean(x, axis=axis, keepdims=True)
    v = jnp.var(x, axis=axis, keepdims=True)
    return (x - m) / jnp.sqrt(v + eps)

def _scatter_add(tgt, idx, src, axis=0):
    return tgt.at[idx].add(src)

def _segment_sum(src, seg, n):
    return jax.ops.segment_sum(src, seg, n)
kernel_name = 'mk_xattn_seq_d4_seqx_r4_85a322'

def setup_inputs(seed: int=0):
    np.random.seed(seed)
    _w = jnp.asarray

    def _rec_inputs():
        import jax
        import jax.numpy as jnp
        _rk = jax.random.key(seed)
        x = -0.0001233 + 1 * jax.random.normal(jax.random.fold_in(_rk, 1), (8, 112, 320), jnp.float32)
        _lenS = 112 - jax.random.randint(jax.random.fold_in(_rk, 7), (8,), 0, max(1, 112 // 4) + 1, jnp.int32)
        _lenS2 = 375 - jax.random.randint(jax.random.fold_in(_rk, 8), (8,), 0, max(1, 375 // 4) + 1, jnp.int32)
        _ctx_2048P = jax.random.normal(jax.random.fold_in(_rk, 11), (8, 16, 512), jnp.float32)
        _ctx_2048c = jax.random.dirichlet(jax.random.fold_in(_rk, 511), 0.3 * jnp.ones((16,), jnp.float32), (8, 375))
        _ctx_2048t = jnp.einsum('bsk,bkd->bsd', _ctx_2048c, _ctx_2048P)
        _ctx_2048t = _ctx_2048t * jax.lax.rsqrt(jnp.mean(jnp.square(_ctx_2048t)) + 1e-12) * 0.953939
        ctx_2048 = 0.00266749 + 0.998873 * (_ctx_2048t + 0.3 * jax.random.normal(jax.random.fold_in(_rk, 611), (8, 375, 512), jnp.float32))
        fside_Bx4x4_0 = jax.random.uniform(jax.random.fold_in(_rk, 12), (8, 4, 4), jnp.float32, 0.0, 0.981965)
        fside_S_0 = jax.random.uniform(jax.random.fold_in(_rk, 13), (112,), jnp.float32, 0.0, 0.999706)
        return (x, ctx_2048, fside_Bx4x4_0, fside_S_0)
    x, ctx_2048, fside_Bx4x4_0, fside_S_0 = _rec_inputs()

    def _L0_xattn_setup():
        import jax, jax.numpy as jnp
        import numpy as np
        B, S, C = (2, 1024, 320)
        CA = 512
        HEADS = 20
        HD = C // HEADS
        N_TXT, N_OBJ, N_OTH, N_IP = (77, 4, 4, 16)
        SCALE_OBJ = SCALE_OTH = SCALE_IP = 1.0
        RESCALE = 1.0

        def _heads(x):
            b, l, _ = x.shape
            return x.reshape(b, l, HEADS, HD).transpose(0, 2, 1, 3)

        def _merge(x):
            b, h, l, d = x.shape
            return x.transpose(0, 2, 1, 3).reshape(b, l, h * d)

        def _sdpa(q, k, v):
            scale = 1.0 / np.sqrt(HD).astype(np.float32)
            s = jnp.einsum('bhqd,bhkd->bhqk', q, k) * scale
            p = jax.nn.softmax(s, axis=-1)
            return jnp.einsum('bhqk,bhkd->bhqd', p, v)
        key = jax.random.key(seed)
        ks = jax.random.split(key, 16)
        g = lambda k, shp, fan: jax.random.normal(k, shp, jnp.float32) / np.sqrt(fan).astype(np.float32)
        return {'hidden_states': jax.random.normal(ks[0], (B, S, C), jnp.float32), 'encoder_hidden_states': jax.random.normal(ks[1], (B, N_TXT + N_OBJ + N_OTH + N_IP, CA), jnp.float32), 'to_q_w': g(ks[2], (C, C), C), 'to_k_w': g(ks[3], (CA, C), CA), 'to_v_w': g(ks[4], (CA, C), CA), 'to_k_object_w': g(ks[5], (CA, C), CA), 'to_v_object_w': g(ks[6], (CA, C), CA), 'to_k_others_w': g(ks[7], (CA, C), CA), 'to_v_others_w': g(ks[8], (CA, C), CA), 'to_k_ip_w': g(ks[9], (CA, C), CA), 'to_v_ip_w': g(ks[10], (CA, C), CA), 'to_out_w': g(ks[11], (C, C), C), 'to_out_b': jnp.zeros((C,), jnp.float32)}
    _L0_xattn_all = _L0_xattn_setup()
    _L0_xattn_in = {k: v for k, v in _L0_xattn_all.items() if k in ('to_q_w', 'to_k_w', 'to_v_w', 'to_k_object_w', 'to_v_object_w', 'to_k_others_w', 'to_v_others_w', 'to_k_ip_w', 'to_v_ip_w', 'to_out_w', 'to_out_b')}
    del _L0_xattn_all

    def _L1_xattn_setup():
        import jax, jax.numpy as jnp
        import numpy as np
        HEADS = 20
        NUM_IP_TOKENS = 4
        NUM_DUMMY_TOKENS = 4
        IP_SCALE = 1.0
        ASPECT_RATIO = 1.0
        NEG = -10000.0

        def _grid_hw(seq_len, aspect_ratio):
            width = int((seq_len / aspect_ratio) ** 0.5)
            height = seq_len // width
            while width * height != seq_len:
                if width * height < seq_len:
                    width += 1
                else:
                    width -= 1
                height = seq_len // width
            return (height, width)

        def _sdpa(q, k, v, mask=None):
            dh = q.shape[-1]
            scores = jnp.einsum('bhqd,bhkd->bhqk', q, k) / jnp.sqrt(jnp.asarray(dh, q.dtype))
            if mask is not None:
                scores = scores + mask
            probs = jax.nn.softmax(scores, axis=-1)
            return jnp.einsum('bhqk,bhkd->bhqd', probs, v)

        def _split_heads(x, heads):
            b, l, d = x.shape
            return x.reshape(b, l, heads, d // heads).transpose(0, 2, 1, 3)

        def _merge_heads(x):
            b, h, l, dh = x.shape
            return x.transpose(0, 2, 1, 3).reshape(b, l, h * dh)

        def _ip_mask(bbox, batch_size, seq_len, dtype):
            M = bbox.shape[1]
            height, width = _grid_hw(seq_len, ASPECT_RATIO)
            x = jnp.linspace(0.0, 1.0, width, dtype=dtype)
            y = jnp.linspace(0.0, 1.0, height, dtype=dtype)
            yg, xg = jnp.meshgrid(y, x, indexing='ij')
            xg = xg.reshape(-1)
            yg = yg.reshape(-1)
            x1, y1, x2, y2 = (bbox[..., 0:1], bbox[..., 1:2], bbox[..., 2:3], bbox[..., 3:4])
            inside = (xg >= x1) & (xg <= x2) & (yg >= y1) & (yg <= y2)
            ip_mask = jnp.where(inside, 0.0, NEG).astype(dtype)
            ip_mask = jnp.transpose(ip_mask, (0, 2, 1))[:, None]
            ip_mask = jnp.repeat(ip_mask, NUM_IP_TOKENS // M, axis=-1)
            dummy = jnp.where(jnp.any(inside, axis=1), NEG, 0.0).astype(dtype)
            dummy = jnp.repeat(dummy[:, None, :, None], NUM_DUMMY_TOKENS, axis=-1)
            return jnp.concatenate([dummy, ip_mask], axis=-1)
        key = jax.random.key(seed)
        ks = jax.random.split(key, 12)
        B, S, D, C = (4, 1024, 320, 512)
        text_len, M = (77, 4)
        hidden_states = jax.random.normal(ks[0], (B, S, D), jnp.float32)
        encoder_hidden_states = jax.random.normal(ks[1], (B, text_len + NUM_IP_TOKENS + NUM_DUMMY_TOKENS, C), jnp.float32)
        p1 = jax.random.uniform(ks[2], (B, M, 2), jnp.float32)
        p2 = jax.random.uniform(ks[3], (B, M, 2), jnp.float32)
        bbox = jnp.concatenate([jnp.minimum(p1, p2), jnp.maximum(p1, p2)], axis=-1)
        s = 0.02
        w_q = jax.random.normal(ks[4], (D, D), jnp.float32) * s
        w_k = jax.random.normal(ks[5], (C, D), jnp.float32) * s
        w_v = jax.random.normal(ks[6], (C, D), jnp.float32) * s
        w_k_ip = jax.random.normal(ks[7], (C, D), jnp.float32) * s
        w_v_ip = jax.random.normal(ks[8], (C, D), jnp.float32) * s
        w_out = jax.random.normal(ks[9], (D, D), jnp.float32) * s
        b_out = jnp.zeros((D,), jnp.float32)
        return {'hidden_states': hidden_states, 'encoder_hidden_states': encoder_hidden_states, 'bbox': bbox, 'w_q': w_q, 'w_k': w_k, 'w_v': w_v, 'w_k_ip': w_k_ip, 'w_v_ip': w_v_ip, 'w_out': w_out, 'b_out': b_out}
    _L1_xattn_all = _L1_xattn_setup()
    _L1_xattn_in = {k: v for k, v in _L1_xattn_all.items() if k in ('w_q', 'w_k', 'w_v', 'w_k_ip', 'w_v_ip', 'w_out', 'b_out')}
    del _L1_xattn_all

    def _L2_xattn_setup():
        import jax, jax.numpy as jnp
        import numpy as np
        NUM_HEADS = 20
        TEXT_LEN = 77
        IP_SCALE = 1.0

        def _attend(q, k, v, sm_scale):
            scores = jnp.einsum('bhsd,bhld->bhsl', q, k) * sm_scale
            probs = jax.nn.softmax(scores, axis=-1)
            return jnp.einsum('bhsl,bhld->bhsd', probs, v)

        def _split_heads(x, h):
            b, s, c = x.shape
            return x.reshape(b, s, h, c // h).transpose(0, 2, 1, 3)

        def _merge_heads(x):
            b, h, s, d = x.shape
            return x.transpose(0, 2, 1, 3).reshape(b, s, h * d)
        key = jax.random.key(seed)
        ks = jax.random.split(key, 8)
        B, S, C, CC, L = (8, 1024, 320, 512, TEXT_LEN + 4)
        sd_q = 1.0 / np.sqrt(C)
        sd_kv = 1.0 / np.sqrt(CC)
        return {'hidden_states': jax.random.normal(ks[0], (B, S, C), jnp.float32), 'encoder_hidden_states': jax.random.normal(ks[1], (B, L, CC), jnp.float32), 'Wq': jax.random.normal(ks[2], (C, C), jnp.float32) * sd_q, 'Wk': jax.random.normal(ks[3], (C, CC), jnp.float32) * sd_kv, 'Wv': jax.random.normal(ks[4], (C, CC), jnp.float32) * sd_kv, 'Wk_ip': jax.random.normal(ks[5], (C, CC), jnp.float32) * sd_kv, 'Wv_ip': jax.random.normal(ks[6], (C, CC), jnp.float32) * sd_kv, 'Wo': jax.random.normal(ks[7], (C, C), jnp.float32) * sd_q, 'bo': jnp.zeros((C,), jnp.float32)}
    _L2_xattn_all = _L2_xattn_setup()
    _L2_xattn_in = {k: v for k, v in _L2_xattn_all.items() if k in ('Wq', 'Wk', 'Wv', 'Wk_ip', 'Wv_ip', 'Wo', 'bo')}
    del _L2_xattn_all

    def _L3_xattn_setup():
        import jax, jax.numpy as jnp
        import numpy as np
        HEADS = 20
        NUM_TOKENS = 4
        IP_SCALE = 1.0
        SEM_SCALE = 0.5
        RESCALE = 1.0
        EPS = 1e-12

        def _l2norm(x, axis=-1):
            n = jnp.sqrt(jnp.sum(x * x, axis=axis, keepdims=True))
            return x / jnp.maximum(n, EPS)
        key = jax.random.key(seed)
        ks = jax.random.split(key, 10)
        B, S, C = (2, 256, 320)
        T, E = (81, 512)
        inp = {'hidden_states': jax.random.normal(ks[0], (B, S, C), jnp.float32), 'encoder_hidden_states': jax.random.normal(ks[1], (B, T, E), jnp.float32), 'spatial_mask': jax.random.uniform(ks[2], (S,), jnp.float32), 'W_q': jax.random.normal(ks[3], (C, C), jnp.float32) * C ** (-0.5), 'W_k': jax.random.normal(ks[4], (E, C), jnp.float32) * E ** (-0.5), 'W_v': jax.random.normal(ks[5], (E, C), jnp.float32) * E ** (-0.5), 'W_k_ip': jax.random.normal(ks[6], (E, C), jnp.float32) * E ** (-0.5), 'W_v_ip': jax.random.normal(ks[7], (E, C), jnp.float32) * E ** (-0.5), 'W_out': jax.random.normal(ks[8], (C, C), jnp.float32) * C ** (-0.5), 'b_out': jnp.zeros((C,), jnp.float32)}
        return inp
    _L3_xattn_all = _L3_xattn_setup()
    _L3_xattn_in = {k: v for k, v in _L3_xattn_all.items() if k in ('W_q', 'W_k', 'W_v', 'W_k_ip', 'W_v_ip', 'W_out', 'b_out')}
    del _L3_xattn_all
    return {'x': x, 'ctx_2048': ctx_2048, 'fside_Bx4x4_0': fside_Bx4x4_0, 'fside_S_0': fside_S_0, 'L0_xattn_to_q_w': _L0_xattn_in['to_q_w'], 'L0_xattn_to_k_w': _L0_xattn_in['to_k_w'], 'L0_xattn_to_v_w': _L0_xattn_in['to_v_w'], 'L0_xattn_to_k_object_w': _L0_xattn_in['to_k_object_w'], 'L0_xattn_to_v_object_w': _L0_xattn_in['to_v_object_w'], 'L0_xattn_to_k_others_w': _L0_xattn_in['to_k_others_w'], 'L0_xattn_to_v_others_w': _L0_xattn_in['to_v_others_w'], 'L0_xattn_to_k_ip_w': _L0_xattn_in['to_k_ip_w'], 'L0_xattn_to_v_ip_w': _L0_xattn_in['to_v_ip_w'], 'L0_xattn_to_out_w': _L0_xattn_in['to_out_w'], 'L0_xattn_to_out_b': _L0_xattn_in['to_out_b'], 'L1_xattn_w_q': _L1_xattn_in['w_q'], 'L1_xattn_w_k': _L1_xattn_in['w_k'], 'L1_xattn_w_v': _L1_xattn_in['w_v'], 'L1_xattn_w_k_ip': _L1_xattn_in['w_k_ip'], 'L1_xattn_w_v_ip': _L1_xattn_in['w_v_ip'], 'L1_xattn_w_out': _L1_xattn_in['w_out'], 'L1_xattn_b_out': _L1_xattn_in['b_out'], 'L2_xattn_Wq': _L2_xattn_in['Wq'], 'L2_xattn_Wk': _L2_xattn_in['Wk'], 'L2_xattn_Wv': _L2_xattn_in['Wv'], 'L2_xattn_Wk_ip': _L2_xattn_in['Wk_ip'], 'L2_xattn_Wv_ip': _L2_xattn_in['Wv_ip'], 'L2_xattn_Wo': _L2_xattn_in['Wo'], 'L2_xattn_bo': _L2_xattn_in['bo'], 'L3_xattn_W_q': _L3_xattn_in['W_q'], 'L3_xattn_W_k': _L3_xattn_in['W_k'], 'L3_xattn_W_v': _L3_xattn_in['W_v'], 'L3_xattn_W_k_ip': _L3_xattn_in['W_k_ip'], 'L3_xattn_W_v_ip': _L3_xattn_in['W_v_ip'], 'L3_xattn_W_out': _L3_xattn_in['W_out'], 'L3_xattn_b_out': _L3_xattn_in['b_out']}

def reference(x, ctx_2048, fside_Bx4x4_0, fside_S_0, L0_xattn_to_q_w, L0_xattn_to_k_w, L0_xattn_to_v_w, L0_xattn_to_k_object_w, L0_xattn_to_v_object_w, L0_xattn_to_k_others_w, L0_xattn_to_v_others_w, L0_xattn_to_k_ip_w, L0_xattn_to_v_ip_w, L0_xattn_to_out_w, L0_xattn_to_out_b, L1_xattn_w_q, L1_xattn_w_k, L1_xattn_w_v, L1_xattn_w_k_ip, L1_xattn_w_v_ip, L1_xattn_w_out, L1_xattn_b_out, L2_xattn_Wq, L2_xattn_Wk, L2_xattn_Wv, L2_xattn_Wk_ip, L2_xattn_Wv_ip, L2_xattn_Wo, L2_xattn_bo, L3_xattn_W_q, L3_xattn_W_k, L3_xattn_W_v, L3_xattn_W_k_ip, L3_xattn_W_v_ip, L3_xattn_W_out, L3_xattn_b_out):
    import jax
    import jax.numpy as jnp

    def _L0_xattn_ref(hidden_states, encoder_hidden_states, to_q_w, to_k_w, to_v_w, to_k_object_w, to_v_object_w, to_k_others_w, to_v_others_w, to_k_ip_w, to_v_ip_w, to_out_w, to_out_b):
        import jax, jax.numpy as jnp
        import numpy as np
        B, S, C = (2, 1024, 320)
        CA = 512
        HEADS = 20
        HD = C // HEADS
        N_TXT, N_OBJ, N_OTH, N_IP = (77, 4, 4, 16)
        SCALE_OBJ = SCALE_OTH = SCALE_IP = 1.0
        RESCALE = 1.0

        def _heads(x):
            b, l, _ = x.shape
            return x.reshape(b, l, HEADS, HD).transpose(0, 2, 1, 3)

        def _merge(x):
            b, h, l, d = x.shape
            return x.transpose(0, 2, 1, 3).reshape(b, l, h * d)

        def _sdpa(q, k, v):
            scale = 1.0 / np.sqrt(HD).astype(np.float32)
            s = jnp.einsum('bhqd,bhkd->bhqk', q, k) * scale
            p = jax.nn.softmax(s, axis=-1)
            return jnp.einsum('bhqk,bhkd->bhqd', p, v)
        residual = hidden_states
        end = N_TXT
        ehs_txt = encoder_hidden_states[:, :end]
        ehs_obj = encoder_hidden_states[:, end:end + N_OBJ]
        ehs_oth = encoder_hidden_states[:, end + N_OBJ:end + N_OBJ + N_OTH]
        ehs_ip = encoder_hidden_states[:, end + N_OBJ + N_OTH:]
        q = _heads(hidden_states @ to_q_w)
        h_txt = _sdpa(q, _heads(ehs_txt @ to_k_w), _heads(ehs_txt @ to_v_w))
        h_obj = _sdpa(q, _heads(ehs_obj @ to_k_object_w), _heads(ehs_obj @ to_v_object_w))
        h_oth = _sdpa(q, _heads(ehs_oth @ to_k_others_w), _heads(ehs_oth @ to_v_others_w))
        h_ip = _sdpa(q, _heads(ehs_ip @ to_k_ip_w), _heads(ehs_ip @ to_v_ip_w))
        out = _merge(h_txt) + SCALE_OBJ * _merge(h_obj) + SCALE_OTH * _merge(h_oth) + SCALE_IP * _merge(h_ip)
        out = out @ to_out_w + to_out_b
        out = (out + residual) / RESCALE
        return out

    def _L1_xattn_ref(hidden_states, encoder_hidden_states, bbox, w_q, w_k, w_v, w_k_ip, w_v_ip, w_out, b_out):
        import jax, jax.numpy as jnp
        import numpy as np
        HEADS = 20
        NUM_IP_TOKENS = 4
        NUM_DUMMY_TOKENS = 4
        IP_SCALE = 1.0
        ASPECT_RATIO = 1.0
        NEG = -10000.0

        def _grid_hw(seq_len, aspect_ratio):
            width = int((seq_len / aspect_ratio) ** 0.5)
            height = seq_len // width
            while width * height != seq_len:
                if width * height < seq_len:
                    width += 1
                else:
                    width -= 1
                height = seq_len // width
            return (height, width)

        def _sdpa(q, k, v, mask=None):
            dh = q.shape[-1]
            scores = jnp.einsum('bhqd,bhkd->bhqk', q, k) / jnp.sqrt(jnp.asarray(dh, q.dtype))
            if mask is not None:
                scores = scores + mask
            probs = jax.nn.softmax(scores, axis=-1)
            return jnp.einsum('bhqk,bhkd->bhqd', probs, v)

        def _split_heads(x, heads):
            b, l, d = x.shape
            return x.reshape(b, l, heads, d // heads).transpose(0, 2, 1, 3)

        def _merge_heads(x):
            b, h, l, dh = x.shape
            return x.transpose(0, 2, 1, 3).reshape(b, l, h * dh)

        def _ip_mask(bbox, batch_size, seq_len, dtype):
            M = bbox.shape[1]
            height, width = _grid_hw(seq_len, ASPECT_RATIO)
            x = jnp.linspace(0.0, 1.0, width, dtype=dtype)
            y = jnp.linspace(0.0, 1.0, height, dtype=dtype)
            yg, xg = jnp.meshgrid(y, x, indexing='ij')
            xg = xg.reshape(-1)
            yg = yg.reshape(-1)
            x1, y1, x2, y2 = (bbox[..., 0:1], bbox[..., 1:2], bbox[..., 2:3], bbox[..., 3:4])
            inside = (xg >= x1) & (xg <= x2) & (yg >= y1) & (yg <= y2)
            ip_mask = jnp.where(inside, 0.0, NEG).astype(dtype)
            ip_mask = jnp.transpose(ip_mask, (0, 2, 1))[:, None]
            ip_mask = jnp.repeat(ip_mask, NUM_IP_TOKENS // M, axis=-1)
            dummy = jnp.where(jnp.any(inside, axis=1), NEG, 0.0).astype(dtype)
            dummy = jnp.repeat(dummy[:, None, :, None], NUM_DUMMY_TOKENS, axis=-1)
            return jnp.concatenate([dummy, ip_mask], axis=-1)
        B, S, D = hidden_states.shape
        residual = hidden_states
        end_pos = encoder_hidden_states.shape[1] - (NUM_IP_TOKENS + NUM_DUMMY_TOKENS)
        text = encoder_hidden_states[:, :end_pos]
        ip_h = encoder_hidden_states[:, end_pos:]
        q = _split_heads(hidden_states @ w_q, HEADS)
        k = _split_heads(text @ w_k, HEADS)
        v = _split_heads(text @ w_v, HEADS)
        out_text = _sdpa(q, k, v)
        out_text = _merge_heads(out_text)
        mask_ip = _ip_mask(bbox, B, S, hidden_states.dtype)
        k_ip = _split_heads(ip_h @ w_k_ip, HEADS)
        v_ip = _split_heads(ip_h @ w_v_ip, HEADS)
        out_ip = _merge_heads(_sdpa(q, k_ip, v_ip, mask=mask_ip))
        out = out_text + IP_SCALE * out_ip
        out = out @ w_out + b_out
        out = out + residual
        return out

    def _L2_xattn_ref(hidden_states, encoder_hidden_states, Wq, Wk, Wv, Wk_ip, Wv_ip, Wo, bo):
        import jax, jax.numpy as jnp
        import numpy as np
        NUM_HEADS = 20
        TEXT_LEN = 77
        IP_SCALE = 1.0

        def _attend(q, k, v, sm_scale):
            scores = jnp.einsum('bhsd,bhld->bhsl', q, k) * sm_scale
            probs = jax.nn.softmax(scores, axis=-1)
            return jnp.einsum('bhsl,bhld->bhsd', probs, v)

        def _split_heads(x, h):
            b, s, c = x.shape
            return x.reshape(b, s, h, c // h).transpose(0, 2, 1, 3)

        def _merge_heads(x):
            b, h, s, d = x.shape
            return x.transpose(0, 2, 1, 3).reshape(b, s, h * d)
        residual = hidden_states
        B, S, C = hidden_states.shape
        H = NUM_HEADS
        D = C // H
        sm_scale = 1.0 / jnp.sqrt(jnp.asarray(D, hidden_states.dtype))
        text = encoder_hidden_states[:, :TEXT_LEN, :]
        ip = encoder_hidden_states[:, TEXT_LEN:, :]
        q = _split_heads(hidden_states @ Wq.T, H)
        k = _split_heads(text @ Wk.T, H)
        v = _split_heads(text @ Wv.T, H)
        out_text = _merge_heads(_attend(q, k, v, sm_scale))
        k_ip = _split_heads(ip @ Wk_ip.T, H)
        v_ip = _split_heads(ip @ Wv_ip.T, H)
        out_ip = _merge_heads(_attend(q, k_ip, v_ip, sm_scale))
        out = out_text + IP_SCALE * out_ip
        out = out @ Wo.T + bo
        return out + residual

    def _L3_xattn_ref(hidden_states, encoder_hidden_states, spatial_mask, W_q, W_k, W_v, W_k_ip, W_v_ip, W_out, b_out):
        import jax, jax.numpy as jnp
        import numpy as np
        HEADS = 20
        NUM_TOKENS = 4
        IP_SCALE = 1.0
        SEM_SCALE = 0.5
        RESCALE = 1.0
        EPS = 1e-12

        def _l2norm(x, axis=-1):
            n = jnp.sqrt(jnp.sum(x * x, axis=axis, keepdims=True))
            return x / jnp.maximum(n, EPS)
        B, S, C = hidden_states.shape
        H = HEADS
        Dh = C // H
        attn_scale = Dh ** (-0.5)
        residual = hidden_states
        text_ehs = encoder_hidden_states[:, :-NUM_TOKENS]
        ip_ehs = encoder_hidden_states[:, -NUM_TOKENS:]

        def heads(x):
            return x.reshape(B, -1, H, Dh).transpose(0, 2, 1, 3)
        q = heads(hidden_states @ W_q)
        k_t = heads(text_ehs @ W_k)
        v_t = heads(text_ehs @ W_v)
        scores_t = jnp.einsum('bhsd,bhtd->bhst', q, k_t) * attn_scale
        probs_t = jax.nn.softmax(scores_t, axis=-1)
        text_out = jnp.einsum('bhst,bhtd->bhsd', probs_t, v_t)
        text_out = text_out.transpose(0, 2, 1, 3).reshape(B, S, C)
        k_ip = heads(ip_ehs @ W_k_ip)
        v_ip = heads(ip_ehs @ W_v_ip)
        attn_scores = jnp.einsum('bhsd,bhnd->bhsn', q, k_ip) * attn_scale
        qsem = jnp.einsum('bhst,bte->bhse', probs_t, text_ehs)
        qsem = _l2norm(qsem)
        ip_n = _l2norm(ip_ehs)
        sem = jnp.einsum('bhse,bne->bhsn', qsem, ip_n)
        sem = jax.lax.stop_gradient(sem)
        fused = attn_scores + SEM_SCALE * sem
        probs_ip = jax.nn.softmax(fused, axis=-1)
        probs_ip = probs_ip * spatial_mask[None, None, :, None]
        ip_out = jnp.einsum('bhsn,bhnd->bhsd', probs_ip, v_ip)
        ip_out = ip_out.transpose(0, 2, 1, 3).reshape(B, S, C)
        out = text_out + IP_SCALE * ip_out
        out = out @ W_out + b_out
        out = out + residual
        return out / RESCALE
    x = _L0_xattn_ref(x, ctx_2048, L0_xattn_to_q_w, L0_xattn_to_k_w, L0_xattn_to_v_w, L0_xattn_to_k_object_w, L0_xattn_to_v_object_w, L0_xattn_to_k_others_w, L0_xattn_to_v_others_w, L0_xattn_to_k_ip_w, L0_xattn_to_v_ip_w, L0_xattn_to_out_w, L0_xattn_to_out_b)
    x = _L1_xattn_ref(x, ctx_2048, fside_Bx4x4_0, L1_xattn_w_q, L1_xattn_w_k, L1_xattn_w_v, L1_xattn_w_k_ip, L1_xattn_w_v_ip, L1_xattn_w_out, L1_xattn_b_out)
    x = _L2_xattn_ref(x, ctx_2048, L2_xattn_Wq, L2_xattn_Wk, L2_xattn_Wv, L2_xattn_Wk_ip, L2_xattn_Wv_ip, L2_xattn_Wo, L2_xattn_bo)
    x = _L3_xattn_ref(x, ctx_2048, fside_S_0, L3_xattn_W_q, L3_xattn_W_k, L3_xattn_W_v, L3_xattn_W_k_ip, L3_xattn_W_v_ip, L3_xattn_W_out, L3_xattn_b_out)
    return x

_drawn_inputs = setup_inputs


def setup_inputs(seed=0):
    import zlib

    import numpy as np

    out = dict(_drawn_inputs(seed))
    spreads = {'L0_xattn_to_out_b': (0.0, 0.1),
     'L1_xattn_b_out': (0.0, 0.1),
     'L2_xattn_bo': (0.0, 0.1),
     'L3_xattn_b_out': (0.0, 0.1)}
    factors = {'L1_xattn_w_q': 6.638, 'L1_xattn_w_k': 8.0, 'L1_xattn_w_k_ip': 8.0}
    for name, (base, spread) in spreads.items():
        noise = np.random.default_rng([zlib.crc32(name.encode()), seed]).standard_normal(out[name].shape)
        drawn = base * np.exp(spread * noise) if base else spread * noise
        out[name] = jnp.asarray(drawn.astype(out[name].dtype))
    for name, factor in factors.items():
        out[name] = (out[name] * factor).astype(out[name].dtype)
    return out
```

```python
from contextlib import ExitStack

import concourse.bass as bass
from concourse import mybir

F32 = mybir.dt.float32
BF16 = mybir.dt.bfloat16
ACT = mybir.ActivationFunctionType
ALU = mybir.AluOpType
AX = mybir.AxisListType

B, SQ, C, T, CC = 8, 112, 320, 375, 512
H, D = 20, 16
SCALE = D ** -0.5
NEG = -10000.0
EPS = 1e-12
SEM_SCALE = 0.5
TXT = 77
MAIN = [367, 367, 375, 371]
SEGS = [[(0, TXT), (TXT, 367)], [(0, 367)], [(0, TXT), (TXT, 375)], [(0, 371)]]
SMALL = [[0, 1], [2, 3], [], [4]]
QUAD = [0, 1, 2, 3, 3]
NCK = CC // 128
CH = [(0, 128), (128, 128), (256, 64)]
NT = 3
PAIRS = B // 2
UNITS = 8
GROUPS = 5
VW = 22
ONE_COL, R_COL, N_COL = 16, 17, 21
KPARTS = [0, 0, 0, 1, 1, 2]
QPARTS = [0, 1, 2, 0, 1, 0]
PROWS = 16 * len(KPARTS)
XROWS = PROWS + 4

PIECES = [
    [("K", 0), ("K", 1), ("K", 2), ("VT", 0), ("V", 0), ("V", 1), ("V", 2)],
    [("K", 0), ("K", 1), ("K", 2), ("V", 0), ("V", 1), ("V", 2)],
    [("K", 0), ("K", 1), ("K", 2), ("VT", 0), ("V", 0), ("V", 1), ("V", 2)],
    [("K", 0), ("K", 1), ("K", 2), ("V", 0), ("V", 1), ("V", 2), ("G", 0), ("G", 1), ("G", 2)],
]
PLACES = {6: [1, 1, 0, 1, 0, 0, 1, 1, 1, 0], 7: [1, 1, 1, 0, 1, 0, 1, 1, 1, 0], 9: [1, 1, 1, 1, 1, 0, 1, 1, 1, 1]}
BANK_USES = [(u, kind, n) for u in range(UNITS) for kind, n in PIECES[u // 2]]
N_PIECES = len(BANK_USES)
BANK_USES += [(u, "Y", 3 * g + i) for u in (6, 7) for g in range(GROUPS) for i in range(NT)]


def rows_of(l, c):
    return min(128, MAIN[l] - 128 * c)


def piece_index(u, p):
    return sum(len(PIECES[v // 2]) for v in range(u)) + p


def nth(kinds, n):
    return sum(1 for _, kind, _ in BANK_USES[:n + 1] if kind in kinds)


def at_place(u, place):
    if u >= UNITS:
        return []
    counts = PLACES[len(PIECES[u // 2])]
    first = sum(counts[:place])
    return list(range(first, first + counts[place]))


def build(nc, ins, out_t):
    dram_vs = nc.dram_tensor("small_v", (5, B, 4, C), F32, kind="Internal").ap()
    with ExitStack() as ctx:
        def sb(name, shape, dt=F32):
            return ctx.enter_context(nc.sbuf_tensor(name, shape, dt))

        def sem(name):
            return ctx.enter_context(nc.semaphore(name))

        per_pass = {}

        def signal(name, total):
            s = sem(name)
            per_pass[s.name] = total
            return s

        def level(s, it, n):
            return it * per_pass[s.name] + (1 + max(n, 0))

        KV_W = [["L0_k", "L0_v", "L0_kip", "L0_vip"], ["L1_k", "L1_v"],
                ["L2_k", "L2_v", "L2_kip", "L2_vip"], ["L3_k", "L3_v"]]
        W = {n: sb("w_" + n, [128, NCK, C]) for l in (0, 1, 3) for n in KV_W[l]}
        for n0, n2 in zip(KV_W[0], KV_W[2]):
            W[n2] = W[n0]
        WQ = [sb(f"wq{l}", [128, NT, C]) for l in range(4)]
        WO = [sb(f"wo{l}", [128, NT, C]) for l in range(4)]
        BIAS = sb("bias", [128, 4, NT])
        CT = [sb(f"ctx{p}", [128, NCK, T]) for p in range(2)]
        XT = [sb(f"xt{p}", [128, NT, SQ]) for p in range(2)]
        KP_ALL = sb("k_packed", [128, 3 * H * T], BF16)
        KP = [KP_ALL[:, k * H * T:(k + 1) * H * T].rearrange("p (h t) -> p h t", h=H) for k in range(3)]
        WS_NAMES = ["S0_k", "S0_v", "S1_k", "S1_v", "S2_k", "S2_v", "S4_k", "S4_v"]
        KP32 = KP_ALL[:, :].bitcast(F32)
        WS = {n: KP32[:, i * NCK * C:(i + 1) * NCK * C].rearrange("p (k c) -> p k c", k=NCK)
              for i, n in enumerate(WS_NAMES)}
        WS["S3_k"], WS["S3_v"] = WS["S2_k"], WS["S2_v"]
        QP = [sb(f"q_packed{p}", [128, H, SQ], BF16) for p in range(2)]
        VA = [sb(f"v{k}", [128, NT, H, VW]) for k in range(3)]
        VT = [sb(f"v_text{p}", [128, H, VW]) for p in range(2)]
        KC = [sb(f"k_parts{t}", [128, 3, T], BF16) for t in range(NT)]
        KR = [sb(f"k_rest{t}", [128, T]) for t in range(NT)]
        QC = sb("q_parts", [128, 3, NT * SQ], BF16)
        QR = sb("q_rest", [128, NT * SQ])
        PT = [sb(f"probs{k}", [128, NT, 4 * SQ]) for k in range(2)]
        ZT = [sb(f"gp{k}", [128, 4 * SQ]) for k in range(2)]
        GM_ALL = sb("gram", [128, 2, NT, 384])
        GM = [GM_ALL[:, p, :, :] for p in range(2)]
        SETUP = GM_ALL[:, :, :, :].rearrange("p a b c -> p (a b c)")
        OTS = sb("o_heads", [128, GROUPS, 2, SQ])
        MX = sb("neg_max", [SQ, 4 * H])
        MP = sb("max_parts", [2 * H, 2, SQ], BF16)
        SM = sb("small_scores", [SQ, 2, H, 4])
        SM3 = [sb(f"small_scores3{p}", [SQ, 1, H, 4]) for p in range(2)]
        SE = sb("small_exp", [SQ, 2, H, 4])
        SP_ = sb("small_probs", [SQ, 2, H, 4])
        SX = sb("small_max", [SQ, 2 * H])
        SS = sb("small_sum", [SQ, 2 * H])
        SR = sb("small_rec", [SQ, 2 * H])
        QN = sb("sem_norm", [SQ, 3, H])
        QS = sb("sem", [SQ, H, 4])
        PST = [sb(f"small_probs_t{p}", [80, 2, SQ]) for p in range(2)]
        VR = sb("small_v_rep", [80, 2, C])
        VB = sb("small_v_blk", [80, 2, C])
        ZR = sb("z_rec", [SQ, 2, H])
        OS = sb("o_sum", [SQ, C])
        O2 = sb("o_second", [SQ, C])
        OTF = sb("o_t", [128, NT, SQ])
        KSM = sb("small_k_parts", [128, 3, 5, NT, B, 4], BF16)
        KSR = SETUP[:, 1600:1600 + 5 * NT * B * 4]
        CS = sb("ctx_small", [128, NCK, 4, B * 4])
        SQI = sb("ip_squares", [128, NCK, B * 4])
        IPI = sb("ip_inv_norm", [SQ, B, 4])
        VSB = SETUP[0:32, 0:5 * C].rearrange("p (g c) -> p g c", g=5)
        BB = sb("boxes", [SQ, B, 4, 4])
        IN = sb("inside", [SQ, 4, B, 4])
        MSK = sb("ip_mask", [SQ, B, 2, 4])
        ANY = sb("any_inside", [SQ, B])
        IDN = sb("ident", [128, 128])
        HM = sb("head_mask", [80, C])
        GXY = sb("grid", [SQ, 2])
        IPM = sb("image_rows", [128, 2])
        SPM = sb("spatial", [SQ, 1])
        ONES = sb("ones", [128, 128])
        NSEL = sb("norm_select", [128, VW])
        TI = sb("image_cols", [2, T], BF16)

        def bank(name):
            return ctx.enter_context(nc.psum_tensor(name, [128, 512], F32))

        SB_ = [bank("scores0"), bank("scores1")]
        ST = [bank("scores_t0"), bank("scores_t1")]
        KVB = [bank("kv0"), bank("kv1")]
        OT = bank("o_acc")
        MI = bank("misc")
        ALL_BANKS = SB_ + ST + KVB + [OT, MI]

        w_in = [sem(f"w_in{l}") for l in range(4)]
        small_in = sem("small_in")
        const_in = sem("const_in")
        rows_in = sem("rows_in")
        zeroed = sem("zeroed")
        pool_set = sem("pool_set")
        ks_ready = sem("ks_ready")
        ks_copy = sem("ks_copy")
        vs_ready = sem("vs_ready")
        vs_copied = sem("vs_copied")
        vs_stored = sem("vs_stored")
        ip_sq = sem("ip_sq")
        ip_summed = sem("ip_summed")
        ip_sqrt = sem("ip_sqrt")
        ip_ready = sem("ip_ready")
        setup_step = sem("setup_step")

        n_small = [len(SMALL[u // 2]) for u in range(UNITS)]
        ctx_in = [signal(f"ctx_in{p}", 32) for p in range(2)]
        xt_in = [signal(f"xt_in{p}", 32) for p in range(2)]
        kv_ready = signal("kv_ready", len(BANK_USES))
        k1_ready = signal("k1_ready", 3 * UNITS)
        k_rest = signal("k_rest", 3 * UNITS)
        k2_ready = signal("k2_ready", 3 * UNITS)
        k3_ready = signal("k3_ready", 3 * UNITS)
        v_ready = signal("v_ready", nth(("V", "VT"), N_PIECES))
        ones_ready = signal("ones_ready", UNITS)
        g_ready = signal("g_ready", 6)
        z_ready = signal("z_ready", 2 * GROUPS * NT)
        k_packed = [signal(f"k_packed{t}", 96 * UNITS) for t in range(NT)]
        q_packed = signal("q_packed", 288 * UNITS)
        m_packed = signal("m_packed", 64 * UNITS)
        zt_used = signal("zt_used", 2 * GROUPS * 2)
        q_ready = signal("q_ready", UNITS)
        q1_ready = signal("q1_ready", UNITS)
        q_rest = signal("q_rest", UNITS)
        q2_ready = signal("q2_ready", UNITS)
        q3_ready = signal("q3_ready", UNITS)
        s_ready = signal("s_ready", H * UNITS)
        s_used = signal("s_used", H * UNITS)
        m_ready = signal("m_ready", UNITS)
        m1_ready = signal("m1_ready", UNITS)
        m2_ready = signal("m2_ready", UNITS)
        st_ready = signal("st_ready", UNITS * GROUPS * NT)
        exp_done = signal("exp_done", UNITS * GROUPS * NT)
        pv_done = signal("pv_done", UNITS * GROUPS)
        ot_used = signal("ot_used", UNITS * GROUPS)
        sq_ready = signal("sq_ready", 4)
        sq_done = signal("sq_done", 2)
        sx_ready = signal("sx_ready", 6)
        se_ready = signal("se_ready", 6)
        ps_ready = signal("ps_ready", 6)
        pst_ready = signal("pst_ready", 6)
        pst_copied = signal("pst_copied", 6)
        w0_in = signal("w0_in", 2 * 64)
        vr_in = signal("vr_in", 16 * sum(n_small))
        vb_ready = signal("vb_ready", 6)
        o2_ready = signal("o2_ready", UNITS)
        o_ready = signal("o_ready", UNITS)
        otf_ready = signal("otf_ready", UNITS)
        otf_copied = signal("otf_copied", UNITS)
        y_ready = signal("y_ready", UNITS)
        x_ready = signal("x_ready", UNITS)
        stored = [signal(f"stored{p}", 32) for p in range(2)]
        dve_step = signal("dve_step", DVE_STEPS)

        def small_nth(u):
            return sum(1 for v in range(u + 1) if n_small[v])

        block = ctx.enter_context(nc.Block())

        @block.sync
        def _(sp):
            def load_w(name, dst, s):
                sp.dma_start(dst[:, :, :], ins[name].rearrange("(k p) c -> p k c", p=128)).then_inc(s, 16)

            def load_wo(name, dst, s):
                sp.dma_start(dst[:, 0:2, :], ins[name][0:256, :].rearrange("(k p) c -> p k c", p=128)).then_inc(s, 16)
                sp.dma_start(dst[0:64, 2, :], ins[name][256:C, :]).then_inc(s, 16)

            sp.dma_start(CS[:, :, :, :], ins["ctx_small"].rearrange("(k p) g n -> p k g n", p=128)).then_inc(small_in, 16)
            for n in WS_NAMES:
                load_w(n, WS[n], small_in)
            sp.dma_start(IDN[:, :], ins["ident"]).then_inc(const_in, 16)
            sp.dma_start(HM[:, :], ins["head_mask"]).then_inc(const_in, 16)
            sp.dma_start(GXY[:, :], ins["grid"]).then_inc(const_in, 16)
            sp.dma_start(IPM[:, :], ins["image_rows"]).then_inc(const_in, 16)
            sp.dma_start(SPM[:, :], ins["spatial"]).then_inc(const_in, 16)
            sp.dma_start(BB[:, :, :, :], ins["boxes"].rearrange("(o b) m c -> o b m c", o=1)
                         .to_broadcast([SQ, B, 4, 4])).then_inc(const_in, 16)
            for l in range(4):
                for t, (c0, cn) in enumerate(CH):
                    sp.dma_start(BIAS[0:cn, l, t:t + 1], ins[f"L{l}_b"][c0:c0 + cn, :]).then_inc(const_in, 16)
            for l in range(4):
                for n in KV_W[l] if l in (1, 3) else []:
                    load_w(n, W[n], w_in[l])
                load_wo(f"L{l}_q", WQ[l], w_in[l])
                load_wo(f"L{l}_o", WO[l], w_in[l])
            sp.wait_ge(vs_copied, 5)
            sp.dma_start(dram_vs.rearrange("g b n c -> (b n) g c"), VSB[:, :, :]).then_inc(vs_stored, 16)
            sp.wait_ge(pool_set, 1)
            for k in range(3):
                sp.dma_start(KP[k][PROWS + 2:PROWS + 4, :, :],
                             TI[:, :].rearrange("p (o t) -> p o t", o=1).to_broadcast([2, H, T])).then_inc(rows_in, 16)
            sp.wait_ge(vs_stored, 16)

            for sig in k_packed + [q_packed, m_packed, w0_in]:
                sp.sem_inc(sig, 1)
            with sp.Fori(0, PAIRS) as it:
                def pack_k(u, p):
                    kind, t = PIECES[u // 2][p]
                    if kind != "K":
                        return
                    sp.wait_ge(k3_ready, level(k3_ready, it, 3 * u + t + 1))
                    hn = CH[t][1] // D
                    for r, part in enumerate(KPARTS):
                        sp.dma_start(
                            KP[u % 3][D * r:D * r + D, 8 * t:8 * t + hn, :],
                            KC[t][0:CH[t][1], part, :]).then_inc(k_packed[t], 16)

                def pack_q(u):
                    sp.wait_ge(q3_ready, level(q3_ready, it, u + 1))
                    for r, part in enumerate(QPARTS):
                        for t, (c0, cn) in enumerate(CH):
                            sp.dma_start(
                                QP[u % 2][D * r:D * r + D, 8 * t:8 * t + cn // D, :],
                                QC[0:cn, part, t * SQ:(t + 1) * SQ]).then_inc(q_packed, 16)

                def pack_m(u):
                    sp.wait_ge(m2_ready, level(m2_ready, it, u + 1))
                    last = len(SEGS[u // 2]) - 1
                    for s in range(2):
                        for part in range(2):
                            row = PROWS + 2 * s + part
                            sp.dma_start(
                                QP[u % 2][row:row + 1, :, :],
                                MP[H * min(s, last):H * min(s, last) + H, part, :]).then_inc(m_packed, 16)

                def load_kv_weights(l):
                    for n in KV_W[l]:
                        sp.dma_start(W[n][:, :, :], ins[n].rearrange("(k p) c -> p k c", p=128)).then_inc(w0_in, 16)

                sp.wait_ge(kv_ready, level(kv_ready, it, 0))
                load_kv_weights(0)
                for p in range(len(PIECES[0])):
                    pack_k(0, p)
                for s in range(UNITS + 1):
                    if s < UNITS:
                        pack_q(s)
                    for place in range(7):
                        for p in at_place(s + 1, place):
                            pack_k(s + 1, p)
                    if s < UNITS:
                        pack_m(s)
                    for place in range(7, 10):
                        for p in at_place(s + 1, place):
                            pack_k(s + 1, p)
                    if s == 0:
                        sp.wait_ge(kv_ready, level(kv_ready, it, piece_index(2, 0)))
                        load_kv_weights(2)
            for p in range(2):
                sp.wait_ge(stored[p], 1 + PAIRS * per_pass[stored[p].name])

        @block.tensor
        def _(pe):
            mm = nc.tensor.matmul
            pe.wait_ge(zeroed, 1)
            pe.wait_ge(small_in, 16 * (1 + len(WS_NAMES)))
            for g in range(5):
                for t, (c0, cn) in enumerate(CH):
                    for k in range(NCK):
                        last = mm(MI[0:cn, (g * NT + t) * 32:(g * NT + t) * 32 + 32], WS[f"S{g}_k"][:, k, c0:c0 + cn],
                                  CS[:, k, QUAD[g], :], start=(k == 0), stop=(k == NCK - 1))
            last.then_inc(ks_ready, 1)
            for g in range(5):
                for k in range(NCK):
                    last = mm(ALL_BANKS[g][0:32, 0:C], CS[:, k, QUAD[g], :],
                              WS[f"S{g}_v"][:, k, :], start=(k == 0), stop=(k == NCK - 1))
                last.then_inc(vs_ready, 1)
            pe.wait_ge(ip_sq, 1)
            mm(ALL_BANKS[5][0:SQ, 0:NCK * 32], ONES[:, 0:SQ], SQI[:, :, :].rearrange("p k n -> p (k n)"),
               start=True, stop=True).then_inc(ip_ready, 1)
            pe.wait_ge(const_in, 16 * CONSTS)
            pe.wait_ge(rows_in, 48)
            pe.wait_ge(setup_step, SETUP_STEPS)
            pe.wait_ge(vs_copied, 5)
            for l in range(4):
                pe.wait_ge(w_in[l], 16 * (4 + (len(KV_W[l]) if l in (1, 3) else 0)))

            for sig in [kv_ready, q_ready, s_ready, m_ready, st_ready, pv_done, zt_used, pst_ready, o2_ready,
                        otf_ready, y_ready]:
                pe.sem_inc(sig, 1)
            with pe.Fori(0, PAIRS) as it:
                def bank_free(n):
                    kind = BANK_USES[n - 2][1] if n >= 2 else "Y"
                    m = n - 2 if n >= 2 else -1
                    sig, kinds = {"K": (k_rest, ("K",)), "V": (v_ready, ("V", "VT")), "VT": (v_ready, ("V", "VT")),
                                  "G": (g_ready, ("G",)), "Y": (z_ready, ("Y",))}[kind]
                    pe.wait_ge(sig, level(sig, it, nth(kinds, m) if m >= 0 else 0))

                def kv_piece(u, p):
                    l, par = u // 2, u % 2
                    kind, i = PIECES[l][p]
                    n = piece_index(u, p)
                    dst = KVB[n % 2]
                    if p == 0:
                        pe.wait_ge(ctx_in[par], level(ctx_in[par], it, 16 if l == 0 else 32))
                        if l in (0, 2):
                            pe.wait_ge(w0_in, level(w0_in, it, 64 * (l // 2 + 1)))
                    bank_free(n)
                    if kind == "K":
                        c0, cn = CH[i]
                        for s, (t0, t1) in enumerate(SEGS[l]):
                            w = W[f"L{l}_k" + ("ip" if s else "")]
                            for k in range(NCK):
                                last = mm(dst[0:cn, t0:t1], w[:, k, c0:c0 + cn], CT[par][:, k, t0:t1],
                                          start=(k == 0), stop=(k == NCK - 1))
                    elif kind == "VT":
                        for k in range(NCK):
                            last = mm(dst[0:TXT, 0:C], CT[par][:, k, 0:TXT], W[f"L{l}_v"][:, k, :],
                                      start=(k == 0), stop=(k == NCK - 1))
                    elif kind == "V":
                        w = W[f"L{l}_v" + ("ip" if len(SEGS[l]) == 2 else "")]
                        r = rows_of(l, i)
                        for k in range(NCK):
                            last = mm(dst[0:r, 0:C], CT[par][:, k, 128 * i:128 * i + r], w[:, k, :],
                                      start=(k == 0), stop=(k == NCK - 1))
                        if l == 3:
                            for k in range(NCK):
                                last = mm(dst[0:r, C:C + 4], CT[par][:, k, 128 * i:128 * i + r],
                                          CT[par][:, k, MAIN[3]:T], start=(k == 0), stop=(k == NCK - 1))
                    else:
                        r, wd = rows_of(3, i), min(128 * i + 128, MAIN[3])
                        for k in range(NCK):
                            last = mm(dst[0:r, 0:wd], CT[par][:, k, 128 * i:128 * i + r], CT[par][:, k, 0:wd],
                                      start=(k == 0), stop=(k == NCK - 1))
                    last.then_inc(kv_ready, 1)

                def kv_place(s, place):
                    for p in at_place(s + 1, place):
                        kv_piece(s + 1, p)

                def queries(u):
                    l, par = u // 2, u % 2
                    if l == 0:
                        pe.wait_ge(xt_in[par], level(xt_in[par], it, 32))
                    pe.wait_ge(x_ready, level(x_ready, it, u - 1))
                    if u >= 1:
                        pe.wait_ge(m2_ready, level(m2_ready, it, u))
                        if (u - 1) // 2 < 2:
                            pe.wait_ge(pst_copied, level(pst_copied, it, small_nth(u - 1)))
                    for t, (c0, cn) in enumerate(CH):
                        for k, (_, kn) in enumerate(CH):
                            last = mm(MI[0:cn, t * SQ:(t + 1) * SQ], WQ[l][0:kn, k, c0:c0 + cn],
                                      XT[par][0:kn, k, :], start=(k == 0), stop=(k == NT - 1))
                    last.then_inc(q_ready, 1)

                def scores(u, g):
                    if g == 0:
                        pe.wait_ge(q_packed, level(q_packed, it, 288 * (u + 1)))
                        for t in range(NT):
                            pe.wait_ge(k_packed[t], level(k_packed[t], it, 96 * (u + 1)))
                        pe.wait_ge(o_ready, level(o_ready, it, u - 1))
                    for j in range(4):
                        h = 4 * g + j
                        n = u * H + h
                        pe.wait_ge(s_used, level(s_used, it, n - 1))
                        mm(SB_[n % 2][0:SQ, 0:T], QP[u % 2][0:PROWS, h, :], KP[u % 3][0:PROWS, h, :],
                                      start=True, stop=True).then_inc(s_ready, 1)

                def maxima(u):
                    pe.wait_ge(s_used, level(s_used, it, (u + 1) * H))
                    pe.wait_ge(q_rest, level(q_rest, it, u + 1))
                    nc.tensor.transpose(MI[0:4 * H, 0:SQ], MX[:, :], IDN[0:SQ, 0:SQ]).then_inc(m_ready, 1)

                def small_t(u):
                    if u // 2 < 2:
                        pe.wait_ge(m2_ready, level(m2_ready, it, u + 1))
                    pe.wait_ge(ps_ready, level(ps_ready, it, small_nth(u)))
                    for k in range(n_small[u]):
                        last = nc.tensor.transpose(MI[0:80, (k + 1) * 128:(k + 1) * 128 + SQ],
                                                   SP_[:, k, :, :].rearrange("p h n -> p (h n)"), IDN[0:SQ, 0:SQ])
                    last.then_inc(pst_ready, 1)

                def back_scores(u, g):
                    l = u // 2
                    if g == 0:
                        pe.wait_ge(m_packed, level(m_packed, it, 64 * (u + 1)))
                    for c in range(NT):
                        n = (u * GROUPS + g) * NT + c
                        r = rows_of(l, c)
                        pe.wait_ge(exp_done, level(exp_done, it, n - 1))
                        for j in range(4):
                            h = 4 * g + j
                            last = mm(ST[n % 2][0:r, j * SQ:(j + 1) * SQ],
                                      KP[u % 3][0:XROWS, h, 128 * c:128 * c + r], QP[u % 2][0:XROWS, h, :],
                                      start=True, stop=True)
                        last.then_inc(st_ready, 1)

                def back_values(u, g):
                    l, par = u // 2, u % 2
                    gn = u * GROUPS + g
                    ns = len(SEGS[l])
                    if g == 0:
                        pe.wait_ge(v_ready, level(v_ready, it, nth(("V", "VT"), piece_index(u + 1, 0) - 1)))
                        pe.wait_ge(ones_ready, level(ones_ready, it, u + 1))
                        if l == 3:
                            pe.wait_ge(g_ready, level(g_ready, it, 3 * (par + 1)))
                    pe.wait_ge(ot_used, level(ot_used, it, gn))
                    o0 = (ns - 1) * SQ
                    pt = PT[gn % 2]
                    for c in range(NT):
                        pe.wait_ge(exp_done, level(exp_done, it, gn * NT + c + 1))
                        r = rows_of(l, c)
                        if c == 0 and ns == 2:
                            for j in range(4):
                                mm(OT[32 * j:32 * j + VW, 0:SQ], VT[par][0:TXT, 4 * g + j, :],
                                   pt[0:TXT, 0, j * SQ:(j + 1) * SQ], start=True, stop=True, tile_position=(0, 32 * j))
                        for j in range(4):
                            last = mm(OT[32 * j:32 * j + VW, o0:o0 + SQ], VA[u % 3][0:r, c, 4 * g + j, :],
                                      pt[0:r, c, j * SQ:(j + 1) * SQ], start=(c == 0), stop=(c == 2 and l < 3),
                                      tile_position=(0, 32 * j))
                    if l < 3:
                        last.then_inc(pv_done, 1)
                        return

                    def gram(i):
                        n = N_PIECES + (par * GROUPS + g) * NT + i
                        r = rows_of(3, i)
                        bank_free(n)
                        for j in range(i, NT):
                            rj = rows_of(3, j)
                            m = mm(KVB[n % 2][0:r, 0:4 * SQ], GM[par][0:rj, j, 128 * i:128 * i + r],
                                   pt[0:rj, j, :], start=(j == i), stop=(j == NT - 1))
                        m.then_inc(kv_ready, 1)

                    def norm(i):
                        n = (par * GROUPS + g) * NT + i
                        pe.wait_ge(z_ready, level(z_ready, it, n + 1))
                        r = rows_of(3, i)
                        for j in range(4):
                            m = mm(OT[32 * j:32 * j + VW, 0:SQ], NSEL[0:r, :], ZT[n % 2][0:r, j * SQ:(j + 1) * SQ],
                                   start=False, stop=(i == NT - 1), tile_position=(0, 32 * j))
                        m.then_inc((zt_used if i < 2 else pv_done), 1)

                    gram(0)
                    gram(1)
                    norm(0)
                    gram(2)
                    norm(1)
                    norm(2)

                def final_heads(u):
                    l = u // 2
                    pe.wait_ge(ot_used, level(ot_used, it, (u + 1) * GROUPS))
                    pe.wait_ge(o_ready, level(o_ready, it, u))
                    pe.wait_ge(x_ready, level(x_ready, it, u))
                    if u + 1 < UNITS:
                        pe.wait_ge(s_used, level(s_used, it, (u + 2) * H))
                        pe.wait_ge(m2_ready, level(m2_ready, it, u + 2))
                        if n_small[u + 1] and (u + 1) // 2 < 2:
                            pe.wait_ge(pst_copied, level(pst_copied, it, small_nth(u + 1)))
                    for s in range(len(SEGS[l])):
                        for g in range(GROUPS):
                            dst = SB_[1][0:SQ, s * 128:s * 128 + 128] if g == 4 else \
                                [SB_[0], MI][s][0:SQ, g * 128:g * 128 + 128]
                            last = nc.tensor.transpose(dst, OTS[:, g, s, :], IDN[:, :])
                    last.then_inc(o2_ready, 1)

                def final_transpose(u):
                    l = u // 2
                    pe.wait_ge(o_ready, level(o_ready, it, u + 1))
                    if l == 3:
                        small_t(u)
                    if n_small[u]:
                        pe.wait_ge(pst_copied, level(pst_copied, it, small_nth(u)))
                        pe.wait_ge(vb_ready, level(vb_ready, it, small_nth(u)))
                    for t, (c0, cn) in enumerate(CH):
                        last = mm(MI[0:cn, t * SQ:(t + 1) * SQ], OS[:, c0:c0 + cn], IDN[0:SQ, 0:SQ],
                                  start=True, stop=(n_small[u] == 0))
                        for k in range(n_small[u]):
                            last = mm(MI[0:cn, t * SQ:(t + 1) * SQ], VB[:, k, c0:c0 + cn], PST[u % 2][:, k, :],
                                      start=False, stop=(k == n_small[u] - 1))
                    last.then_inc(otf_ready, 1)

                def final_project(u):
                    l = u // 2
                    pe.wait_ge(otf_copied, level(otf_copied, it, u + 1))
                    for t, (c0, cn) in enumerate(CH):
                        for k, (_, kn) in enumerate(CH):
                            last = mm(MI[0:cn, t * SQ:(t + 1) * SQ], WO[l][0:kn, k, c0:c0 + cn],
                                      OTF[0:kn, k, :], start=(k == 0), stop=(k == NT - 1))
                    last.then_inc(y_ready, 1)

                for p in range(len(PIECES[0])):
                    kv_piece(0, p)
                for s in range(UNITS + 1):
                    if s < UNITS:
                        queries(s)
                    kv_place(s, 0)
                    for g in range(GROUPS):
                        if s < UNITS:
                            scores(s, g)
                        if s >= 1:
                            back_scores(s - 1, g)
                            if g >= 1:
                                back_values(s - 1, g - 1)
                        kv_place(s, 1 + g)
                    if s >= 1:
                        back_values(s - 1, GROUPS - 1)
                    if s < UNITS:
                        maxima(s)
                    kv_place(s, 6)
                    if s < UNITS and s // 2 < 2:
                        small_t(s)
                    if s >= 1:
                        final_heads(s - 1)
                    kv_place(s, 7)
                    if s >= 1:
                        final_transpose(s - 1)
                    kv_place(s, 8)
                    if s >= 1:
                        final_project(s - 1)
                    kv_place(s, 9)

        @block.scalar
        def _(act):
            def copy(dst, src, scale=1.0):
                return nc.scalar.activation(dst, src, ACT.Copy, scale=scale)

            act.wait_ge(const_in, 16 * CONSTS)
            for g in range(5):
                act.wait_ge(vs_ready, g + 1)
                copy(VSB[:, g, :], ALL_BANKS[g][0:32, 0:C]).then_inc(vs_copied, 1)
            act.wait_ge(ip_summed, 1)
            flat_ipi = IPI[:, :, :].rearrange("p b n -> p (b n)")
            nc.scalar.activation(flat_ipi, flat_ipi, ACT.Sqrt).then_inc(ip_sqrt, 1)

            for sig in ctx_in + xt_in + stored + [k1_ready, k2_ready, v_ready, q1_ready, q2_ready, m1_ready, exp_done,
                                                  se_ready, sq_done, pst_copied, vr_in, otf_copied]:
                act.sem_inc(sig, 1)
            with act.Fori(0, PAIRS) as it:
                def kv_piece(u, p):
                    l, par = u // 2, u % 2
                    kind, i = PIECES[l][p]
                    n = piece_index(u, p)
                    src = KVB[n % 2]
                    if kind == "K":
                        cn = CH[i][1]
                        m = MAIN[l]
                        act.wait_ge(kv_ready, level(kv_ready, it, n + 1))
                        act.wait_ge(k_packed[i], level(k_packed[i], it, 96 * u))
                        copy(KC[i][0:cn, 0, 0:m], src[0:cn, 0:m]).then_inc(k1_ready, 1)
                        act.wait_ge(k_rest, level(k_rest, it, 3 * u + i + 1))
                        copy(KC[i][0:cn, 1, 0:m], KR[i][0:cn, 0:m]).then_inc(k2_ready, 1)
                    elif kind in ("V", "VT"):
                        act.wait_ge(kv_ready, level(kv_ready, it, n + 1))
                        if kind == "VT":
                            act.wait_ge(pv_done, level(pv_done, it, (u - 3) * GROUPS))
                            copy(VT[par][0:TXT, :, 0:D],
                                            src[0:TXT, 0:C].rearrange("p (h c) -> p h c", h=H)).then_inc(v_ready, 1)
                            return
                        act.wait_ge(pv_done, level(pv_done, it, (u - 2) * GROUPS))
                        r = rows_of(l, i)
                        if l == 3:
                            copy(VA[u % 3][0:r, i, :, R_COL:R_COL + 4],
                                 src[0:r, C:C + 4].rearrange("p (o c) -> p o c", o=1).to_broadcast([r, H, 4]))
                        copy(VA[u % 3][0:r, i, :, 0:D], src[0:r, 0:C].rearrange("p (h c) -> p h c", h=H),
                                        scale=IPM[0:r, 1:2] if i == 0 and len(SEGS[l]) == 2 else 1.0).then_inc(v_ready, 1)

                def kv_place(s, place):
                    for p in at_place(s + 1, place):
                        kv_piece(s + 1, p)

                def queries(u):
                    act.wait_ge(q_ready, level(q_ready, it, u + 1))
                    act.wait_ge(q_packed, level(q_packed, it, 288 * u))
                    copy(QC[:, 0, :], MI[:, 0:NT * SQ]).then_inc(q1_ready, 1)
                    act.wait_ge(q_rest, level(q_rest, it, u + 1))
                    copy(QC[:, 1, :], QR[:, :]).then_inc(q2_ready, 1)

                def exponentials(u, g):
                    l = u // 2
                    gn = u * GROUPS + g
                    for c in range(NT):
                        act.wait_ge(st_ready, level(st_ready, it, gn * NT + c + 1))
                        if c == 0:
                            act.wait_ge(pv_done, level(pv_done, it, gn - 1))
                        r = rows_of(l, c)
                        nc.scalar.activation(PT[gn % 2][0:r, c, :], ST[(gn * NT + c) % 2][0:r, 0:4 * SQ],
                                                         ACT.Exp, scale=SCALE).then_inc(exp_done, 1)

                def small_exp(u):
                    k = n_small[u]
                    act.wait_ge(sx_ready, level(sx_ready, it, small_nth(u)))
                    nc.scalar.activation(SE[:, 0:k, :, :], SE[:, 0:k, :, :], ACT.Exp,
                                                     scale=SCALE if u // 2 == 0 else 1.0).then_inc(se_ready, 1)

                def small_t(u):
                    k = n_small[u]
                    act.wait_ge(pst_ready, level(pst_ready, it, small_nth(u)))
                    act.wait_ge(otf_ready, level(otf_ready, it, u - 1))
                    copy(PST[u % 2][:, 0:k, :], MI[0:80, 128:128 + 128 * k]
                                       .rearrange("p (k q) -> p k q", k=k)[:, :, 0:SQ]).then_inc(pst_copied, 1)

                def maxima(u):
                    ns = len(SEGS[u // 2])
                    act.wait_ge(m_ready, level(m_ready, it, u + 1))
                    act.wait_ge(m_packed, level(m_packed, it, 64 * u))
                    copy(MP[0:ns * H, 0, :], MI[0:ns * H, 0:SQ]).then_inc(m1_ready, 1)
                    if u // 2 < 2:
                        small_exp(u)

                def load_small_v(u):
                    if not n_small[u]:
                        return
                    act.wait_ge(vb_ready, level(vb_ready, it, small_nth(u) - 1))
                    for k, g in enumerate(SMALL[u // 2]):
                        act.dma_start(
                            VR[:, k, :], dram_vs[g, it * 2 + u % 2].rearrange("(o n) c -> o n c", o=1)
                            .to_broadcast([H, 4, C])).then_inc(vr_in, 16)

                def load_ctx(name, p):
                    act.dma_start(CT[p][:, :, :], ins[name][it * 2 + p]
                                              .rearrange("(k p) t -> p k t", p=128)).then_inc(ctx_in[p], 16)

                act.wait_ge(kv_ready, level(kv_ready, it, 0))
                for p in range(2):
                    load_ctx("ctx0", p)
                    act.wait_ge(stored[p], level(stored[p], it, 0))
                    act.dma_start(XT[p][:, 0:2, :], ins["x_t"][it * 2 + p, 0:256, :]
                                              .rearrange("(k p) q -> p k q", p=128)).then_inc(xt_in[p], 16)
                    act.dma_start(XT[p][0:64, 2, :], ins["x_t"][it * 2 + p, 256:C, :]).then_inc(xt_in[p], 16)
                for p in range(len(PIECES[0])):
                    kv_piece(0, p)
                load_ctx("ctx1", 0)
                for s in range(UNITS + 1):
                    if s < UNITS:
                        queries(s)
                    kv_place(s, 0)
                    if s >= 1:
                        load_small_v(s - 1)
                    for g in range(GROUPS):
                        if s >= 1:
                            exponentials(s - 1, g)
                        kv_place(s, 1 + g)
                    if s < UNITS:
                        maxima(s)
                    kv_place(s, 6)
                    if s < UNITS and s // 2 < 2:
                        small_t(s)
                    kv_place(s, 7)
                    if s >= 1:
                        if (s - 1) // 2 == 3:
                            act.wait_ge(sq_ready, level(sq_ready, it, 2 * (s - 1 - 6) + 2))
                            nc.scalar.activation(QN[:, 0, :], QN[:, 0, :], ACT.Sqrt).then_inc(sq_done, 1)
                            small_exp(s - 1)
                            small_t(s - 1)
                        act.wait_ge(otf_ready, level(otf_ready, it, s))
                        copy(OTF[:, :, :].rearrange("p t q -> p (t q)"), MI[:, 0:NT * SQ]).then_inc(otf_copied, 1)
                    kv_place(s, 8)
                    kv_place(s, 9)
                    if s == 0:
                        load_ctx("ctx1", 1)
                    if s >= UNITS - 1:
                        p = (s - 1) % 2
                        act.wait_ge(x_ready, level(x_ready, it, s))
                        act.dma_start(out_t[it * 2 + p, 0:256, :].rearrange("(k p) q -> p k q", p=128),
                                                  XT[p][:, 0:2, :]).then_inc(stored[p], 16)
                        act.dma_start(out_t[it * 2 + p, 256:C, :], XT[p][0:64, 2, :]).then_inc(stored[p], 16)

        @block.vector
        def _(dve):
            v = nc.vector
            steps = [0]

            def setup(instruction):
                steps[0] += 1
                instruction.then_inc(setup_step, 1)
                dve.wait_ge(setup_step, steps[0])

            for bank_ in ALL_BANKS:
                setup(v.memset(bank_[:, :], 0.0))
            for buf in [MX[:, :], QC[:, :, :], QR[:, :], KC[0][:, :, :], KC[1][:, :, :], KC[2][:, :, :], OTF[:, :, :],
                        KSM[:, 0, :, :, :, :], KSM[:, 1, :, :, :, :], KSM[:, 2, :, :, :, :]] \
                    + [VA[k][:, :, :, :] for k in range(3)] + [VT[k][:, :, :] for k in range(2)]:
                setup(v.memset(buf, 0.0))
            for k in range(3):
                setup(v.memset(VA[k][:, :, :, ONE_COL:ONE_COL + 1], 1.0))
            for k in range(2):
                setup(v.memset(VT[k][:, :, ONE_COL:ONE_COL + 1], 1.0))
            setup(v.memset(NSEL[:, :], 0.0))
            setup(v.memset(NSEL[:, N_COL:N_COL + 1], 1.0))
            setup(v.memset(ONES[:, :], 1.0))
            v.memset(SM[:, :, :, :], 0.0).then_inc(zeroed, 1)
            dve.wait_ge(small_in, 16 * (1 + len(WS_NAMES)))
            for k in range(NCK):
                ip = CS[:, k, QUAD[4], :]
                ins_ = v.tensor_tensor(SQI[:, k, :], ip, ip, ALU.mult)
                if k < NCK - 1:
                    setup(ins_)
            ins_.then_inc(ip_sq, 1)
            dve.wait_ge(const_in, 16 * CONSTS)
            for k, (edge, axis, op) in enumerate([(0, 0, ALU.is_le), (1, 1, ALU.is_le), (2, 0, ALU.is_ge), (3, 1, ALU.is_ge)]):
                setup(v.tensor_scalar(IN[:, k, :, :], BB[:, :, :, edge], GXY[:, axis:axis + 1], None, op))
            for k in range(1, 4):
                setup(v.tensor_tensor(IN[:, 0, :, :], IN[:, 0, :, :], IN[:, k, :, :], ALU.mult))
            setup(v.tensor_scalar(MSK[:, :, 1, :], IN[:, 0, :, :], -NEG, NEG, ALU.mult, ALU.add))
            setup(v.tensor_reduce(ANY[:, :], IN[:, 0, :, :], AX.X, ALU.max))
            setup(v.tensor_scalar(MSK[:, :, 0, :], ANY[:, :].rearrange("p (b o) -> p b o", o=1).to_broadcast([SQ, B, 4]),
                                  NEG, None, ALU.mult))
            dve.wait_ge(ks_ready, 1)
            flat = [KSM[:, part, :, :, :, :].rearrange("p g t b n -> p (g t b n)") for part in range(3)]
            src = MI[:, 0:5 * NT * 32]
            setup(v.tensor_copy(flat[0], src))
            setup(v.tensor_tensor(KSR[:, :], src, flat[0], ALU.subtract))
            setup(v.tensor_copy(flat[1], KSR[:, :]))
            v.tensor_tensor(flat[2], KSR[:, :], flat[1], ALU.subtract).then_inc(ks_copy, 1)
            dve.wait_ge(ip_ready, 1)
            flat_ipi = IPI[:, :, :].rearrange("p b n -> p (b n)")
            v.tensor_reduce(flat_ipi, ALL_BANKS[5][0:SQ, 0:NCK * 32].rearrange("p (k n) -> p n k", k=NCK),
                            AX.X, ALU.add).then_inc(ip_summed, 1)
            dve.wait_ge(ip_sqrt, 1)
            setup(v.tensor_scalar(flat_ipi, flat_ipi, EPS, None, ALU.max))
            setup(v.reciprocal(flat_ipi, flat_ipi))
            assert steps[0] == SETUP_STEPS, steps[0]

            for sig in [k_rest, g_ready, z_ready, q_rest, q3_ready, s_used, m2_ready, ot_used, sx_ready, ps_ready,
                        sq_ready, o_ready, x_ready, dve_step]:
                dve.sem_inc(sig, 1)
            with dve.Fori(0, PAIRS) as it:
                steps[0] = 0

                def step(instruction):
                    steps[0] += 1
                    instruction.then_inc(dve_step, 1)
                    dve.wait_ge(dve_step, level(dve_step, it, steps[0]))

                def kv_piece(u, p):
                    l, par = u // 2, u % 2
                    kind, i = PIECES[l][p]
                    n = piece_index(u, p)
                    if kind == "K":
                        cn, m = CH[i][1], MAIN[l]
                        dve.wait_ge(k1_ready, level(k1_ready, it, 3 * u + i + 1))
                        dve.wait_ge(k3_ready, level(k3_ready, it, 3 * (u - 1) + i + 1 if u else 0))
                        v.tensor_tensor(KR[i][0:cn, 0:m], KVB[n % 2][0:cn, 0:m], KC[i][0:cn, 0, 0:m],
                                                  ALU.subtract).then_inc(k_rest, 1)
                    elif kind == "G":
                        dve.wait_ge(kv_ready, level(kv_ready, it, n + 1))
                        r, wd = rows_of(3, i), min(128 * i + 128, MAIN[3])
                        dve.wait_ge(pv_done, level(pv_done, it, 0))
                        if i:
                            step(v.tensor_scalar_mul(GM[par][0:r, i, 0:128 * i], KVB[n % 2][0:r, 0:128 * i], 2.0))
                        v.tensor_copy(GM[par][0:r, i, 128 * i:wd], KVB[n % 2][0:r, 128 * i:wd]).then_inc(g_ready, 1)

                def kv_place(s, place):
                    for p in at_place(s + 1, place):
                        kv_piece(s + 1, p)

                def queries(u):
                    dve.wait_ge(q1_ready, level(q1_ready, it, u + 1))
                    v.tensor_tensor(QR[:, :], MI[:, 0:NT * SQ], QC[:, 0, :], ALU.subtract).then_inc(q_rest, 1)
                    dve.wait_ge(st_ready, level(st_ready, it, (u - 1) * GROUPS * NT))
                    dve.wait_ge(q2_ready, level(q2_ready, it, u + 1))
                    v.tensor_tensor(QC[:, 2, :], QR[:, :], QC[:, 1, :], ALU.subtract).then_inc(q3_ready, 1)

                def max_of(u, g):
                    l = u // 2
                    if g == 0:
                        dve.wait_ge(m_ready, level(m_ready, it, u))
                    for j in range(4):
                        h = 4 * g + j
                        n = u * H + h
                        dve.wait_ge(s_ready, level(s_ready, it, n + 1))
                        src = SB_[n % 2]
                        if n_small[u]:
                            m = n_small[u]
                            dst = SM3[u % 2][:, :, h, :] if l == 3 else SM[:, :, h, :]
                            v.tensor_copy(dst, src[0:SQ, MAIN[l]:MAIN[l] + 4 * m]
                                          .rearrange("p (g n) -> p g n", g=m))
                        for s, (t0, t1) in enumerate(SEGS[l]):
                            last = v.tensor_reduce(MX[:, s * H + h:s * H + h + 1], src[0:SQ, t0:t1], AX.X, ALU.max,
                                                   negate=True)
                        last.then_inc(s_used, 1)

                def small_softmax(u, scores_, last_scale=None):
                    l, k = u // 2, n_small[u]
                    if l == 1:
                        def view(buf):
                            return buf[:, 0:k, :, :].rearrange("p g h n -> p h g n")
                        m = H
                        axis = AX.XY

                        def wide(vec):
                            return vec[:, 0:H].rearrange("p (o h i) -> p o h i", o=1, i=1).to_broadcast([SQ, k, H, 4])
                        full = lambda buf: buf[:, 0:k, :, :]
                    else:
                        m = k * H
                        axis = AX.X

                        def view(buf):
                            return buf[:, 0:k, :, :].rearrange("p g h n -> p (g h) n")

                        def wide(vec):
                            return vec[:, 0:m].rearrange("p (h i) -> p h i", i=1).to_broadcast([SQ, m, 4])
                        full = view
                    step(v.tensor_reduce(SX[:, 0:m], view(scores_), axis, ALU.max))
                    v.tensor_tensor(full(SE), full(scores_), wide(SX), ALU.subtract).then_inc(sx_ready, 1)
                    dve.wait_ge(se_ready, level(se_ready, it, small_nth(u)))
                    step(v.tensor_reduce(SS[:, 0:m], view(SE), axis, ALU.add))
                    step(v.reciprocal(SR[:, 0:m], SS[:, 0:m]))
                    if l == 3:
                        v.scalar_tensor_tensor(full(SP_), full(SE), SPM[:, 0:1], wide(SR), ALU.mult, ALU.mult).then_inc(ps_ready, 1)
                    else:
                        v.tensor_tensor(full(SP_), full(SE), wide(SR), ALU.mult).then_inc(ps_ready, 1)

                def maxima(u):
                    l = u // 2
                    ns = len(SEGS[l])
                    dve.wait_ge(m1_ready, level(m1_ready, it, u + 1))
                    v.tensor_tensor(MP[0:ns * H, 1, :], MI[0:ns * H, 0:SQ], MP[0:ns * H, 0, :],
                                                ALU.subtract).then_inc(m2_ready, 1)
                    if l < 2:
                        dve.wait_ge(s_used, level(s_used, it, (u + 1) * H))
                        dve.wait_ge(pst_ready, level(pst_ready, it, small_nth(u) - 1))
                        if l == 1:
                            for g in range(2):
                                step(v.scalar_tensor_tensor(
                                    SM[:, g, :, :], SM[:, g, :, :], SCALE,
                                    MSK[:, it * 2 + u % 2, g, :].rearrange("p (o n) -> p o n", o=1)
                                    .to_broadcast([SQ, H, 4]), ALU.mult, ALU.add))
                        small_softmax(u, SM)

                def back(u, g):
                    l, par = u // 2, u % 2
                    gn = u * GROUPS + g
                    ns = len(SEGS[l])
                    if l == 3:
                        for i in range(NT):
                            n = (par * GROUPS + g) * NT + i
                            r = rows_of(3, i)
                            dve.wait_ge(kv_ready, level(kv_ready, it, N_PIECES + n + 1))
                            if i == 1:
                                dve.wait_ge(pv_done, level(pv_done, it, gn))
                            else:
                                dve.wait_ge(zt_used, level(zt_used, it, 2 * (par * GROUPS + g) + i // 2))
                            v.tensor_tensor(ZT[n % 2][0:r, :], KVB[(N_PIECES + n) % 2][0:r, 0:4 * SQ],
                                                       PT[gn % 2][0:r, i, :], ALU.mult).then_inc(z_ready, 1)
                    dve.wait_ge(pv_done, level(pv_done, it, gn + 1))
                    if g == 0:
                        dve.wait_ge(o2_ready, level(o2_ready, it, u))
                    v.tensor_copy(OTS[:, g, 0:ns, :], OT[:, 0:ns * SQ].rearrange("p (s q) -> p s q", s=ns)).then_inc(ot_used, 1)

                def parts(s, lo, hi):
                    return [([SB_[0], MI][s][0:SQ, 0:512].rearrange("p (h c) -> p h c", c=32)[:, :, lo:hi], 0, 16),
                            (SB_[1][0:SQ, s * 128:s * 128 + 128].rearrange("p (h c) -> p h c", c=32)[:, :, lo:hi], 16, H)]

                def final(u):
                    l, par = u // 2, u % 2
                    ns = len(SEGS[l])
                    dve.wait_ge(o2_ready, level(o2_ready, it, u + 1))
                    dve.wait_ge(otf_ready, level(otf_ready, it, u))
                    for s in range(ns):
                        for src_, h0, h1 in parts(s, ONE_COL, ONE_COL + 1):
                            step(v.reciprocal(ZR[:, s, h0:h1].rearrange("p (h o) -> p h o", o=1), src_))
                    for s in range(ns):
                        dst = [OS, O2][s]
                        for src_, h0, h1 in parts(s, 0, D):
                            ins_ = v.tensor_tensor(dst[:, h0 * D:h1 * D].rearrange("p (h c) -> p h c", c=D), src_,
                                                   ZR[:, s, h0:h1].rearrange("p (h o) -> p h o", o=1)
                                                   .to_broadcast([SQ, h1 - h0, D]), ALU.mult)
                            if h0 == 0 or s < ns - 1 or ns == 2 or l == 3:
                                step(ins_)
                    if l == 3:
                        for src_, h0, h1 in parts(0, N_COL, N_COL + 1):
                            v.tensor_scalar(QN[:, 0, h0:h1].rearrange("p (h o) -> p h o", o=1), src_, 0.0,
                                                        None, ALU.max).then_inc(sq_ready, 1)
                        dve.wait_ge(sq_done, level(sq_done, it, par + 1))
                        for src_, h0, h1 in parts(0, ONE_COL, ONE_COL + 1):
                            step(v.scalar_tensor_tensor(QN[:, 1, h0:h1].rearrange("p (h o) -> p h o", o=1), src_, EPS,
                                                        QN[:, 0, h0:h1].rearrange("p (h o) -> p h o", o=1),
                                                        ALU.mult, ALU.max))
                        step(v.reciprocal(QN[:, 2, :], QN[:, 1, :]))
                        for src_, h0, h1 in parts(0, R_COL, R_COL + 4):
                            ins_ = v.tensor_tensor(QS[:, h0:h1, :], src_, QN[:, 2, h0:h1].rearrange("p (h o) -> p h o", o=1)
                                                   .to_broadcast([SQ, h1 - h0, 4]), ALU.mult)
                            if h0 == 0:
                                step(ins_)
                        ins_.then_inc(o_ready, 1)
                        dve.wait_ge(o_ready, level(o_ready, it, u + 1))
                        step(v.scalar_tensor_tensor(QS[:, :, :], QS[:, :, :], SEM_SCALE,
                                                    IPI[:, it * 2 + u % 2, :].rearrange("p (o n) -> p o n", o=1)
                                                    .to_broadcast([SQ, H, 4]), ALU.mult, ALU.mult))
                        step(v.scalar_tensor_tensor(QS[:, :, :], SM3[u % 2][:, 0, :, :], SCALE, QS[:, :, :],
                                                    ALU.mult, ALU.add))
                        dve.wait_ge(pst_ready, level(pst_ready, it, small_nth(u) - 1))
                        small_softmax(u, QS[:, :, :].rearrange("p (g h) n -> p g h n", g=1))
                    elif ns == 2:
                        v.tensor_tensor(OS[:, :], OS[:, :], O2[:, :], ALU.add).then_inc(o_ready, 1)
                    else:
                        ins_.then_inc(o_ready, 1)

                def result(u):
                    l, par = u // 2, u % 2
                    dve.wait_ge(y_ready, level(y_ready, it, u + 1))
                    for t, (c0, cn) in enumerate(CH):
                        x = XT[par][0:cn, t, :]
                        last = v.scalar_tensor_tensor(x, MI[0:cn, t * SQ:(t + 1) * SQ], BIAS[0:cn, l, t:t + 1], x,
                                                      ALU.add, ALU.add)
                    last.then_inc(x_ready, 1)

                for p in range(len(PIECES[0])):
                    kv_piece(0, p)
                for s in range(UNITS + 1):
                    if s < UNITS:
                        queries(s)
                    kv_place(s, 0)
                    for g in range(GROUPS):
                        if s < UNITS:
                            max_of(s, g)
                        if s >= 1 and g >= 1:
                            back(s - 1, g - 1)
                        kv_place(s, 1 + g)
                    if s >= 1:
                        back(s - 1, GROUPS - 1)
                    if s < UNITS:
                        maxima(s)
                    kv_place(s, 6)
                    kv_place(s, 7)
                    if s >= 1:
                        final(s - 1)
                    kv_place(s, 8)
                    if s >= 1:
                        result(s - 1)
                    kv_place(s, 9)

                assert steps[0] == DVE_STEPS, steps[0]

        @block.gpsimd
        def _(pool):
            g_ = nc.gpsimd
            pool.wait_ge(vs_copied, 5)
            pool.wait_ge(ks_copy, 1)
            for k in range(3):
                g_.memset(KP[k][PROWS:PROWS + 4, :, TXT:T], 0.0)
                g_.memset(KP[k][PROWS:PROWS + 4, :, 0:TXT], 1.0)
            g_.memset(TI[:, 0:TXT], 0.0)
            g_.memset(TI[:, TXT:T], 1.0).then_inc(pool_set, 1)
            pool.wait_ge(const_in, 16 * CONSTS)

            for sig in [k3_ready, ones_ready, vb_ready]:
                pool.sem_inc(sig, 1)
            with pool.Fori(0, PAIRS) as it:
                def kv_piece(u, p):
                    l, par = u // 2, u % 2
                    kind, i = PIECES[l][p]
                    if kind == "K":
                        cn, m = CH[i][1], MAIN[l]
                        pool.wait_ge(pv_done, level(pv_done, it, (u - 2) * GROUPS))
                        pool.wait_ge(k2_ready, level(k2_ready, it, 3 * u + i + 1))
                        last = g_.tensor_tensor(KC[i][0:cn, 2, 0:m], KR[i][0:cn, 0:m], KC[i][0:cn, 1, 0:m],
                                                ALU.subtract)
                        for k, grp in enumerate(SMALL[l]):
                            last = g_.tensor_copy(KC[i][:, :, m + 4 * k:m + 4 * k + 4],
                                                  KSM[:, :, grp, i, it * 2 + par, :])
                        last.then_inc(k3_ready, 1)
                    elif kind == "V" and i == 0:
                        pool.wait_ge(pv_done, level(pv_done, it, (u - 2) * GROUPS))
                        col = 1 if len(SEGS[l]) == 2 else 0
                        marks = IPM[:, col:col + 1].rearrange("p (o i) -> p o i", o=1).to_broadcast([128, H, 1])
                        g_.tensor_tensor(VA[u % 3][:, 0, :, ONE_COL:ONE_COL + 1], marks, marks, ALU.mult).then_inc(ones_ready, 1)

                def kv_place(s, place):
                    for p in at_place(s + 1, place):
                        kv_piece(s + 1, p)

                for p in range(len(PIECES[0])):
                    kv_piece(0, p)
                for s in range(UNITS + 1):
                    kv_place(s, 0)
                    if s >= 1 and n_small[s - 1]:
                        u = s - 1
                        pool.wait_ge(vr_in, level(vr_in, it, 16 * sum(n_small[:u + 1])))
                        pool.wait_ge(otf_ready, level(otf_ready, it, u))
                        for k in range(n_small[u]):
                            last = g_.tensor_tensor(VB[:, k, :], VR[:, k, :], HM[:, :], ALU.mult)
                        last.then_inc(vb_ready, 1)
                    for place in range(1, 10):
                        kv_place(s, place)


CONSTS = 6 + 4 * NT
SETUP_STEPS = 49
DVE_STEPS = 84


def kernel(**inputs):
    import numpy as np
    import concourse.bacc as bacc
    from concourse.bass_utils import run_bass_kernel_spmd

    def arr(name):
        return np.asarray(inputs[name])

    ctx = arr("ctx_2048").transpose(0, 2, 1)
    order0 = list(range(TXT)) + list(range(TXT + 8, T)) + list(range(TXT, TXT + 8))
    small = list(range(TXT, TXT + 8)) + list(range(T - 8, T))
    data = {
        "x_t": arr("x").transpose(0, 2, 1),
        "ctx0": ctx[:, :, order0],
        "ctx1": ctx,
        "ctx_small": ctx[:, :, small].reshape(B, CC, 4, 4).transpose(1, 2, 0, 3).reshape(CC, 4, 4 * B),
        "boxes": arr("fside_Bx4x4_0"),
        "spatial": arr("fside_S_0").reshape(SQ, 1),
    }
    names = {
        "L0_q": "L0_xattn_to_q_w", "L0_k": "L0_xattn_to_k_w", "L0_v": "L0_xattn_to_v_w",
        "L0_kip": "L0_xattn_to_k_ip_w", "L0_vip": "L0_xattn_to_v_ip_w", "L0_o": "L0_xattn_to_out_w",
        "S0_k": "L0_xattn_to_k_object_w", "S0_v": "L0_xattn_to_v_object_w",
        "S1_k": "L0_xattn_to_k_others_w", "S1_v": "L0_xattn_to_v_others_w",
        "L1_q": "L1_xattn_w_q", "L1_k": "L1_xattn_w_k", "L1_v": "L1_xattn_w_v", "L1_o": "L1_xattn_w_out",
        "S2_k": "L1_xattn_w_k_ip", "S2_v": "L1_xattn_w_v_ip",
        "L3_q": "L3_xattn_W_q", "L3_k": "L3_xattn_W_k", "L3_v": "L3_xattn_W_v", "L3_o": "L3_xattn_W_out",
        "S4_k": "L3_xattn_W_k_ip", "S4_v": "L3_xattn_W_v_ip",
    }
    for short, name in names.items():
        data[short] = arr(name)
    by_channel = np.concatenate([c0 + np.arange(cn).reshape(cn // D, D).T.ravel() for c0, cn in CH])
    for short, name in {"L2_q": "Wq", "L2_k": "Wk", "L2_v": "Wv", "L2_kip": "Wk_ip", "L2_vip": "Wv_ip", "L2_o": "Wo"}.items():
        data[short] = arr("L2_xattn_" + name).T
    for short in data:
        if short.endswith(("_q", "_k", "_kip")):
            data[short] = data[short][:, by_channel]
    for l, name in enumerate(["L0_xattn_to_out_b", "L1_xattn_b_out", "L2_xattn_bo", "L3_xattn_b_out"]):
        data[f"L{l}_b"] = arr(name).reshape(C, 1)
    f = np.float32
    gh, gw = 8, 14
    data["ident"] = np.eye(128, dtype=f)
    data["head_mask"] = (np.arange(80)[:, None] // 4 == np.arange(C)[None, :] // D).astype(f)
    q = np.arange(SQ)
    data["grid"] = np.stack([(q % gw).astype(f) / f(gw - 1), (q // gw).astype(f) / f(gh - 1)], 1).astype(f)
    data["image_rows"] = np.stack([np.ones(128, f), (np.arange(128) >= TXT).astype(f)], 1)

    nc = bacc.Bacc("TRN2", target_bir_lowering=False, num_devices=1, dynamic_dma_scratch_size=512)
    arrays, ins = {}, {}
    for name, a in data.items():
        a = np.ascontiguousarray(a)
        arrays["in_" + name] = a
        ins[name] = nc.dram_tensor("in_" + name, a.shape, mybir.dt.from_np(a.dtype), kind="ExternalInput").ap()
    out_t = nc.dram_tensor("out_t", (B, C, SQ), F32, kind="ExternalOutput").ap()
    build(nc, ins, out_t)
    r = run_bass_kernel_spmd(nc, [arrays], core_ids=[0])
    return np.ascontiguousarray(r.results[0]["out_t"].transpose(0, 2, 1))
```

```python
from contextlib import ExitStack

import concourse.bass as bass
from concourse import mybir

F32 = mybir.dt.float32
BF16 = mybir.dt.bfloat16
ACT = mybir.ActivationFunctionType
ALU = mybir.AluOpType
AX = mybir.AxisListType

B, SQ, C, T, CC = 8, 112, 320, 375, 512
H, D = 20, 16
SCALE = D ** -0.5
NEG = -10000.0
EPS = 1e-12
SEM_SCALE = 0.5
TXT = 77
MAIN = [367, 367, 375, 371]
SEGS = [[(0, TXT), (TXT, 367)], [(0, 367)], [(0, TXT), (TXT, 375)], [(0, 371)]]
SMALL = [[0, 1], [2, 3], [], [4]]
QUAD = [0, 1, 2, 3, 3]
NCK = CC // 128
CH = [(0, 128), (128, 128), (256, 64)]
NT = 3
PAIRS = B // 2
UNITS = 8
GROUPS = 5
VW = 22
ONE_COL, R_COL, N_COL = 16, 17, 21
KPARTS = [0, 0, 0, 1, 1, 2]
QPARTS = [0, 1, 2, 0, 1, 0]
PROWS = 16 * len(KPARTS)
XROWS = PROWS + 4

PIECES = [
    [("K", 0), ("K", 1), ("K", 2), ("VT", 0), ("V", 0), ("V", 1), ("V", 2)],
    [("K", 0), ("K", 1), ("K", 2), ("V", 0), ("V", 1), ("V", 2)],
    [("K", 0), ("K", 1), ("K", 2), ("VT", 0), ("V", 0), ("V", 1), ("V", 2)],
    [("K", 0), ("K", 1), ("K", 2), ("V", 0), ("V", 1), ("V", 2), ("G", 0), ("G", 1), ("G", 2)],
]
SLOT_FIRST = "spspspsppQppsspspsppspspss"
SLOT = "ssbbspbsvtbbspbVsosbbspbVsopsbbsbVsosbbsbVsopVsopHsTpRspQ"
SLOT_GRAM = "ssvbbsbbb" + 3 * "VggzbsngzsnzssnbboM" + "VggzbsngzsnzssnoVggzngzsnzssnoMHTR"


def plan(s):
    text = {-1: "Qq", 0: SLOT_FIRST, UNITS - 1: SLOT_GRAM, UNITS: SLOT_GRAM}.get(s, SLOT)
    front = 0 <= s < UNITS
    total = {"s": H if front else 0, "p": 2 * len(PIECES[(s + 1) // 2]) if s + 1 < UNITS else 0,
             "t": 1 if 1 <= s <= 4 else 0}
    if s != UNITS - 1:
        text = text.replace("M", "")
        for kind, number in [("s", total["s"]), ("p", text.count("p") + 1), ("M", int(front)),
                             ("q", int(0 <= s < UNITS - 1)), ("p", total["p"])]:
            text += max(number - text.count(kind), 0) * kind
    unit = {"s": s, "M": s, "p": s + 1, "Q": s + 1, "q": s + 1}
    steps, counts, k_parts = [], {}, []
    for kind in text:
        if kind == "M" and counts["s"] < H:
            continue
        n = counts.get(kind, 0)
        if n < total.get(kind, len(text)):
            counts[kind] = n + 1
            if kind == "p":
                kind, n = "hp"[n % 2], n // 2
                steps.append((kind, s + 1, n))
            else:
                steps.append((kind, unit.get(kind, s - 1), n))
            if kind == "p" and PIECES[(s + 1) // 2][n][0] == "K":
                k_parts.append([2, n])
            elif k_parts:
                k_parts[0][0] -= 1
                if k_parts[0][0] <= 0:
                    steps.append(("k", s + 1, k_parts.pop(0)[1]))
    return steps + [("k", s + 1, n) for _, n in k_parts]


BANK_USES = [(u, kind, n) for u in range(UNITS) for kind, n in PIECES[u // 2]]
N_PIECES = len(BANK_USES)
BANK_USES += [(u, "Y", 3 * g + i) for u in (6, 7) for g in range(GROUPS) for i in range(NT)]


def rows_of(l, c):
    return min(128, MAIN[l] - 128 * c)


def piece_index(u, p):
    return sum(len(PIECES[v // 2]) for v in range(u)) + p


def nth(kinds, n):
    return sum(1 for _, kind, _ in BANK_USES[:n + 1] if kind in kinds)


def build(nc, ins, out_t):
    dram_vs = nc.dram_tensor("small_v", (5, B, 4, C), F32, kind="Internal").ap()
    with ExitStack() as ctx:
        def sb(name, shape, dt=F32):
            return ctx.enter_context(nc.sbuf_tensor(name, shape, dt))

        def sem(name):
            return ctx.enter_context(nc.semaphore(name))

        per_pass = {}

        def signal(name, total):
            s = sem(name)
            per_pass[s.name] = total
            return s

        def level(s, it, n):
            return it * per_pass[s.name] + (1 + max(n, 0))

        KV_W = [["L0_k", "L0_v", "L0_kip", "L0_vip"], ["L1_k", "L1_v"],
                ["L2_k", "L2_v", "L2_kip", "L2_vip"], ["L3_k", "L3_v"]]
        W = {n: sb("w_" + n, [128, NCK, C]) for l in (0, 1, 3) for n in KV_W[l]}
        for n0, n2 in zip(KV_W[0], KV_W[2]):
            W[n2] = W[n0]
        WQ = [sb(f"wq{l}", [128, NT, C]) for l in range(4)]
        WO = [sb(f"wo{l}", [128, NT, C]) for l in range(4)]
        BIAS = sb("bias", [128, 4, NT])
        CT = [sb(f"ctx{p}", [128, NCK, T]) for p in range(2)]
        XT = [sb(f"xt{p}", [128, NT, SQ]) for p in range(2)]
        KP_ALL = sb("k_packed", [128, 3 * H * T], BF16)
        KP = [KP_ALL[:, k * H * T:(k + 1) * H * T].rearrange("p (h t) -> p h t", h=H) for k in range(3)]
        WS_NAMES = ["S0_k", "S0_v", "S1_k", "S1_v", "S2_k", "S2_v", "S4_k", "S4_v"]
        KP32 = KP_ALL[:, :].bitcast(F32)
        WS = {n: KP32[:, i * NCK * C:(i + 1) * NCK * C].rearrange("p (k c) -> p k c", k=NCK)
              for i, n in enumerate(WS_NAMES)}
        WS["S3_k"], WS["S3_v"] = WS["S2_k"], WS["S2_v"]
        QP = [sb(f"q_packed{p}", [128, H, SQ], BF16) for p in range(2)]
        VA = [sb(f"v{k}", [128, NT, H, VW]) for k in range(3)]
        VT = [sb(f"v_text{p}", [128, H, VW]) for p in range(2)]
        KC01 = sb("k_parts01", [128, 3, 2, T], BF16)
        KC = [KC01[:, :, 0, :], KC01[:, :, 1, :], sb("k_parts2", [128, 3, T], BF16)]
        KR = [sb(f"k_rest{t}", [128, T]) for t in range(NT)]
        QC = sb("q_parts", [128, 3, NT * SQ], BF16)
        QR = sb("q_rest", [128, NT * SQ])
        PT = [sb(f"probs{k}", [128, NT, 4 * SQ]) for k in range(2)]
        ZT = [sb(f"gp{k}", [128, 4 * SQ]) for k in range(2)]
        GM_ALL = sb("gram", [128, 2, NT, 384])
        GM = [GM_ALL[:, p, :, :] for p in range(2)]
        SETUP = GM_ALL[:, :, :, :].rearrange("p a b c -> p (a b c)")
        OTS = sb("o_heads", [128, GROUPS, 2, SQ])
        MX = sb("neg_max", [SQ, 4 * H])
        MP = sb("max_parts", [2 * H, 2, SQ], BF16)
        SM = sb("small_scores", [SQ, 2, H, 4])
        SM3 = [sb(f"small_scores3{p}", [SQ, 1, H, 4]) for p in range(2)]
        SE = sb("small_exp", [SQ, 2, H, 4])
        SP_ = sb("small_probs", [SQ, 2, H, 4])
        SX = sb("small_max", [SQ, 2 * H])
        SS = sb("small_sum", [SQ, 2 * H])
        SR = sb("small_rec", [SQ, 2 * H])
        QN = sb("sem_norm", [SQ, 3, H])
        QS = sb("sem", [SQ, H, 4])
        PST = [sb(f"small_probs_t{p}", [80, 2, SQ]) for p in range(2)]
        VR = sb("small_v_rep", [80, 2, C])
        VB = sb("small_v_blk", [80, 2, C])
        ZR = sb("z_rec", [SQ, 2, H])
        OS = sb("o_sum", [SQ, C])
        O2 = sb("o_second", [SQ, C])
        OTF = sb("o_t", [128, NT, SQ])
        KSM = sb("small_k_parts", [128, 3, 5, NT, B, 4], BF16)
        KSR = SETUP[:, 1600:1600 + 5 * NT * B * 4]
        CS = sb("ctx_small", [128, NCK, 4, B * 4])
        SQI = sb("ip_squares", [128, NCK, B * 4])
        IPI = sb("ip_inv_norm", [SQ, B, 4])
        VSB = SETUP[0:32, 0:5 * C].rearrange("p (g c) -> p g c", g=5)
        BB = sb("boxes", [SQ, B, 4, 4])
        IN = sb("inside", [SQ, 4, B, 4])
        MSK = sb("ip_mask", [SQ, B, 2, 4])
        ANY = sb("any_inside", [SQ, B])
        IDN = sb("ident", [128, 128])
        HM = sb("head_mask", [80, C])
        GXY = sb("grid", [SQ, 2])
        IPM = sb("image_rows", [128, 2])
        SPM = sb("spatial", [SQ, 1])
        ONES = sb("ones", [128, 128])
        NSEL = sb("norm_select", [128, VW])
        TI = sb("image_cols", [2, T], BF16)

        def bank(name):
            return ctx.enter_context(nc.psum_tensor(name, [128, 512], F32))

        SB_ = [bank("scores0"), bank("scores1")]
        ST = [bank("scores_t0"), bank("scores_t1")]
        KVB = [bank("kv0"), bank("kv1")]
        OT = bank("o_acc")
        MI = bank("misc")
        ALL_BANKS = SB_ + ST + KVB + [OT, MI]

        w_in = [sem(f"w_in{l}") for l in range(4)]
        small_in = sem("small_in")
        const_in = sem("const_in")
        rows_in = sem("rows_in")
        zeroed = sem("zeroed")
        pool_set = sem("pool_set")
        ks_ready = sem("ks_ready")
        ks_copy = sem("ks_copy")
        vs_ready = sem("vs_ready")
        vs_copied = sem("vs_copied")
        vs_stored = sem("vs_stored")
        ip_sq = sem("ip_sq")
        ip_summed = sem("ip_summed")
        ip_sqrt = sem("ip_sqrt")
        ip_ready = sem("ip_ready")
        setup_step = sem("setup_step")

        n_small = [len(SMALL[u // 2]) for u in range(UNITS)]
        ctx_in = [signal(f"ctx_in{p}", 32) for p in range(2)]
        xt_in = [signal(f"xt_in{p}", 32) for p in range(2)]
        kv_ready = signal("kv_ready", len(BANK_USES))
        k1_ready = signal("k1_ready", 3 * UNITS)
        k_rest = signal("k_rest", 3 * UNITS)
        k2_ready = signal("k2_ready", 3 * UNITS)
        k3_ready = signal("k3_ready", 3 * UNITS)
        v_ready = signal("v_ready", nth(("V", "VT"), N_PIECES))
        ones_ready = signal("ones_ready", UNITS)
        g_ready = signal("g_ready", 6)
        z_ready = signal("z_ready", 2 * GROUPS * NT)
        k_packed = [signal(f"k_packed{t}", 96 * UNITS) for t in ("01", "2")]
        q_packed = [signal(f"q_packed{t}", 96 * UNITS) for t in ("01", "2")]
        m_packed = signal("m_packed", 64 * UNITS)
        zt_used = signal("zt_used", 2 * GROUPS * 2)
        q_ready = signal("q_ready", UNITS)
        q1_ready = signal("q1_ready", UNITS)
        q_rest = signal("q_rest", UNITS)
        q2_ready = signal("q2_ready", UNITS)
        q3_ready = signal("q3_ready", UNITS)
        s_ready = signal("s_ready", H * UNITS)
        s_used = signal("s_used", H * UNITS)
        m_ready = signal("m_ready", UNITS)
        m1_ready = signal("m1_ready", UNITS)
        m2_ready = signal("m2_ready", UNITS)
        st_ready = signal("st_ready", UNITS * GROUPS * NT)
        exp_done = signal("exp_done", UNITS * GROUPS * NT)
        pv_done = signal("pv_done", UNITS * GROUPS)
        ot_used = signal("ot_used", UNITS * GROUPS)
        sq_ready = signal("sq_ready", 4)
        sq_done = signal("sq_done", 2)
        sx_ready = signal("sx_ready", 6)
        se_ready = signal("se_ready", 6)
        ps_ready = signal("ps_ready", 6)
        pst_ready = signal("pst_ready", 6)
        pst_copied = signal("pst_copied", 6)
        w0_in = signal("w0_in", 2 * 64)
        vr_in = signal("vr_in", 16 * sum(n_small))
        vb_ready = signal("vb_ready", 6)
        o2_ready = signal("o2_ready", UNITS)
        o_ready = signal("o_ready", UNITS)
        otf_ready = signal("otf_ready", UNITS)
        otf_copied = signal("otf_copied", UNITS)
        y_ready = signal("y_ready", UNITS)
        x_ready = signal("x_ready", UNITS)
        stored = [signal(f"stored{p}", 32) for p in range(2)]
        dve_step = signal("dve_step", DVE_STEPS)

        def small_nth(u):
            return sum(1 for v in range(u + 1) if n_small[v])

        block = ctx.enter_context(nc.Block())

        @block.sync
        def _(sp):
            def load_w(name, dst, s):
                sp.dma_start(dst[:, :, :], ins[name].rearrange("(k p) c -> p k c", p=128)).then_inc(s, 16)

            def load_wo(name, dst, s):
                sp.dma_start(dst[:, 0:2, :], ins[name][0:256, :].rearrange("(k p) c -> p k c", p=128)).then_inc(s, 16)
                sp.dma_start(dst[0:64, 2, :], ins[name][256:C, :]).then_inc(s, 16)

            sp.dma_start(CS[:, :, :, :], ins["ctx_small"].rearrange("(k p) g n -> p k g n", p=128)).then_inc(small_in, 16)
            for n in WS_NAMES:
                load_w(n, WS[n], small_in)
            sp.dma_start(IDN[:, :], ins["ident"]).then_inc(const_in, 16)
            sp.dma_start(HM[:, :], ins["head_mask"]).then_inc(const_in, 16)
            sp.dma_start(GXY[:, :], ins["grid"]).then_inc(const_in, 16)
            sp.dma_start(IPM[:, :], ins["image_rows"]).then_inc(const_in, 16)
            sp.dma_start(SPM[:, :], ins["spatial"]).then_inc(const_in, 16)
            sp.dma_start(BB[:, :, :, :], ins["boxes"].rearrange("(o b) m c -> o b m c", o=1)
                         .to_broadcast([SQ, B, 4, 4])).then_inc(const_in, 16)
            for l in range(4):
                for t, (c0, cn) in enumerate(CH):
                    sp.dma_start(BIAS[0:cn, l, t:t + 1], ins[f"L{l}_b"][c0:c0 + cn, :]).then_inc(const_in, 16)
            for l in range(4):
                for n in KV_W[l] if l in (1, 3) else []:
                    load_w(n, W[n], w_in[l])
                load_wo(f"L{l}_q", WQ[l], w_in[l])
                load_wo(f"L{l}_o", WO[l], w_in[l])
            sp.wait_ge(vs_copied, 5)
            sp.dma_start(dram_vs.rearrange("g b n c -> (b n) g c"), VSB[:, :, :]).then_inc(vs_stored, 16)
            sp.wait_ge(pool_set, 1)
            for k in range(3):
                sp.dma_start(KP[k][PROWS + 2:PROWS + 4, :, :],
                             TI[:, :].rearrange("p (o t) -> p o t", o=1).to_broadcast([2, H, T])).then_inc(rows_in, 16)
            sp.wait_ge(vs_stored, 16)

            for sig in k_packed + q_packed + [m_packed, w0_in]:
                sp.sem_inc(sig, 1)

            def load_kv_weights(l):
                for n in KV_W[l]:
                    sp.dma_start(W[n][:, :, :], ins[n].rearrange("(k p) c -> p k c", p=128)).then_inc(w0_in, 16)

            load_kv_weights(0)
            with sp.Fori(0, PAIRS) as it:
                def pack_k(u, p):
                    kind, t = PIECES[u // 2][p]
                    if kind != "K" or t == 0:
                        return
                    sp.wait_ge(k3_ready, level(k3_ready, it, 3 * u + t + 1))
                    for r, part in enumerate(KPARTS):
                        rows = KP[u % 3][D * r:D * r + D, :, :]
                        if t == 1:
                            sp.dma_start(rows[:, 0:16, :], KC01[:, part, :, :]).then_inc(k_packed[0], 16)
                        else:
                            sp.dma_start(rows[:, 16:H, :], KC[2][0:64, part, :]).then_inc(k_packed[1], 16)

                def pack_q(u):
                    sp.wait_ge(q3_ready, level(q3_ready, it, u + 1))
                    for r, part in enumerate(QPARTS):
                        rows = QP[u % 2][D * r:D * r + D, :, :]
                        sp.dma_start(rows[:, 0:16, :], QC[:, part, 0:2 * SQ]).then_inc(q_packed[0], 16)

                def pack_q_rest(u):
                    for r, part in enumerate(QPARTS):
                        rows = QP[u % 2][D * r:D * r + D, :, :]
                        sp.dma_start(rows[:, 16:H, :], QC[0:64, part, 2 * SQ:]).then_inc(q_packed[1], 16)

                def pack_m(u):
                    sp.wait_ge(m2_ready, level(m2_ready, it, u + 1))
                    last = len(SEGS[u // 2]) - 1
                    for s in range(2):
                        for part in range(2):
                            row = PROWS + 2 * s + part
                            sp.dma_start(
                                QP[u % 2][row:row + 1, :, :],
                                MP[H * min(s, last):H * min(s, last) + H, part, :]).then_inc(m_packed, 16)

                for s in range(-1, UNITS + 1):
                    if s == 1:
                        sp.wait_ge(kv_ready, level(kv_ready, it, piece_index(2, 0)))
                        load_kv_weights(2)
                    if s == 5:
                        sp.wait_ge(kv_ready, level(kv_ready, it, piece_index(6, 0)))
                        load_kv_weights(0)
                    for kind, u, n in plan(s):
                        if kind == "Q":
                            pack_q(u)
                        elif kind == "q":
                            pack_q_rest(u)
                        elif kind == "p":
                            pack_k(u, n)
                        elif kind == "M":
                            pack_m(u)
            sp.wait_ge(w0_in, 1 + 64 + PAIRS * per_pass[w0_in.name])
            sp.wait_ge(ctx_in[0], 1 + 16 + PAIRS * per_pass[ctx_in[0].name])
            sp.wait_ge(ctx_in[1], 1 + 16 + PAIRS * per_pass[ctx_in[1].name])
            sp.wait_ge(xt_in[0], 1 + 32 + PAIRS * per_pass[xt_in[0].name])
            for p in range(2):
                sp.wait_ge(stored[p], 1 + PAIRS * per_pass[stored[p].name])

        @block.tensor
        def _(pe):
            mm = nc.tensor.matmul
            pe.wait_ge(zeroed, 1)
            pe.wait_ge(small_in, 16 * (1 + len(WS_NAMES)))
            for g in range(5):
                for t, (c0, cn) in enumerate(CH):
                    for k in range(NCK):
                        last = mm(MI[0:cn, (g * NT + t) * 32:(g * NT + t) * 32 + 32], WS[f"S{g}_k"][:, k, c0:c0 + cn],
                                  CS[:, k, QUAD[g], :], start=(k == 0), stop=(k == NCK - 1))
            last.then_inc(ks_ready, 1)
            for g in range(5):
                for k in range(NCK):
                    last = mm(ALL_BANKS[g][0:32, 0:C], CS[:, k, QUAD[g], :],
                              WS[f"S{g}_v"][:, k, :], start=(k == 0), stop=(k == NCK - 1))
                last.then_inc(vs_ready, 1)
            pe.wait_ge(ip_sq, 1)
            mm(ALL_BANKS[5][0:SQ, 0:NCK * 32], ONES[:, 0:SQ], SQI[:, :, :].rearrange("p k n -> p (k n)"),
               start=True, stop=True).then_inc(ip_ready, 1)
            pe.wait_ge(const_in, 16 * CONSTS)
            pe.wait_ge(rows_in, 48)
            pe.wait_ge(setup_step, SETUP_STEPS)
            pe.wait_ge(vs_copied, 5)
            for l in range(4):
                pe.wait_ge(w_in[l], 16 * (4 + (len(KV_W[l]) if l in (1, 3) else 0)))

            for sig in [kv_ready, q_ready, s_ready, m_ready, st_ready, pv_done, zt_used, pst_ready, o2_ready,
                        otf_ready, y_ready]:
                pe.sem_inc(sig, 1)
            with pe.Fori(0, PAIRS) as it:
                def bank_free(n):
                    kind = BANK_USES[n - 2][1] if n >= 2 else "Y"
                    m = n - 2 if n >= 2 else -1
                    sig, kinds = {"K": (k_rest, ("K",)), "V": (v_ready, ("V", "VT")), "VT": (v_ready, ("V", "VT")),
                                  "G": (g_ready, ("G",)), "Y": (z_ready, ("Y",))}[kind]
                    pe.wait_ge(sig, level(sig, it, nth(kinds, m) if m >= 0 else 0))

                def kv_piece(u, p, half):
                    l, par = u // 2, u % 2
                    kind, i = PIECES[l][p]
                    n = piece_index(u, p)
                    dst = KVB[n % 2]
                    if half == 0:
                        if p == 0:
                            pe.wait_ge(ctx_in[par], level(ctx_in[par], it, 16 if l == 0 else 32))
                            if l in (0, 2):
                                pe.wait_ge(w0_in, level(w0_in, it, 64 * (l // 2 + 1)))
                        bank_free(n)
                    chunks = range(2 * half, 2 * half + 2)
                    if kind == "K":
                        c0, cn = CH[i]
                        t0, t1 = SEGS[l][-1]
                        w = W[f"L{l}_k" + ("ip" if t0 else "")]
                        for k in chunks:
                            last = mm(dst[0:cn, t0:t1], w[:, k, c0:c0 + cn], CT[par][:, k, t0:t1],
                                      start=(k == 0), stop=(k == NCK - 1))
                        if t0 and half == 1:
                            for k in range(NCK):
                                last = mm(dst[0:cn, 0:TXT], W[f"L{l}_k"][:, k, c0:c0 + cn], CT[par][:, k, 0:TXT],
                                          start=(k == 0), stop=(k == NCK - 1))
                    elif kind == "VT":
                        for k in chunks:
                            last = mm(dst[0:TXT, 0:C], CT[par][:, k, 0:TXT], W[f"L{l}_v"][:, k, :],
                                      start=(k == 0), stop=(k == NCK - 1))
                    elif kind == "V":
                        w = W[f"L{l}_v" + ("ip" if len(SEGS[l]) == 2 else "")]
                        r = rows_of(l, i)
                        for k in chunks:
                            last = mm(dst[0:r, 0:C], CT[par][:, k, 128 * i:128 * i + r], w[:, k, :],
                                      start=(k == 0), stop=(k == NCK - 1))
                        if l == 3 and half == 1:
                            for k in range(NCK):
                                last = mm(dst[0:r, C:C + 4], CT[par][:, k, 128 * i:128 * i + r],
                                          CT[par][:, k, MAIN[3]:T], start=(k == 0), stop=(k == NCK - 1))
                    else:
                        r, wd = rows_of(3, i), min(128 * i + 128, MAIN[3])
                        for k in chunks:
                            last = mm(dst[0:r, 0:wd], CT[par][:, k, 128 * i:128 * i + r], CT[par][:, k, 0:wd],
                                      start=(k == 0), stop=(k == NCK - 1))
                    if half == 1:
                        last.then_inc(kv_ready, 1)

                def queries(u):
                    l, par = u // 2, u % 2
                    if l == 0:
                        pe.wait_ge(xt_in[par], level(xt_in[par], it, 32))
                    pe.wait_ge(x_ready, level(x_ready, it, u - 1))
                    if u == 1:
                        pe.wait_ge(q_rest, level(q_rest, it, 1))
                    for t, (c0, cn) in enumerate(CH):
                        for k, (_, kn) in enumerate(CH):
                            last = mm(MI[0:cn, t * SQ:(t + 1) * SQ], WQ[l][0:kn, k, c0:c0 + cn],
                                      XT[par][0:kn, k, :], start=(k == 0), stop=(k == NT - 1))
                    last.then_inc(q_ready, 1)

                def scores(u, h):
                    if h == 0:
                        pe.wait_ge(q_packed[0], level(q_packed[0], it, 96 * (u + 1)))
                        pe.wait_ge(k_packed[0], level(k_packed[0], it, 96 * (u + 1)))
                    if h == 16:
                        pe.wait_ge(q_packed[1], level(q_packed[1], it, 96 * (u + 1)))
                        pe.wait_ge(k_packed[1], level(k_packed[1], it, 96 * (u + 1)))
                    n = u * H + h
                    pe.wait_ge(s_used, level(s_used, it, n - 1))
                    mm(SB_[n % 2][0:SQ, 0:T], QP[u % 2][0:PROWS, h, :], KP[u % 3][0:PROWS, h, :],
                       start=True, stop=True).then_inc(s_ready, 1)

                def maxima(u):
                    pe.wait_ge(s_used, level(s_used, it, (u + 1) * H))
                    pe.wait_ge(q_rest, level(q_rest, it, min(u + 2, UNITS)))
                    nc.tensor.transpose(MI[0:4 * H, 0:SQ], MX[:, :], IDN[0:SQ, 0:SQ]).then_inc(m_ready, 1)

                def small_t(u):
                    if u // 2 < 2:
                        pe.wait_ge(m2_ready, level(m2_ready, it, u + 1))
                    pe.wait_ge(ps_ready, level(ps_ready, it, small_nth(u)))
                    for k in range(n_small[u]):
                        last = nc.tensor.transpose(MI[0:80, (k + 1) * 128:(k + 1) * 128 + SQ],
                                                   SP_[:, k, :, :].rearrange("p h n -> p (h n)"), IDN[0:SQ, 0:SQ])
                    last.then_inc(pst_ready, 1)

                def back_scores(u, k):
                    g, c = k // NT, k % NT
                    if k == 0:
                        pe.wait_ge(m_packed, level(m_packed, it, 64 * (u + 1)))
                        pe.wait_ge(o_ready, level(o_ready, it, u))
                    n = u * GROUPS * NT + k
                    r = rows_of(u // 2, c)
                    pe.wait_ge(exp_done, level(exp_done, it, n - 1))
                    for j in range(4):
                        h = 4 * g + j
                        last = mm(ST[n % 2][0:r, j * SQ:(j + 1) * SQ],
                                  KP[u % 3][0:XROWS, h, 128 * c:128 * c + r], QP[u % 2][0:XROWS, h, :],
                                  start=True, stop=True)
                    last.then_inc(st_ready, 1)

                def back_values(u, g):
                    l, par = u // 2, u % 2
                    gn = u * GROUPS + g
                    ns = len(SEGS[l])
                    if g == 0:
                        pe.wait_ge(v_ready, level(v_ready, it, nth(("V", "VT"), piece_index(u + 1, 0) - 1)))
                        pe.wait_ge(ones_ready, level(ones_ready, it, u + 1))
                        if l == 3:
                            pe.wait_ge(g_ready, level(g_ready, it, 3 * (par + 1)))
                    pe.wait_ge(ot_used, level(ot_used, it, gn))
                    o0 = (ns - 1) * SQ
                    pt = PT[gn % 2]
                    for c in range(NT):
                        pe.wait_ge(exp_done, level(exp_done, it, gn * NT + c + 1))
                        r = rows_of(l, c)
                        if c == 0 and ns == 2:
                            for j in range(4):
                                mm(OT[32 * j:32 * j + VW, 0:SQ], VT[par][0:TXT, 4 * g + j, :],
                                   pt[0:TXT, 0, j * SQ:(j + 1) * SQ], start=True, stop=True, tile_position=(0, 32 * j))
                        for j in range(4):
                            last = mm(OT[32 * j:32 * j + VW, o0:o0 + SQ], VA[u % 3][0:r, c, 4 * g + j, :],
                                      pt[0:r, c, j * SQ:(j + 1) * SQ], start=(c == 0), stop=(c == 2 and l < 3),
                                      tile_position=(0, 32 * j))
                    if l < 3:
                        last.then_inc(pv_done, 1)

                def gram(u, k):
                    g, i = k // NT, k % NT
                    par, gn = u % 2, u * GROUPS + g
                    n = N_PIECES + par * GROUPS * NT + k
                    r = rows_of(3, i)
                    bank_free(n)
                    for j in range(i, NT):
                        rj = rows_of(3, j)
                        m = mm(KVB[n % 2][0:r, 0:4 * SQ], GM[par][0:rj, j, 128 * i:128 * i + r],
                               PT[gn % 2][0:rj, j, :], start=(j == i), stop=(j == NT - 1))
                    m.then_inc(kv_ready, 1)

                def norm(u, k):
                    i = k % NT
                    n = (u % 2) * GROUPS * NT + k
                    pe.wait_ge(z_ready, level(z_ready, it, n + 1))
                    r = rows_of(3, i)
                    for j in range(4):
                        m = mm(OT[32 * j:32 * j + VW, 0:SQ], NSEL[0:r, :], ZT[n % 2][0:r, j * SQ:(j + 1) * SQ],
                               start=False, stop=(i == NT - 1), tile_position=(0, 32 * j))
                    m.then_inc((zt_used if i < 2 else pv_done), 1)

                def final_heads(u):
                    l = u // 2
                    pe.wait_ge(ot_used, level(ot_used, it, (u + 1) * GROUPS))
                    pe.wait_ge(exp_done, level(exp_done, it, (u + 1) * GROUPS * NT))
                    for s in range(len(SEGS[l])):
                        for g in range(GROUPS):
                            dst = ST[1][0:SQ, s * 128:s * 128 + 128] if g == 4 else \
                                [ST[0], OT][s][0:SQ, g * 128:g * 128 + 128]
                            last = nc.tensor.transpose(dst, OTS[:, g, s, :], IDN[:, :])
                    last.then_inc(o2_ready, 1)

                def final_transpose(u):
                    l = u // 2
                    pe.wait_ge(o_ready, level(o_ready, it, u + 1))
                    pe.wait_ge(m2_ready, level(m2_ready, it, UNITS if u == UNITS - 2 else u + 1))
                    if l == 3:
                        small_t(u)
                    if n_small[u]:
                        pe.wait_ge(pst_copied, level(pst_copied, it, small_nth(u)))
                        pe.wait_ge(vb_ready, level(vb_ready, it, small_nth(u)))
                    for t, (c0, cn) in enumerate(CH):
                        last = mm(MI[0:cn, t * SQ:(t + 1) * SQ], OS[:, c0:c0 + cn], IDN[0:SQ, 0:SQ],
                                  start=True, stop=(n_small[u] == 0))
                        for k in range(n_small[u]):
                            last = mm(MI[0:cn, t * SQ:(t + 1) * SQ], VB[:, k, c0:c0 + cn], PST[u % 2][:, k, :],
                                      start=False, stop=(k == n_small[u] - 1))
                    last.then_inc(otf_ready, 1)

                def final_project(u):
                    l = u // 2
                    pe.wait_ge(otf_copied, level(otf_copied, it, u + 1))
                    for t, (c0, cn) in enumerate(CH):
                        for k, (_, kn) in enumerate(CH):
                            last = mm(MI[0:cn, t * SQ:(t + 1) * SQ], WO[l][0:kn, k, c0:c0 + cn],
                                      OTF[0:kn, k, :], start=(k == 0), stop=(k == NT - 1))
                    last.then_inc(y_ready, 1)

                for s in range(-1, UNITS + 1):
                    for kind, u, n in plan(s):
                        if kind == "s":
                            scores(u, n)
                        elif kind == "h":
                            kv_piece(u, n, 0)
                        elif kind == "p":
                            kv_piece(u, n, 1)
                        elif kind == "Q":
                            queries(u)
                        elif kind == "b":
                            back_scores(u, n)
                        elif kind == "V":
                            back_values(u, n)
                        elif kind == "g":
                            gram(u, n)
                        elif kind == "n":
                            norm(u, n)
                        elif kind == "M":
                            maxima(u)
                        elif kind == "t":
                            small_t(u)
                        elif kind == "H":
                            final_heads(u)
                        elif kind == "T":
                            final_transpose(u)
                        elif kind == "R":
                            final_project(u)

        @block.scalar
        def _(act):
            def copy(dst, src, scale=1.0):
                return nc.scalar.activation(dst, src, ACT.Copy, scale=scale)

            act.wait_ge(const_in, 16 * CONSTS)
            for g in range(5):
                act.wait_ge(vs_ready, g + 1)
                copy(VSB[:, g, :], ALL_BANKS[g][0:32, 0:C]).then_inc(vs_copied, 1)
            act.wait_ge(ip_summed, 1)
            flat_ipi = IPI[:, :, :].rearrange("p b n -> p (b n)")
            nc.scalar.activation(flat_ipi, flat_ipi, ACT.Sqrt).then_inc(ip_sqrt, 1)

            for sig in ctx_in + xt_in + stored + [k1_ready, k2_ready, v_ready, q1_ready, q2_ready, m1_ready, exp_done,
                                                  se_ready, sq_done, pst_copied, vr_in, otf_copied]:
                act.sem_inc(sig, 1)
            def load_ctx(name, p, batch):
                act.dma_start(CT[p][:, :, :], ins[name][batch].rearrange("(k p) t -> p k t", p=128)).then_inc(ctx_in[p], 16)

            def load_x(p, batch):
                act.dma_start(XT[p][:, 0:2, :], ins["x_t"][batch, 0:256, :]
                              .rearrange("(k p) q -> p k q", p=128)).then_inc(xt_in[p], 16)
                act.dma_start(XT[p][0:64, 2, :], ins["x_t"][batch, 256:C, :]).then_inc(xt_in[p], 16)

            load_ctx("ctx0", 0, 0)
            load_ctx("ctx0", 1, 1)
            load_x(0, 0)
            with act.Fori(0, PAIRS) as it:
                def kv_piece(u, p):
                    l, par = u // 2, u % 2
                    kind, i = PIECES[l][p]
                    n = piece_index(u, p)
                    src = KVB[n % 2]
                    if kind == "K":
                        cn = CH[i][1]
                        m = MAIN[l]
                        act.wait_ge(kv_ready, level(kv_ready, it, n + 1))
                        act.wait_ge(k_packed[i // 2], level(k_packed[i // 2], it, 96 * u))
                        copy(KC[i][0:cn, 0, 0:m], src[0:cn, 0:m]).then_inc(k1_ready, 1)
                    elif kind in ("V", "VT"):
                        act.wait_ge(kv_ready, level(kv_ready, it, n + 1))
                        if kind == "VT":
                            act.wait_ge(pv_done, level(pv_done, it, (u - 3) * GROUPS))
                            copy(VT[par][0:TXT, :, 0:D],
                                            src[0:TXT, 0:C].rearrange("p (h c) -> p h c", h=H)).then_inc(v_ready, 1)
                            return
                        act.wait_ge(pv_done, level(pv_done, it, (u - 2) * GROUPS))
                        r = rows_of(l, i)
                        if l == 3:
                            copy(VA[u % 3][0:r, i, :, R_COL:R_COL + 4],
                                 src[0:r, C:C + 4].rearrange("p (o c) -> p o c", o=1).to_broadcast([r, H, 4]))
                        copy(VA[u % 3][0:r, i, :, 0:D], src[0:r, 0:C].rearrange("p (h c) -> p h c", h=H),
                                        scale=IPM[0:r, 1:2] if i == 0 and len(SEGS[l]) == 2 else 1.0).then_inc(v_ready, 1)

                def k_second(u, i):
                    cn, m = CH[i][1], MAIN[u // 2]
                    act.wait_ge(k_rest, level(k_rest, it, 3 * u + i + 1))
                    copy(KC[i][0:cn, 1, 0:m], KR[i][0:cn, 0:m]).then_inc(k2_ready, 1)

                def queries(u):
                    act.wait_ge(q_ready, level(q_ready, it, u + 1))
                    act.wait_ge(q_packed[0], level(q_packed[0], it, 96 * u))
                    act.wait_ge(q_packed[1], level(q_packed[1], it, 96 * u))
                    copy(QC[:, 0, :], MI[:, 0:NT * SQ]).then_inc(q1_ready, 1)
                    act.wait_ge(q_rest, level(q_rest, it, u + 1))
                    copy(QC[:, 1, :], QR[:, :]).then_inc(q2_ready, 1)

                def exponentials(u, k):
                    gn, c = u * GROUPS + k // NT, k % NT
                    n = u * GROUPS * NT + k
                    act.wait_ge(st_ready, level(st_ready, it, n + 1))
                    if c == 0:
                        act.wait_ge(pv_done, level(pv_done, it, gn - 1))
                    r = rows_of(u // 2, c)
                    nc.scalar.activation(PT[gn % 2][0:r, c, :], ST[n % 2][0:r, 0:4 * SQ],
                                         ACT.Exp, scale=SCALE).then_inc(exp_done, 1)

                def small_exp(u):
                    k = n_small[u]
                    act.wait_ge(sx_ready, level(sx_ready, it, small_nth(u)))
                    nc.scalar.activation(SE[:, 0:k, :, :], SE[:, 0:k, :, :], ACT.Exp,
                                                     scale=SCALE if u // 2 == 0 else 1.0).then_inc(se_ready, 1)

                def small_t(u):
                    k = n_small[u]
                    act.wait_ge(pst_ready, level(pst_ready, it, small_nth(u)))
                    act.wait_ge(otf_ready, level(otf_ready, it, u - 1))
                    copy(PST[u % 2][:, 0:k, :], MI[0:80, 128:128 + 128 * k]
                                       .rearrange("p (k q) -> p k q", k=k)[:, :, 0:SQ]).then_inc(pst_copied, 1)

                def maxima(u):
                    ns = len(SEGS[u // 2])
                    act.wait_ge(m_ready, level(m_ready, it, u + 1))
                    act.wait_ge(m_packed, level(m_packed, it, 64 * u))
                    copy(MP[0:ns * H, 0, :], MI[0:ns * H, 0:SQ]).then_inc(m1_ready, 1)
                    if u // 2 < 2:
                        small_exp(u)

                def load_small_v(u):
                    if not n_small[u]:
                        return
                    act.wait_ge(vb_ready, level(vb_ready, it, small_nth(u) - 1))
                    for k, g in enumerate(SMALL[u // 2]):
                        act.dma_start(
                            VR[:, k, :], dram_vs[g, it * 2 + u % 2].rearrange("(o n) c -> o n c", o=1)
                            .to_broadcast([H, 4, C])).then_inc(vr_in, 16)

                act.wait_ge(stored[1], level(stored[1], it, 0))
                load_x(1, it * 2 + 1)
                for s in range(-1, UNITS + 1):
                    if s in (0, 1):
                        act.wait_ge(kv_ready, level(kv_ready, it, piece_index(s + 1, 0)))
                        load_ctx("ctx1", s, it * 2 + s)
                    if s in (6, 7):
                        act.wait_ge(kv_ready, level(kv_ready, it, piece_index(s + 1, 0)))
                        load_ctx("ctx0", s - 6, it * 2 + 2 + s - 6)
                    for kind, u, n in plan(s):
                        if kind == "p":
                            kv_piece(u, n)
                        elif kind == "k":
                            k_second(u, n)
                        elif kind == "Q":
                            queries(u)
                        elif kind == "v":
                            load_small_v(u)
                            if s == UNITS:
                                act.wait_ge(stored[0], level(stored[0], it, 32))
                                load_x(0, it * 2 + 2)
                        elif kind == "b":
                            exponentials(u, n)
                        elif kind == "M":
                            maxima(u)
                        elif kind == "t":
                            small_t(u)
                        elif kind == "H" and u // 2 == 3:
                            act.wait_ge(sq_ready, level(sq_ready, it, 2 * (u - 6) + 2))
                            nc.scalar.activation(QN[:, 0, :], QN[:, 0, :], ACT.Sqrt).then_inc(sq_done, 1)
                            small_exp(u)
                        elif kind == "T":
                            if u // 2 == 3:
                                small_t(u)
                            act.wait_ge(otf_ready, level(otf_ready, it, u + 1))
                            copy(OTF[:, :, :].rearrange("p t q -> p (t q)"), MI[:, 0:NT * SQ]).then_inc(otf_copied, 1)
                    if s >= UNITS - 1:
                        p = (s - 1) % 2
                        act.wait_ge(x_ready, level(x_ready, it, s))
                        act.dma_start(out_t[it * 2 + p, 0:256, :].rearrange("(k p) q -> p k q", p=128),
                                      XT[p][:, 0:2, :]).then_inc(stored[p], 16)
                        act.dma_start(out_t[it * 2 + p, 256:C, :], XT[p][0:64, 2, :]).then_inc(stored[p], 16)

        @block.vector
        def _(dve):
            v = nc.vector
            steps = [0]

            def setup(instruction):
                steps[0] += 1
                instruction.then_inc(setup_step, 1)
                dve.wait_ge(setup_step, steps[0])

            for bank_ in ALL_BANKS:
                setup(v.memset(bank_[:, :], 0.0))
            for buf in [MX[:, :], QC[:, :, :], QR[:, :], KC[0][:, :, :], KC[1][:, :, :], KC[2][:, :, :], OTF[:, :, :],
                        KSM[:, 0, :, :, :, :], KSM[:, 1, :, :, :, :], KSM[:, 2, :, :, :, :]] \
                    + [VA[k][:, :, :, :] for k in range(3)] + [VT[k][:, :, :] for k in range(2)]:
                setup(v.memset(buf, 0.0))
            for k in range(3):
                setup(v.memset(VA[k][:, :, :, ONE_COL:ONE_COL + 1], 1.0))
            for k in range(2):
                setup(v.memset(VT[k][:, :, ONE_COL:ONE_COL + 1], 1.0))
            setup(v.memset(NSEL[:, :], 0.0))
            setup(v.memset(NSEL[:, N_COL:N_COL + 1], 1.0))
            setup(v.memset(ONES[:, :], 1.0))
            v.memset(SM[:, :, :, :], 0.0).then_inc(zeroed, 1)
            dve.wait_ge(small_in, 16 * (1 + len(WS_NAMES)))
            for k in range(NCK):
                ip = CS[:, k, QUAD[4], :]
                ins_ = v.tensor_tensor(SQI[:, k, :], ip, ip, ALU.mult)
                if k < NCK - 1:
                    setup(ins_)
            ins_.then_inc(ip_sq, 1)
            dve.wait_ge(const_in, 16 * CONSTS)
            for k, (edge, axis, op) in enumerate([(0, 0, ALU.is_le), (1, 1, ALU.is_le), (2, 0, ALU.is_ge), (3, 1, ALU.is_ge)]):
                setup(v.tensor_scalar(IN[:, k, :, :], BB[:, :, :, edge], GXY[:, axis:axis + 1], None, op))
            for k in range(1, 4):
                setup(v.tensor_tensor(IN[:, 0, :, :], IN[:, 0, :, :], IN[:, k, :, :], ALU.mult))
            setup(v.tensor_scalar(MSK[:, :, 1, :], IN[:, 0, :, :], -NEG, NEG, ALU.mult, ALU.add))
            setup(v.tensor_reduce(ANY[:, :], IN[:, 0, :, :], AX.X, ALU.max))
            setup(v.tensor_scalar(MSK[:, :, 0, :], ANY[:, :].rearrange("p (b o) -> p b o", o=1).to_broadcast([SQ, B, 4]),
                                  NEG, None, ALU.mult))
            dve.wait_ge(ks_ready, 1)
            flat = [KSM[:, part, :, :, :, :].rearrange("p g t b n -> p (g t b n)") for part in range(3)]
            src = MI[:, 0:5 * NT * 32]
            setup(v.tensor_copy(flat[0], src))
            setup(v.tensor_tensor(KSR[:, :], src, flat[0], ALU.subtract))
            setup(v.tensor_copy(flat[1], KSR[:, :]))
            v.tensor_tensor(flat[2], KSR[:, :], flat[1], ALU.subtract).then_inc(ks_copy, 1)
            dve.wait_ge(ip_ready, 1)
            flat_ipi = IPI[:, :, :].rearrange("p b n -> p (b n)")
            v.tensor_reduce(flat_ipi, ALL_BANKS[5][0:SQ, 0:NCK * 32].rearrange("p (k n) -> p n k", k=NCK),
                            AX.X, ALU.add).then_inc(ip_summed, 1)
            dve.wait_ge(ip_sqrt, 1)
            setup(v.tensor_scalar(flat_ipi, flat_ipi, EPS, None, ALU.max))
            setup(v.reciprocal(flat_ipi, flat_ipi))
            assert steps[0] == SETUP_STEPS, steps[0]

            for sig in [k_rest, g_ready, z_ready, q_rest, q3_ready, s_used, m2_ready, ot_used, sx_ready, ps_ready,
                        sq_ready, o_ready, x_ready, dve_step]:
                dve.sem_inc(sig, 1)
            with dve.Fori(0, PAIRS) as it:
                steps[0] = 0

                def step(instruction):
                    steps[0] += 1
                    instruction.then_inc(dve_step, 1)
                    dve.wait_ge(dve_step, level(dve_step, it, steps[0]))

                def kv_piece(u, p):
                    l, par = u // 2, u % 2
                    kind, i = PIECES[l][p]
                    n = piece_index(u, p)
                    if kind == "K":
                        cn, m = CH[i][1], MAIN[l]
                        dve.wait_ge(k1_ready, level(k1_ready, it, 3 * u + i + 1))
                        dve.wait_ge(k3_ready, level(k3_ready, it, 3 * (u - 1) + i + 1 if u else 0))
                        v.tensor_tensor(KR[i][0:cn, 0:m], KVB[n % 2][0:cn, 0:m], KC[i][0:cn, 0, 0:m],
                                                  ALU.subtract).then_inc(k_rest, 1)
                    elif kind == "G":
                        dve.wait_ge(kv_ready, level(kv_ready, it, n + 1))
                        r, wd = rows_of(3, i), min(128 * i + 128, MAIN[3])
                        dve.wait_ge(pv_done, level(pv_done, it, 0))
                        if i:
                            step(v.tensor_scalar_mul(GM[par][0:r, i, 0:128 * i], KVB[n % 2][0:r, 0:128 * i], 2.0))
                        v.tensor_copy(GM[par][0:r, i, 128 * i:wd], KVB[n % 2][0:r, 128 * i:wd]).then_inc(g_ready, 1)

                def queries(u):
                    dve.wait_ge(q1_ready, level(q1_ready, it, u + 1))
                    v.tensor_tensor(QR[:, :], MI[:, 0:NT * SQ], QC[:, 0, :], ALU.subtract).then_inc(q_rest, 1)
                    dve.wait_ge(st_ready, level(st_ready, it, (u - 1) * GROUPS * NT))
                    dve.wait_ge(q2_ready, level(q2_ready, it, u + 1))
                    v.tensor_tensor(QC[:, 2, :], QR[:, :], QC[:, 1, :], ALU.subtract).then_inc(q3_ready, 1)

                def max_of(u, h):
                    l = u // 2
                    if h == 0:
                        dve.wait_ge(m_ready, level(m_ready, it, u))
                    n = u * H + h
                    dve.wait_ge(s_ready, level(s_ready, it, n + 1))
                    src = SB_[n % 2]
                    if n_small[u]:
                        m = n_small[u]
                        dst = SM3[u % 2][:, :, h, :] if l == 3 else SM[:, :, h, :]
                        v.tensor_copy(dst, src[0:SQ, MAIN[l]:MAIN[l] + 4 * m].rearrange("p (g n) -> p g n", g=m))
                    for s, (t0, t1) in enumerate(SEGS[l]):
                        last = v.tensor_reduce(MX[:, s * H + h:s * H + h + 1], src[0:SQ, t0:t1], AX.X, ALU.max,
                                               negate=True)
                    last.then_inc(s_used, 1)

                def small_softmax(u, scores_, last_scale=None):
                    l, k = u // 2, n_small[u]
                    if l == 1:
                        def view(buf):
                            return buf[:, 0:k, :, :].rearrange("p g h n -> p h g n")
                        m = H
                        axis = AX.XY

                        def wide(vec):
                            return vec[:, 0:H].rearrange("p (o h i) -> p o h i", o=1, i=1).to_broadcast([SQ, k, H, 4])
                        full = lambda buf: buf[:, 0:k, :, :]
                    else:
                        m = k * H
                        axis = AX.X

                        def view(buf):
                            return buf[:, 0:k, :, :].rearrange("p g h n -> p (g h) n")

                        def wide(vec):
                            return vec[:, 0:m].rearrange("p (h i) -> p h i", i=1).to_broadcast([SQ, m, 4])
                        full = view
                    step(v.tensor_reduce(SX[:, 0:m], view(scores_), axis, ALU.max))
                    v.tensor_tensor(full(SE), full(scores_), wide(SX), ALU.subtract).then_inc(sx_ready, 1)
                    dve.wait_ge(se_ready, level(se_ready, it, small_nth(u)))
                    step(v.tensor_reduce(SS[:, 0:m], view(SE), axis, ALU.add))
                    step(v.reciprocal(SR[:, 0:m], SS[:, 0:m]))
                    if l == 3:
                        v.scalar_tensor_tensor(full(SP_), full(SE), SPM[:, 0:1], wide(SR), ALU.mult, ALU.mult).then_inc(ps_ready, 1)
                    else:
                        v.tensor_tensor(full(SP_), full(SE), wide(SR), ALU.mult).then_inc(ps_ready, 1)

                def maxima(u):
                    l = u // 2
                    ns = len(SEGS[l])
                    dve.wait_ge(m1_ready, level(m1_ready, it, u + 1))
                    v.tensor_tensor(MP[0:ns * H, 1, :], MI[0:ns * H, 0:SQ], MP[0:ns * H, 0, :],
                                                ALU.subtract).then_inc(m2_ready, 1)
                    if l < 2:
                        dve.wait_ge(s_used, level(s_used, it, (u + 1) * H))
                        dve.wait_ge(pst_ready, level(pst_ready, it, small_nth(u) - 1))
                        if l == 1:
                            for g in range(2):
                                step(v.scalar_tensor_tensor(
                                    SM[:, g, :, :], SM[:, g, :, :], SCALE,
                                    MSK[:, it * 2 + u % 2, g, :].rearrange("p (o n) -> p o n", o=1)
                                    .to_broadcast([SQ, H, 4]), ALU.mult, ALU.add))
                        small_softmax(u, SM)

                def times_probs(u, k):
                    g, i = k // NT, k % NT
                    par, gn = u % 2, u * GROUPS + g
                    n = par * GROUPS * NT + k
                    r = rows_of(3, i)
                    dve.wait_ge(kv_ready, level(kv_ready, it, N_PIECES + n + 1))
                    if i == 1:
                        dve.wait_ge(pv_done, level(pv_done, it, gn))
                    else:
                        dve.wait_ge(zt_used, level(zt_used, it, 2 * (par * GROUPS + g) + i // 2))
                    v.tensor_tensor(ZT[n % 2][0:r, :], KVB[(N_PIECES + n) % 2][0:r, 0:4 * SQ],
                                    PT[gn % 2][0:r, i, :], ALU.mult).then_inc(z_ready, 1)

                def copy_out(u, g):
                    ns = len(SEGS[u // 2])
                    dve.wait_ge(pv_done, level(pv_done, it, u * GROUPS + g + 1))
                    if g == 0:
                        dve.wait_ge(o2_ready, level(o2_ready, it, u))
                    v.tensor_copy(OTS[:, g, 0:ns, :],
                                  OT[:, 0:ns * SQ].rearrange("p (s q) -> p s q", s=ns)).then_inc(ot_used, 1)

                def parts(s, lo, hi):
                    return [([ST[0], OT][s][0:SQ, 0:512].rearrange("p (h c) -> p h c", c=32)[:, :, lo:hi], 0, 16),
                            (ST[1][0:SQ, s * 128:s * 128 + 128].rearrange("p (h c) -> p h c", c=32)[:, :, lo:hi], 16, H)]

                def final(u):
                    l, par = u // 2, u % 2
                    ns = len(SEGS[l])
                    dve.wait_ge(o2_ready, level(o2_ready, it, u + 1))
                    dve.wait_ge(otf_ready, level(otf_ready, it, u))
                    for s in range(ns):
                        for src_, h0, h1 in parts(s, ONE_COL, ONE_COL + 1):
                            step(v.reciprocal(ZR[:, s, h0:h1].rearrange("p (h o) -> p h o", o=1), src_))
                    for s in range(ns):
                        dst = [OS, O2][s]
                        for src_, h0, h1 in parts(s, 0, D):
                            ins_ = v.tensor_tensor(dst[:, h0 * D:h1 * D].rearrange("p (h c) -> p h c", c=D), src_,
                                                   ZR[:, s, h0:h1].rearrange("p (h o) -> p h o", o=1)
                                                   .to_broadcast([SQ, h1 - h0, D]), ALU.mult)
                            if h0 == 0 or s < ns - 1 or ns == 2 or l == 3:
                                step(ins_)
                    if l == 3:
                        for src_, h0, h1 in parts(0, N_COL, N_COL + 1):
                            v.tensor_scalar(QN[:, 0, h0:h1].rearrange("p (h o) -> p h o", o=1), src_, 0.0,
                                                        None, ALU.max).then_inc(sq_ready, 1)
                        dve.wait_ge(sq_done, level(sq_done, it, par + 1))
                        for src_, h0, h1 in parts(0, ONE_COL, ONE_COL + 1):
                            step(v.scalar_tensor_tensor(QN[:, 1, h0:h1].rearrange("p (h o) -> p h o", o=1), src_, EPS,
                                                        QN[:, 0, h0:h1].rearrange("p (h o) -> p h o", o=1),
                                                        ALU.mult, ALU.max))
                        step(v.reciprocal(QN[:, 2, :], QN[:, 1, :]))
                        for src_, h0, h1 in parts(0, R_COL, R_COL + 4):
                            ins_ = v.tensor_tensor(QS[:, h0:h1, :], src_, QN[:, 2, h0:h1].rearrange("p (h o) -> p h o", o=1)
                                                   .to_broadcast([SQ, h1 - h0, 4]), ALU.mult)
                            if h0 == 0:
                                step(ins_)
                        ins_.then_inc(o_ready, 1)
                        dve.wait_ge(o_ready, level(o_ready, it, u + 1))
                        step(v.scalar_tensor_tensor(QS[:, :, :], QS[:, :, :], SEM_SCALE,
                                                    IPI[:, it * 2 + u % 2, :].rearrange("p (o n) -> p o n", o=1)
                                                    .to_broadcast([SQ, H, 4]), ALU.mult, ALU.mult))
                        step(v.scalar_tensor_tensor(QS[:, :, :], SM3[u % 2][:, 0, :, :], SCALE, QS[:, :, :],
                                                    ALU.mult, ALU.add))
                        dve.wait_ge(pst_ready, level(pst_ready, it, small_nth(u) - 1))
                        small_softmax(u, QS[:, :, :].rearrange("p (g h) n -> p g h n", g=1))
                    elif ns == 2:
                        v.tensor_tensor(OS[:, :], OS[:, :], O2[:, :], ALU.add).then_inc(o_ready, 1)
                    else:
                        ins_.then_inc(o_ready, 1)

                def result(u):
                    l, par = u // 2, u % 2
                    dve.wait_ge(y_ready, level(y_ready, it, u + 1))
                    for t, (c0, cn) in enumerate(CH):
                        x = XT[par][0:cn, t, :]
                        last = v.scalar_tensor_tensor(x, MI[0:cn, t * SQ:(t + 1) * SQ], BIAS[0:cn, l, t:t + 1], x,
                                                      ALU.add, ALU.add)
                    last.then_inc(x_ready, 1)

                for s in range(-1, UNITS + 1):
                    for kind, u, n in plan(s):
                        if kind == "s":
                            max_of(u, n)
                        elif kind == "p":
                            kv_piece(u, n)
                        elif kind == "Q":
                            queries(u)
                        elif kind == "z":
                            times_probs(u, n)
                        elif kind == "o":
                            copy_out(u, n)
                        elif kind == "M":
                            maxima(u)
                        elif kind == "H":
                            final(u)
                        elif kind == "R":
                            result(u)

                assert steps[0] == DVE_STEPS, steps[0]

        @block.gpsimd
        def _(pool):
            g_ = nc.gpsimd
            pool.wait_ge(vs_copied, 5)
            pool.wait_ge(ks_copy, 1)
            for k in range(3):
                g_.memset(KP[k][PROWS:PROWS + 4, :, TXT:T], 0.0)
                g_.memset(KP[k][PROWS:PROWS + 4, :, 0:TXT], 1.0)
            g_.memset(TI[:, 0:TXT], 0.0)
            g_.memset(TI[:, TXT:T], 1.0).then_inc(pool_set, 1)
            pool.wait_ge(const_in, 16 * CONSTS)

            for sig in [k3_ready, ones_ready, vb_ready]:
                pool.sem_inc(sig, 1)
            with pool.Fori(0, PAIRS) as it:
                def kv_piece(u, p):
                    l, par = u // 2, u % 2
                    kind, i = PIECES[l][p]
                    if kind == "K":
                        cn, m = CH[i][1], MAIN[l]
                        pool.wait_ge(pv_done, level(pv_done, it, (u - 2) * GROUPS))
                        pool.wait_ge(k2_ready, level(k2_ready, it, 3 * u + i + 1))
                        last = g_.tensor_tensor(KC[i][0:cn, 2, 0:m], KR[i][0:cn, 0:m], KC[i][0:cn, 1, 0:m],
                                                ALU.subtract)
                        for k, grp in enumerate(SMALL[l]):
                            last = g_.tensor_copy(KC[i][:, :, m + 4 * k:m + 4 * k + 4],
                                                  KSM[:, :, grp, i, it * 2 + par, :])
                        last.then_inc(k3_ready, 1)
                    elif kind == "V" and i == 0:
                        pool.wait_ge(pv_done, level(pv_done, it, (u - 2) * GROUPS))
                        col = 1 if len(SEGS[l]) == 2 else 0
                        marks = IPM[:, col:col + 1].rearrange("p (o i) -> p o i", o=1).to_broadcast([128, H, 1])
                        g_.tensor_tensor(VA[u % 3][:, 0, :, ONE_COL:ONE_COL + 1], marks, marks, ALU.mult).then_inc(ones_ready, 1)

                def mask_small_v(u):
                    if n_small[u]:
                        pool.wait_ge(vr_in, level(vr_in, it, 16 * sum(n_small[:u + 1])))
                        pool.wait_ge(otf_ready, level(otf_ready, it, u))
                        for k in range(n_small[u]):
                            last = g_.tensor_tensor(VB[:, k, :], VR[:, k, :], HM[:, :], ALU.mult)
                        last.then_inc(vb_ready, 1)

                for s in range(-1, UNITS + 1):
                    for kind, u, n in plan(s):
                        if kind == "p":
                            kv_piece(u, n)
                        elif kind == "v":
                            mask_small_v(u)


CONSTS = 6 + 4 * NT
SETUP_STEPS = 49
DVE_STEPS = 84


def kernel(**inputs):
    import numpy as np
    import concourse.bacc as bacc
    from concourse.bass_utils import run_bass_kernel_spmd

    def arr(name):
        return np.asarray(inputs[name])

    ctx = arr("ctx_2048").transpose(0, 2, 1)
    order0 = list(range(TXT)) + list(range(TXT + 8, T)) + list(range(TXT, TXT + 8))
    small = list(range(TXT, TXT + 8)) + list(range(T - 8, T))
    ahead = list(range(B)) + [0, 1]
    data = {
        "x_t": arr("x").transpose(0, 2, 1)[ahead],
        "ctx0": ctx[:, :, order0][ahead],
        "ctx1": ctx,
        "ctx_small": ctx[:, :, small].reshape(B, CC, 4, 4).transpose(1, 2, 0, 3).reshape(CC, 4, 4 * B),
        "boxes": arr("fside_Bx4x4_0"),
        "spatial": arr("fside_S_0").reshape(SQ, 1),
    }
    names = {
        "L0_q": "L0_xattn_to_q_w", "L0_k": "L0_xattn_to_k_w", "L0_v": "L0_xattn_to_v_w",
        "L0_kip": "L0_xattn_to_k_ip_w", "L0_vip": "L0_xattn_to_v_ip_w", "L0_o": "L0_xattn_to_out_w",
        "S0_k": "L0_xattn_to_k_object_w", "S0_v": "L0_xattn_to_v_object_w",
        "S1_k": "L0_xattn_to_k_others_w", "S1_v": "L0_xattn_to_v_others_w",
        "L1_q": "L1_xattn_w_q", "L1_k": "L1_xattn_w_k", "L1_v": "L1_xattn_w_v", "L1_o": "L1_xattn_w_out",
        "S2_k": "L1_xattn_w_k_ip", "S2_v": "L1_xattn_w_v_ip",
        "L3_q": "L3_xattn_W_q", "L3_k": "L3_xattn_W_k", "L3_v": "L3_xattn_W_v", "L3_o": "L3_xattn_W_out",
        "S4_k": "L3_xattn_W_k_ip", "S4_v": "L3_xattn_W_v_ip",
    }
    for short, name in names.items():
        data[short] = arr(name)
    heads = [range(0, 16, 2), range(1, 16, 2), range(16, H)]
    by_channel = [D * h + c for tile in heads for c in range(D) for h in tile]
    for short, name in {"L2_q": "Wq", "L2_k": "Wk", "L2_v": "Wv", "L2_kip": "Wk_ip", "L2_vip": "Wv_ip", "L2_o": "Wo"}.items():
        data[short] = arr("L2_xattn_" + name).T
    for short in data:
        if short.endswith(("_q", "_k", "_kip")):
            data[short] = data[short][:, by_channel]
    for l, name in enumerate(["L0_xattn_to_out_b", "L1_xattn_b_out", "L2_xattn_bo", "L3_xattn_b_out"]):
        data[f"L{l}_b"] = arr(name).reshape(C, 1)
    f = np.float32
    gh, gw = 8, 14
    data["ident"] = np.eye(128, dtype=f)
    data["head_mask"] = (np.arange(80)[:, None] // 4 == np.arange(C)[None, :] // D).astype(f)
    q = np.arange(SQ)
    data["grid"] = np.stack([(q % gw).astype(f) / f(gw - 1), (q // gw).astype(f) / f(gh - 1)], 1).astype(f)
    data["image_rows"] = np.stack([np.ones(128, f), (np.arange(128) >= TXT).astype(f)], 1)

    nc = bacc.Bacc("TRN2", target_bir_lowering=False, num_devices=1, dynamic_dma_scratch_size=512)
    arrays, ins = {}, {}
    for name, a in data.items():
        a = np.ascontiguousarray(a)
        arrays["in_" + name] = a
        ins[name] = nc.dram_tensor("in_" + name, a.shape, mybir.dt.from_np(a.dtype), kind="ExternalInput").ap()
    out_t = nc.dram_tensor("out_t", (B, C, SQ), F32, kind="ExternalOutput").ap()
    build(nc, ins, out_t)
    r = run_bass_kernel_spmd(nc, [arrays], core_ids=[0])
    return np.ascontiguousarray(r.results[0]["out_t"].transpose(0, 2, 1))
```

```python
from contextlib import ExitStack

import concourse.bass as bass
from concourse import mybir

F32 = mybir.dt.float32
BF16 = mybir.dt.bfloat16
ACT = mybir.ActivationFunctionType
ALU = mybir.AluOpType
AX = mybir.AxisListType

B, SQ, C, T, CC = 8, 112, 320, 375, 512
H, D = 20, 16
SCALE = D ** -0.5
NEG = -10000.0
EPS = 1e-12
SEM_SCALE = 0.5
TXT = 77
MAIN = [367, 367, 375, 371]
SEGS = [[(0, TXT), (TXT, 367)], [(0, 367)], [(0, TXT), (TXT, 375)], [(0, 371)]]
SMALL = [[0, 1], [2, 3], [], [4]]
QUAD = [0, 1, 2, 3, 3]
NCK = CC // 128
CH = [(0, 128), (128, 128), (256, 64)]
NT = 3
PAIRS = B // 2
UNITS = 8
GROUPS = 5
VW = 22
ONE_COL, R_COL, N_COL = 16, 17, 21
KPARTS = [0, 0, 0, 1, 1, 2]
QPARTS = [0, 1, 2, 0, 1, 0]
PROWS = 16 * len(KPARTS)
XROWS = PROWS + 4

PIECES = [
    [("K", 0), ("K", 1), ("K", 2), ("VT", 0), ("V", 0), ("V", 1), ("V", 2)],
    [("K", 0), ("K", 1), ("K", 2), ("V", 0), ("V", 1), ("V", 2)],
    [("K", 0), ("K", 1), ("K", 2), ("VT", 0), ("V", 0), ("V", 1), ("V", 2)],
    [("K", 0), ("K", 1), ("K", 2), ("V", 0), ("V", 1), ("V", 2), ("G", 0), ("G", 1), ("G", 2)],
]
SLOT_FIRST = "spspspsppQppsspspsppspspss"
SLOT = "ssbbspbsvtbbspbVsosbbspbVsopsbbsbVsosbbsbVsopVsosHppTsRspQ"
GRAMS = 3 * "Vggzbsngzsnzssnbbo" + "VggzbsngzpsnpzssnoVggzppngzpsnpzssno"
SLOT_GRAM = "ssbbsbbb" + GRAMS.replace("o", "ov", 1) + "MHppppTpRpQ"
SLOT_LAST = "bbbbb" + GRAMS.replace("o", "ov", 1) + "ssMHppppTpRpQ"


def layer(u):
    return u % UNITS // 2


def buf(u):
    return u % UNITS % 3


def plan(s, last):
    text = {-1: "Q", 0: SLOT_FIRST, UNITS - 1: SLOT_GRAM, UNITS: SLOT_LAST}.get(s, SLOT)
    front = s >= 0 and not (last and s >= UNITS)
    ahead = not (last and s + 1 >= UNITS)
    total = {"s": H * front, "p": 2 * len(PIECES[layer(s + 1)]) * ahead, "Q": int(ahead), "M": int(front),
             "m": int(front and layer(s) < 2), "q": int(ahead), "t": int(s >= 1 and layer(s - 1) < 2)}
    for kind, number in [("s", total["s"]), ("p", text.count("p") + 2 * int(0 <= s < UNITS - 1)), ("M", total["M"]),
                         ("m", total["m"]), ("q", total["q"]), ("p", total["p"])]:
        text += max(number - text.count(kind), 0) * kind
    unit = {"s": s, "M": s, "m": s, "p": s + 1, "Q": s + 1, "q": s + 1}
    steps, counts, k_parts = [], {}, []
    for kind in text:
        n = counts.get(kind, 0)
        if n < total.get(kind, len(text)):
            counts[kind] = n + 1
            if kind == "p":
                kind, n = "hp"[n % 2], n // 2
                steps.append((kind, s + 1, n))
            else:
                steps.append((kind, unit.get(kind, s - 1), n))
            if kind == "p" and PIECES[layer(s + 1)][n][0] == "K":
                k_parts.append([2, n])
            elif k_parts:
                k_parts[0][0] -= 1
                if k_parts[0][0] <= 0:
                    steps.append(("k", s + 1, k_parts.pop(0)[1]))
    return steps + [("k", s + 1, n) for _, n in k_parts]


def uses_of(slots):
    uses = []
    for s in slots:
        for kind, u, n in plan(s, False):
            if kind == "h":
                uses.append((u,) + PIECES[layer(u)][n])
            elif kind == "g":
                uses.append((u, "Y", n))
    return uses


AHEAD_USES = uses_of([-1, 0])
PASS_USES = uses_of(range(1, UNITS + 1))
BANK = {use: n % 2 for n, use in enumerate(PASS_USES)}
BANK.update({use: BANK[(use[0] + UNITS,) + use[1:]] for use in AHEAD_USES})


def uses_before(last):
    before, held = {}, {}
    for use in AHEAD_USES + [use for use in PASS_USES if not (last and use[0] >= UNITS)]:
        before[use] = held.get(BANK[use])
        held[BANK[use]] = use
    return before


BEFORE = [uses_before(False), uses_before(True)]
V_USES = [sum(1 for kind, _ in PIECES[layer(u)] if kind in ("V", "VT")) for u in range(UNITS)]


def rows_of(l, c):
    return min(128, MAIN[l] - 128 * c)


def over_units(numbers, u):
    return u // UNITS * sum(numbers) + sum(numbers[:u % UNITS])


def piece_index(u, p):
    return over_units([len(PIECES[layer(v)]) for v in range(UNITS)], u) + p


def v_index(u, kind, n):
    order = [use for use in PIECES[layer(u)] if use[0] in ("V", "VT")]
    return over_units(V_USES, u) + order.index((kind, n)) + 1


def build(nc, ins, out_t):
    dram_vs = nc.dram_tensor("small_v", (5, B, 4, C), F32, kind="Internal").ap()
    with ExitStack() as ctx:
        def sb(name, shape, dt=F32):
            return ctx.enter_context(nc.sbuf_tensor(name, shape, dt))

        def sem(name):
            return ctx.enter_context(nc.semaphore(name))

        per_pass = {}

        def signal(name, total):
            s = sem(name)
            per_pass[s.name] = total
            return s

        def level(s, it, n):
            return it * per_pass[s.name] + (1 + max(n, 0))

        def sources(u):
            return XI[u % 2] if layer(u) == 0 else XT[u % 2]

        KV_W = [["L0_k", "L0_v", "L0_kip", "L0_vip"], ["L1_k", "L1_v"],
                ["L2_k", "L2_v", "L2_kip", "L2_vip"], ["L3_k", "L3_v"]]
        W = {n: sb("w_" + n, [128, NCK, C]) for l in (0, 1, 3) for n in KV_W[l]}
        for n0, n2 in zip(KV_W[0], KV_W[2]):
            W[n2] = W[n0]
        WQ = [sb(f"wq{l}", [128, NT, C]) for l in range(4)]
        WO = [sb(f"wo{l}", [128, NT, C]) for l in range(4)]
        BIAS = sb("bias", [128, 4, NT])
        CT = [sb(f"ctx{p}", [128, NCK, T]) for p in range(2)]
        XI = [sb(f"x_first{p}", [128, NT, SQ]) for p in range(2)]
        XT = [sb(f"xt{p}", [128, NT, SQ]) for p in range(2)]
        KP_ALL = sb("k_packed", [128, 3 * H * T], BF16)
        KP = [KP_ALL[:, k * H * T:(k + 1) * H * T].rearrange("p (h t) -> p h t", h=H) for k in range(3)]
        WS_NAMES = ["S0_k", "S0_v", "S1_k", "S1_v", "S2_k", "S2_v", "S4_k", "S4_v"]
        KP32 = KP_ALL[:, :].bitcast(F32)
        WS = {n: KP32[:, i * NCK * C:(i + 1) * NCK * C].rearrange("p (k c) -> p k c", k=NCK)
              for i, n in enumerate(WS_NAMES)}
        WS["S3_k"], WS["S3_v"] = WS["S2_k"], WS["S2_v"]
        QP = [sb(f"q_packed{p}", [128, H, SQ], BF16) for p in range(2)]
        VA = [sb(f"v{k}", [128, NT, H, VW]) for k in range(3)]
        VT = [sb(f"v_text{p}", [128, H, VW]) for p in range(2)]
        KC01 = sb("k_parts01", [128, 3, 2, T], BF16)
        KC = [KC01[:, :, 0, :], KC01[:, :, 1, :], sb("k_parts2", [128, 3, T], BF16)]
        KR = [sb(f"k_rest{t}", [128, T]) for t in range(NT)]
        QC = sb("q_parts", [128, 3, NT * SQ], BF16)
        QR = sb("q_rest", [128, NT * SQ])
        PT = [sb(f"probs{k}", [128, NT, 4 * SQ]) for k in range(2)]
        ZT = [sb(f"gp{k}", [128, 4 * SQ]) for k in range(2)]
        GM_ALL = sb("gram", [128, 2, NT, 384])
        GM = [GM_ALL[:, p, :, :] for p in range(2)]
        SETUP = GM_ALL[:, :, :, :].rearrange("p a b c -> p (a b c)")
        OTS = sb("o_heads", [128, GROUPS, 2, SQ])
        MX = sb("neg_max", [SQ, 4 * H])
        MP = sb("max_parts", [2 * H, 2, SQ], BF16)
        SM = sb("small_scores", [SQ, 2, H, 4])
        SM3 = [sb(f"small_scores3{p}", [SQ, 1, H, 4]) for p in range(2)]
        SE = sb("small_exp", [SQ, 2, H, 4])
        SP_ = sb("small_probs", [SQ, 2, H, 4])
        SX = sb("small_max", [SQ, 2 * H])
        SS = sb("small_sum", [SQ, 2 * H])
        SR = sb("small_rec", [SQ, 2 * H])
        QN = sb("sem_norm", [SQ, 3, H])
        QS = sb("sem", [SQ, H, 4])
        PST = [sb(f"small_probs_t{p}", [80, 2, SQ]) for p in range(2)]
        VR = sb("small_v_rep", [80, 2, C])
        VB = sb("small_v_blk", [80, 2, C])
        ZR = sb("z_rec", [SQ, 2, H])
        OS = sb("o_sum", [SQ, C])
        O2 = sb("o_second", [SQ, C])
        OTF = sb("o_t", [128, NT, SQ])
        KSM = sb("small_k_parts", [128, 3, 5, NT, B, 4], BF16)
        KSR = SETUP[:, 1600:1600 + 5 * NT * B * 4]
        CS = PT[0][:, :, :].rearrange("p c q -> p (c q)")[:, 0:NCK * 4 * B * 4] \
            .rearrange("p (k g n) -> p k g n", k=NCK, g=4)
        SQI = SETUP[:, 2080:2080 + NCK * B * 4].rearrange("p (k n) -> p k n", k=NCK)
        IPI = sb("ip_inv_norm", [SQ, B, 4])
        VSB = SETUP[:, 0:2 * C].rearrange("p (k c) -> p k c", k=2)
        SEG32 = SETUP[0:4, 2 * C:2 * C + T]
        BB = sb("boxes", [SQ, B, 4, 4])
        IN = sb("inside", [SQ, 4, B, 4])
        MSK = sb("ip_mask", [SQ, B, 2, 4])
        ANY = sb("any_inside", [SQ, B])
        IDN = sb("ident", [128, 128])
        HM = sb("head_mask", [80, C])
        GXY = sb("grid", [SQ, 2])
        IPM = sb("image_rows", [128, 2])
        SPM = sb("spatial", [SQ, 1])
        ONES = sb("ones", [128, 128])
        NSEL = sb("norm_select", [128, VW])
        SEG = sb("segments", [4, T], BF16)

        def bank(name):
            return ctx.enter_context(nc.psum_tensor(name, [128, 512], F32))

        SB_ = [bank("scores0"), bank("scores1")]
        ST = [bank("scores_t0"), bank("scores_t1")]
        KVB = [bank("kv0"), bank("kv1")]
        OT = bank("o_acc")
        MI = bank("misc")
        ALL_BANKS = SB_ + ST + KVB + [OT, MI]

        w_in = [sem(f"w_in{l}") for l in range(4)]
        small_in = sem("small_in")
        const_in = sem("const_in")
        rows_in = sem("rows_in")
        zeroed = sem("zeroed")
        seg_ready = sem("seg_ready")
        ks_ready = sem("ks_ready")
        ks_copy = sem("ks_copy")
        vs_ready = sem("vs_ready")
        vs_copied = sem("vs_copied")
        vs_stored = sem("vs_stored")
        ip_sq = sem("ip_sq")
        ip_summed = sem("ip_summed")
        ip_sqrt = sem("ip_sqrt")
        ip_ready = sem("ip_ready")
        setup_step = sem("setup_step")

        def small_groups(u):
            return len(SMALL[layer(u)])

        groups_of_units = [small_groups(u) for u in range(UNITS)]
        ctx_in = [signal(f"ctx_in{p}", 32) for p in range(2)]
        xt_in = [signal(f"xt_in{p}", 32) for p in range(2)]
        kv_ready = signal("kv_ready", piece_index(UNITS, 0))
        gp_ready = signal("gp_ready", 2 * GROUPS * NT)
        k1_ready = signal("k1_ready", 3 * UNITS)
        k_rest = signal("k_rest", 3 * UNITS)
        k2_ready = signal("k2_ready", 3 * UNITS)
        k3_ready = signal("k3_ready", 3 * UNITS)
        v_ready = signal("v_ready", sum(V_USES))
        ones_ready = signal("ones_ready", UNITS)
        g_ready = signal("g_ready", 6)
        z_ready = signal("z_ready", 2 * GROUPS * NT)
        k_packed = [signal(f"k_packed{t}", 96 * UNITS) for t in ("01", "2")]
        q_packed = [signal(f"q_packed{t}", 96 * UNITS) for t in ("01", "2")]
        m_packed = signal("m_packed", 64 * UNITS)
        zt_used = signal("zt_used", 2 * GROUPS * 2)
        q_ready = signal("q_ready", UNITS)
        q1_ready = signal("q1_ready", UNITS)
        q_rest = signal("q_rest", UNITS)
        q2_ready = signal("q2_ready", UNITS)
        q3_ready = signal("q3_ready", UNITS)
        s_ready = signal("s_ready", H * UNITS)
        s_used = signal("s_used", H * UNITS)
        m_ready = signal("m_ready", UNITS)
        m1_ready = signal("m1_ready", UNITS)
        m2_ready = signal("m2_ready", UNITS)
        st_ready = signal("st_ready", UNITS * GROUPS * NT)
        exp_done = signal("exp_done", UNITS * GROUPS * NT)
        pv_done = signal("pv_done", UNITS * GROUPS)
        ot_used = signal("ot_used", UNITS * GROUPS)
        sq_ready = signal("sq_ready", 4)
        sq_done = signal("sq_done", 2)
        sx_ready = signal("sx_ready", 6)
        se_ready = signal("se_ready", 6)
        ps_ready = signal("ps_ready", 6)
        pst_ready = signal("pst_ready", 6)
        pst_copied = signal("pst_copied", 6)
        w0_in = signal("w0_in", 2 * 64)
        vr_in = signal("vr_in", 16 * sum(groups_of_units))
        vb_ready = signal("vb_ready", 6)
        o2_ready = signal("o2_ready", UNITS)
        o_ready = signal("o_ready", UNITS)
        otf_ready = signal("otf_ready", UNITS)
        otf_copied = signal("otf_copied", UNITS)
        y_ready = signal("y_ready", UNITS)
        x_ready = signal("x_ready", UNITS)
        stored = [signal(f"stored{p}", 32) for p in range(2)]
        dve_step = signal("dve_step", DVE_STEPS)

        def small_nth(u):
            return over_units([min(g, 1) for g in groups_of_units], u + 1)

        block = ctx.enter_context(nc.Block())

        @block.sync
        def _(sp):
            def load_w(name, dst, s):
                sp.dma_start(dst[:, :, :], ins[name].rearrange("(k p) c -> p k c", p=128)).then_inc(s, 16)

            def load_wo(name, dst, s):
                sp.dma_start(dst[:, 0:2, :], ins[name][0:256, :].rearrange("(k p) c -> p k c", p=128)).then_inc(s, 16)
                sp.dma_start(dst[0:64, 2, :], ins[name][256:C, :]).then_inc(s, 16)

            sp.dma_start(CS[:, :, :, :],
                         ins["ctx_small"].rearrange("(k p) g n -> p k g n", p=128)).then_inc(small_in, 16)
            for n in WS_NAMES:
                load_w(n, WS[n], small_in)
            sp.dma_start(IDN[:, :], ins["ident"]).then_inc(const_in, 16)
            sp.dma_start(HM[:, :], ins["head_mask"]).then_inc(const_in, 16)
            sp.dma_start(GXY[:, :], ins["grid"]).then_inc(const_in, 16)
            sp.dma_start(IPM[:, :], ins["image_rows"]).then_inc(const_in, 16)
            sp.dma_start(SPM[:, :], ins["spatial"]).then_inc(const_in, 16)
            sp.dma_start(BB[:, :, :, :], ins["boxes"].rearrange("(o b) m c -> o b m c", o=1)
                         .to_broadcast([SQ, B, 4, 4])).then_inc(const_in, 16)
            sp.dma_start(BIAS[:, :, :], ins["biases"]).then_inc(const_in, 16)
            sp.dma_start(SEG32, ins["segments"]).then_inc(const_in, 16)

            def load_kv_weights(l):
                for n in KV_W[l]:
                    load_w(n, W[n], w0_in)

            for l in range(4):
                for n in KV_W[l] if l in (1, 3) else []:
                    load_w(n, W[n], w_in[l])
                load_wo(f"L{l}_q", WQ[l], w_in[l])
                load_wo(f"L{l}_o", WO[l], w_in[l])
                if l == 0:
                    sp.sem_inc(w0_in, 1)
                    load_kv_weights(0)
            sp.wait_ge(vs_copied, 2)
            flat_vs = dram_vs.rearrange("g b n c -> (g b n) c")
            sp.dma_start(flat_vs[0:128, :], VSB[:, 0, :]).then_inc(vs_stored, 16)
            sp.dma_start(flat_vs[128:160, :], VSB[0:32, 1, :]).then_inc(vs_stored, 16)
            sp.wait_ge(ks_ready, 1)
            sp.wait_ge(seg_ready, 1)
            for k in range(3):
                sp.dma_start(KP[k][PROWS:PROWS + 4, :, :],
                             SEG[:, :].rearrange("p (o t) -> p o t", o=1).to_broadcast([4, H, T])).then_inc(rows_in, 16)
            sp.wait_ge(vs_stored, 32)

            for sig in k_packed + q_packed + [m_packed]:
                sp.sem_inc(sig, 1)

            def run_slots(it, slots, at_end):
                def pack_k(u, p):
                    kind, t = PIECES[layer(u)][p]
                    if kind != "K" or t == 0:
                        return
                    sp.wait_ge(k3_ready, level(k3_ready, it, 3 * u + t + 1))
                    for r, part in enumerate(KPARTS):
                        rows = KP[buf(u)][D * r:D * r + D, :, :]
                        if t == 1:
                            sp.dma_start(rows[:, 0:16, :], KC01[:, part, :, :]).then_inc(k_packed[0], 16)
                        else:
                            sp.dma_start(rows[:, 16:H, :], KC[2][0:64, part, :]).then_inc(k_packed[1], 16)

                def pack_q_part(u, part):
                    for r in range(len(QPARTS)):
                        if QPARTS[r] == part:
                            sp.dma_start(QP[u % 2][D * r:D * r + D, 0:16, :],
                                         QC[:, part, 0:2 * SQ]).then_inc(q_packed[0], 16)

                def pack_q(u):
                    sp.wait_ge(q1_ready, level(q1_ready, it, u + 1))
                    pack_q_part(u, 0)
                    sp.wait_ge(q2_ready, level(q2_ready, it, u + 1))
                    pack_q_part(u, 1)
                    sp.wait_ge(q3_ready, level(q3_ready, it, u + 1))
                    pack_q_part(u, 2)

                def pack_q_rest(u):
                    for r, part in enumerate(QPARTS):
                        rows = QP[u % 2][D * r:D * r + D, :, :]
                        sp.dma_start(rows[:, 16:H, :], QC[0:64, part, 2 * SQ:]).then_inc(q_packed[1], 16)

                def pack_m_part(u, part):
                    for s in range(2):
                        row, first = PROWS + 2 * s + part, H * min(s, len(SEGS[layer(u)]) - 1)
                        sp.dma_start(QP[u % 2][row:row + 1, :, :], MP[first:first + H, part, :]).then_inc(m_packed, 16)

                def pack_m(u):
                    sp.wait_ge(m1_ready, level(m1_ready, it, u + 1))
                    pack_m_part(u, 0)
                    sp.wait_ge(m2_ready, level(m2_ready, it, u + 1))
                    pack_m_part(u, 1)

                for s in slots:
                    if s == 1:
                        sp.wait_ge(kv_ready, level(kv_ready, it, piece_index(2, 0)))
                        load_kv_weights(2)
                    if s == 5 and not at_end:
                        sp.wait_ge(kv_ready, level(kv_ready, it, piece_index(6, 0)))
                        load_kv_weights(0)
                    for kind, u, n in plan(s, at_end):
                        if kind == "Q":
                            pack_q(u)
                        elif kind == "q":
                            pack_q_rest(u)
                        elif kind == "p":
                            pack_k(u, n)
                        elif kind == "M":
                            pack_m(u)

            run_slots(0, [-1, 0], False)
            with sp.Fori(0, PAIRS - 1) as it:
                run_slots(it, range(1, UNITS + 1), False)
            run_slots(PAIRS - 1, range(1, UNITS + 1), True)
            for p in range(2):
                sp.wait_ge(stored[p], 1 + PAIRS * per_pass[stored[p].name])

        @block.tensor
        def _(pe):
            mm = nc.tensor.matmul
            pe.wait_ge(zeroed, 1)
            pe.wait_ge(small_in, 16 * (1 + len(WS_NAMES)))
            for g in range(5):
                for t, (c0, cn) in enumerate(CH):
                    for k in range(NCK):
                        last = mm(MI[0:cn, (g * NT + t) * 32:(g * NT + t) * 32 + 32], WS[f"S{g}_k"][:, k, c0:c0 + cn],
                                  CS[:, k, QUAD[g], :], start=(k == 0), stop=(k == NCK - 1))
            last.then_inc(ks_ready, 1)
            for k in range(NCK):
                for g in range(4):
                    last = mm(ALL_BANKS[0][32 * g:32 * g + 32, 0:C], CS[:, k, QUAD[g], :], WS[f"S{g}_v"][:, k, :],
                              start=(k == 0), stop=(k == NCK - 1), tile_position=(0, 32 * g))
            last.then_inc(vs_ready, 1)
            for k in range(NCK):
                last = mm(ALL_BANKS[1][0:32, 0:C], CS[:, k, QUAD[4], :], WS["S4_v"][:, k, :],
                          start=(k == 0), stop=(k == NCK - 1))
            last.then_inc(vs_ready, 1)
            pe.wait_ge(ip_sq, 1)
            mm(ALL_BANKS[5][0:SQ, 0:NCK * 32], ONES[:, 0:SQ], SQI[:, :, :].rearrange("p k n -> p (k n)"),
               start=True, stop=True).then_inc(ip_ready, 1)
            pe.wait_ge(const_in, 16 * CONSTS)
            pe.wait_ge(setup_step, SETUP_STEPS)
            pe.wait_ge(vs_copied, 2)
            pe.wait_ge(w_in[0], 16 * 4)

            for sig in [kv_ready, gp_ready, q_ready, s_ready, m_ready, st_ready, pv_done, zt_used, pst_ready, o2_ready,
                        otf_ready, y_ready]:
                pe.sem_inc(sig, 1)

            def run_slots(it, slots, at_end):
                def bank_free(use):
                    if BEFORE[at_end][use] is None:
                        return
                    u, kind, n = BEFORE[at_end][use]
                    if kind == "K":
                        pe.wait_ge(k_rest, level(k_rest, it, 3 * u + n + 1))
                    elif kind == "G":
                        pe.wait_ge(g_ready, level(g_ready, it, 3 * (u % 2) + n + 1))
                    elif kind == "Y":
                        pe.wait_ge(z_ready, level(z_ready, it, GROUPS * NT * (u % 2) + n + 1))
                    else:
                        pe.wait_ge(v_ready, level(v_ready, it, v_index(u, kind, n)))

                def kv_piece(u, p, half):
                    l, par = layer(u), u % 2
                    kind, i = PIECES[l][p]
                    dst = KVB[BANK[u, kind, i]]
                    if half == 0:
                        if p == 0:
                            pe.wait_ge(ctx_in[par], level(ctx_in[par], it, 32 * (u // UNITS) + (16 if l == 0 else 32)))
                            if l in (0, 2):
                                pe.wait_ge(w0_in, level(w0_in, it, 128 * (u // UNITS) + 64 * (l // 2 + 1)))
                        bank_free((u, kind, i))
                    chunks = range(2 * half, 2 * half + 2)
                    if kind == "K":
                        c0, cn = CH[i]
                        t0, t1 = SEGS[l][-1]
                        w = W[f"L{l}_k" + ("ip" if t0 else "")]
                        for k in chunks:
                            last = mm(dst[0:cn, t0:t1], w[:, k, c0:c0 + cn], CT[par][:, k, t0:t1],
                                      start=(k == 0), stop=(k == NCK - 1))
                        if t0 and half == 1:
                            for k in range(NCK):
                                last = mm(dst[0:cn, 0:TXT], W[f"L{l}_k"][:, k, c0:c0 + cn], CT[par][:, k, 0:TXT],
                                          start=(k == 0), stop=(k == NCK - 1))
                    elif kind == "VT":
                        for k in chunks:
                            last = mm(dst[0:TXT, 0:C], CT[par][:, k, 0:TXT], W[f"L{l}_v"][:, k, :],
                                      start=(k == 0), stop=(k == NCK - 1))
                    elif kind == "V":
                        w = W[f"L{l}_v" + ("ip" if len(SEGS[l]) == 2 else "")]
                        r = rows_of(l, i)
                        for k in chunks:
                            last = mm(dst[0:r, 0:C], CT[par][:, k, 128 * i:128 * i + r], w[:, k, :],
                                      start=(k == 0), stop=(k == NCK - 1))
                        if l == 3 and half == 1:
                            for k in range(NCK):
                                last = mm(dst[0:r, C:C + 4], CT[par][:, k, 128 * i:128 * i + r],
                                          CT[par][:, k, MAIN[3]:T], start=(k == 0), stop=(k == NCK - 1))
                    else:
                        r, wd = rows_of(3, i), min(128 * i + 128, MAIN[3])
                        for k in chunks:
                            last = mm(dst[0:r, 0:wd], CT[par][:, k, 128 * i:128 * i + r], CT[par][:, k, 0:wd],
                                      start=(k == 0), stop=(k == NCK - 1))
                    if half == 1:
                        last.then_inc(kv_ready, 1)

                def queries(u):
                    l, par = layer(u), u % 2
                    if l == 0:
                        pe.wait_ge(xt_in[par], level(xt_in[par], it, 32 * (u // UNITS + 1)))
                    pe.wait_ge(x_ready, level(x_ready, it, u - 1))
                    if u == 1:
                        pe.wait_ge(q_rest, level(q_rest, it, 1))
                    for t, (c0, cn) in enumerate(CH):
                        for k, (_, kn) in enumerate(CH):
                            last = mm(MI[0:cn, t * SQ:(t + 1) * SQ], WQ[l][0:kn, k, c0:c0 + cn],
                                      sources(u)[0:kn, k, :], start=(k == 0), stop=(k == NT - 1))
                    last.then_inc(q_ready, 1)

                def scores(u, h):
                    if h == 0:
                        pe.wait_ge(q_packed[0], level(q_packed[0], it, 96 * (u + 1)))
                        pe.wait_ge(k_packed[0], level(k_packed[0], it, 96 * (u + 1)))
                    if h == 16:
                        pe.wait_ge(q_packed[1], level(q_packed[1], it, 96 * (u + 1)))
                        pe.wait_ge(k_packed[1], level(k_packed[1], it, 96 * (u + 1)))
                    n = u * H + h
                    pe.wait_ge(s_used, level(s_used, it, n - 1))
                    mm(SB_[n % 2][0:SQ, 0:T], QP[u % 2][0:PROWS, h, :], KP[buf(u)][0:PROWS, h, :],
                       start=True, stop=True).then_inc(s_ready, 1)

                def maxima(u):
                    pe.wait_ge(s_used, level(s_used, it, (u + 1) * H))
                    pe.wait_ge(q_rest, level(q_rest, it, u + 1 if u >= UNITS - 1 else u + 2))
                    pe.wait_ge(m2_ready, level(m2_ready, it, u))
                    nc.tensor.transpose(MI[0:4 * H, 0:SQ], MX[:, :], IDN[0:SQ, 0:SQ]).then_inc(m_ready, 1)

                def small_t(u):
                    if layer(u) < 2:
                        pe.wait_ge(m2_ready, level(m2_ready, it, u + 1))
                    pe.wait_ge(ps_ready, level(ps_ready, it, small_nth(u)))
                    for k in range(small_groups(u)):
                        last = nc.tensor.transpose(MI[0:80, (k + 1) * 128:(k + 1) * 128 + SQ],
                                                   SP_[:, k, :, :].rearrange("p h n -> p (h n)"), IDN[0:SQ, 0:SQ])
                    last.then_inc(pst_ready, 1)

                def back_scores(u, k):
                    g, c = k // NT, k % NT
                    if k == 0:
                        pe.wait_ge(m_packed, level(m_packed, it, 64 * (u + 1)))
                        pe.wait_ge(o_ready, level(o_ready, it, u))
                    n = u * GROUPS * NT + k
                    r = rows_of(layer(u), c)
                    pe.wait_ge(exp_done, level(exp_done, it, n - 1))
                    for j in range(4):
                        h = 4 * g + j
                        last = mm(ST[n % 2][0:r, j * SQ:(j + 1) * SQ],
                                  KP[buf(u)][0:XROWS, h, 128 * c:128 * c + r], QP[u % 2][0:XROWS, h, :],
                                  start=True, stop=True)
                    last.then_inc(st_ready, 1)

                def back_values(u, g):
                    l, par = layer(u), u % 2
                    gn = u * GROUPS + g
                    ns = len(SEGS[l])
                    if g == 0:
                        pe.wait_ge(v_ready, level(v_ready, it, over_units(V_USES, u + 1)))
                        pe.wait_ge(ones_ready, level(ones_ready, it, u + 1))
                        if l == 3:
                            pe.wait_ge(g_ready, level(g_ready, it, 3 * (par + 1)))
                    pe.wait_ge(ot_used, level(ot_used, it, gn))
                    o0 = (ns - 1) * SQ
                    pt = PT[gn % 2]
                    for c in range(NT):
                        pe.wait_ge(exp_done, level(exp_done, it, gn * NT + c + 1))
                        r = rows_of(l, c)
                        if c == 0 and ns == 2:
                            for j in range(4):
                                mm(OT[32 * j:32 * j + VW, 0:SQ], VT[par][0:TXT, 4 * g + j, :],
                                   pt[0:TXT, 0, j * SQ:(j + 1) * SQ], start=True, stop=True, tile_position=(0, 32 * j))
                        for j in range(4):
                            last = mm(OT[32 * j:32 * j + VW, o0:o0 + SQ], VA[buf(u)][0:r, c, 4 * g + j, :],
                                      pt[0:r, c, j * SQ:(j + 1) * SQ], start=(c == 0), stop=(c == 2 and l < 3),
                                      tile_position=(0, 32 * j))
                    if l < 3:
                        last.then_inc(pv_done, 1)

                def gram(u, k):
                    g, i = k // NT, k % NT
                    par, gn = u % 2, u * GROUPS + g
                    dst = KVB[BANK[u, "Y", k]]
                    r = rows_of(3, i)
                    bank_free((u, "Y", k))
                    for j in range(i, NT):
                        rj = rows_of(3, j)
                        m = mm(dst[0:r, 0:4 * SQ], GM[par][0:rj, j, 128 * i:128 * i + r],
                               PT[gn % 2][0:rj, j, :], start=(j == i), stop=(j == NT - 1))
                    m.then_inc(gp_ready, 1)

                def norm(u, k):
                    i = k % NT
                    n = (u % 2) * GROUPS * NT + k
                    pe.wait_ge(z_ready, level(z_ready, it, n + 1))
                    r = rows_of(3, i)
                    for j in range(4):
                        m = mm(OT[32 * j:32 * j + VW, 0:SQ], NSEL[0:r, :], ZT[n % 2][0:r, j * SQ:(j + 1) * SQ],
                               start=False, stop=(i == NT - 1), tile_position=(0, 32 * j))
                    m.then_inc((zt_used if i < 2 else pv_done), 1)

                def final_heads(u):
                    l = layer(u)
                    pe.wait_ge(ot_used, level(ot_used, it, (u + 1) * GROUPS))
                    pe.wait_ge(exp_done, level(exp_done, it, (u + 1) * GROUPS * NT))
                    for s in range(len(SEGS[l])):
                        for g in range(GROUPS):
                            dst = ST[1][0:SQ, s * 128:s * 128 + 128] if g == 4 else \
                                [ST[0], OT][s][0:SQ, g * 128:g * 128 + 128]
                            last = nc.tensor.transpose(dst, OTS[:, g, s, :], IDN[:, :])
                    last.then_inc(o2_ready, 1)

                def final_transpose(u):
                    l = layer(u)
                    pe.wait_ge(o_ready, level(o_ready, it, u + 1))
                    ahead = u == UNITS - 2 or u == UNITS - 1 and not at_end
                    pe.wait_ge(m2_ready, level(m2_ready, it, u + 2 if ahead else u + 1))
                    if l == 3:
                        small_t(u)
                    if small_groups(u):
                        pe.wait_ge(pst_copied, level(pst_copied, it, small_nth(u)))
                        pe.wait_ge(vb_ready, level(vb_ready, it, small_nth(u)))
                    for t, (c0, cn) in enumerate(CH):
                        last = mm(MI[0:cn, t * SQ:(t + 1) * SQ], OS[:, c0:c0 + cn], IDN[0:SQ, 0:SQ],
                                  start=True, stop=(small_groups(u) == 0))
                        for k in range(small_groups(u)):
                            last = mm(MI[0:cn, t * SQ:(t + 1) * SQ], VB[:, k, c0:c0 + cn], PST[u % 2][:, k, :],
                                      start=False, stop=(k == small_groups(u) - 1))
                    last.then_inc(otf_ready, 1)

                def final_project(u):
                    l = layer(u)
                    pe.wait_ge(otf_copied, level(otf_copied, it, u + 1))
                    for t, (c0, cn) in enumerate(CH):
                        for k, (_, kn) in enumerate(CH):
                            last = mm(MI[0:cn, t * SQ:(t + 1) * SQ], WO[l][0:kn, k, c0:c0 + cn],
                                      OTF[0:kn, k, :], start=(k == 0), stop=(k == NT - 1))
                    last.then_inc(y_ready, 1)

                for s in slots:
                    for kind, u, n in plan(s, at_end):
                        if kind == "s":
                            scores(u, n)
                        elif kind == "h":
                            kv_piece(u, n, 0)
                        elif kind == "p":
                            kv_piece(u, n, 1)
                        elif kind == "Q":
                            queries(u)
                        elif kind == "b":
                            back_scores(u, n)
                        elif kind == "V":
                            back_values(u, n)
                        elif kind == "g":
                            gram(u, n)
                        elif kind == "n":
                            norm(u, n)
                        elif kind == "M":
                            maxima(u)
                        elif kind == "t":
                            small_t(u)
                        elif kind == "H":
                            final_heads(u)
                        elif kind == "T":
                            final_transpose(u)
                        elif kind == "R":
                            final_project(u)

            run_slots(0, [-1, 0], False)
            pe.wait_ge(rows_in, 48)
            for l in range(1, 4):
                pe.wait_ge(w_in[l], 16 * (4 + (len(KV_W[l]) if l in (1, 3) else 0)))
            with pe.Fori(0, PAIRS - 1) as it:
                run_slots(it, range(1, UNITS + 1), False)
            run_slots(PAIRS - 1, range(1, UNITS + 1), True)

        @block.scalar
        def _(act):
            def copy(dst, src, scale=1.0):
                return nc.scalar.activation(dst, src, ACT.Copy, scale=scale)

            act.wait_ge(const_in, 16 * CONSTS)
            act.wait_ge(vs_ready, 1)
            copy(VSB[:, 0, :], ALL_BANKS[0][:, 0:C]).then_inc(vs_copied, 1)
            act.wait_ge(vs_ready, 2)
            copy(VSB[0:32, 1, :], ALL_BANKS[1][0:32, 0:C]).then_inc(vs_copied, 1)
            act.wait_ge(ip_summed, 1)
            flat_ipi = IPI[:, :, :].rearrange("p b n -> p (b n)")
            nc.scalar.activation(flat_ipi, flat_ipi, ACT.Sqrt).then_inc(ip_sqrt, 1)

            for sig in ctx_in + xt_in + stored + [k1_ready, k2_ready, v_ready, q1_ready, q2_ready, m1_ready, exp_done,
                                                  se_ready, sq_done, pst_copied, vr_in, otf_copied]:
                act.sem_inc(sig, 1)
            def load_ctx(name, p, batch):
                act.dma_start(CT[p][:, :, :],
                              ins[name][batch].rearrange("(k p) t -> p k t", p=128)).then_inc(ctx_in[p], 16)

            def load_x(p, batch):
                act.dma_start(XI[p][:, 0:2, :], ins["x_t"][batch, 0:256, :]
                              .rearrange("(k p) q -> p k q", p=128)).then_inc(xt_in[p], 16)
                act.dma_start(XI[p][0:64, 2, :], ins["x_t"][batch, 256:C, :]).then_inc(xt_in[p], 16)

            load_ctx("ctx0", 0, 0)
            load_ctx("ctx0", 1, 1)
            load_x(0, 0)
            load_x(1, 1)
            def run_slots(it, slots, at_end):
                def kv_piece(u, p):
                    l, par = layer(u), u % 2
                    kind, i = PIECES[l][p]
                    n = piece_index(u, p)
                    src = KVB[BANK[u, kind, i]]
                    if kind == "K":
                        cn = CH[i][1]
                        m = MAIN[l]
                        act.wait_ge(kv_ready, level(kv_ready, it, n + 1))
                        act.wait_ge(k_packed[i // 2], level(k_packed[i // 2], it, 96 * u))
                        copy(KC[i][0:cn, 0, 0:m], src[0:cn, 0:m]).then_inc(k1_ready, 1)
                    elif kind in ("V", "VT"):
                        act.wait_ge(kv_ready, level(kv_ready, it, n + 1))
                        if kind == "VT":
                            act.wait_ge(pv_done, level(pv_done, it, (u - 3) * GROUPS))
                            copy(VT[par][0:TXT, :, 0:D],
                                            src[0:TXT, 0:C].rearrange("p (h c) -> p h c", h=H)).then_inc(v_ready, 1)
                            return
                        act.wait_ge(pv_done, level(pv_done, it, (u - 1 if u >= UNITS else u - 2) * GROUPS))
                        r = rows_of(l, i)
                        if l == 3:
                            copy(VA[buf(u)][0:r, i, :, R_COL:R_COL + 4],
                                 src[0:r, C:C + 4].rearrange("p (o c) -> p o c", o=1).to_broadcast([r, H, 4]))
                        copy(VA[buf(u)][0:r, i, :, 0:D], src[0:r, 0:C].rearrange("p (h c) -> p h c", h=H),
                                        scale=IPM[0:r, 1:2] if i == 0 and len(SEGS[l]) == 2 else 1.0).then_inc(v_ready, 1)

                def k_second(u, i):
                    cn, m = CH[i][1], MAIN[layer(u)]
                    act.wait_ge(k_rest, level(k_rest, it, 3 * u + i + 1))
                    copy(KC[i][0:cn, 1, 0:m], KR[i][0:cn, 0:m]).then_inc(k2_ready, 1)

                def queries(u):
                    act.wait_ge(q_ready, level(q_ready, it, u + 1))
                    act.wait_ge(q_packed[0], level(q_packed[0], it, 96 * u))
                    act.wait_ge(q_packed[1], level(q_packed[1], it, 96 * u))
                    act.wait_ge(st_ready, level(st_ready, it, (u - 1) * GROUPS * NT))
                    copy(QC[:, 0, :], MI[:, 0:NT * SQ]).then_inc(q1_ready, 1)
                    act.wait_ge(q_rest, level(q_rest, it, u + 1))
                    copy(QC[:, 1, :], QR[:, :]).then_inc(q2_ready, 1)

                def exponentials(u, k):
                    gn, c = u * GROUPS + k // NT, k % NT
                    n = u * GROUPS * NT + k
                    act.wait_ge(st_ready, level(st_ready, it, n + 1))
                    if c == 0:
                        act.wait_ge(pv_done, level(pv_done, it, gn - 1))
                    r = rows_of(layer(u), c)
                    nc.scalar.activation(PT[gn % 2][0:r, c, :], ST[n % 2][0:r, 0:4 * SQ],
                                         ACT.Exp, scale=SCALE).then_inc(exp_done, 1)

                def small_exp(u):
                    k = small_groups(u)
                    act.wait_ge(sx_ready, level(sx_ready, it, small_nth(u)))
                    nc.scalar.activation(SE[:, 0:k, :, :], SE[:, 0:k, :, :], ACT.Exp,
                                                     scale=SCALE if layer(u) == 0 else 1.0).then_inc(se_ready, 1)

                def small_t(u):
                    k = small_groups(u)
                    act.wait_ge(pst_ready, level(pst_ready, it, small_nth(u)))
                    act.wait_ge(otf_ready, level(otf_ready, it, u - 1))
                    copy(PST[u % 2][:, 0:k, :], MI[0:80, 128:128 + 128 * k]
                                       .rearrange("p (k q) -> p k q", k=k)[:, :, 0:SQ]).then_inc(pst_copied, 1)

                def maxima(u):
                    ns = len(SEGS[layer(u)])
                    act.wait_ge(m_ready, level(m_ready, it, u + 1))
                    act.wait_ge(m_packed, level(m_packed, it, 64 * u))
                    copy(MP[0:ns * H, 0, :], MI[0:ns * H, 0:SQ]).then_inc(m1_ready, 1)

                def load_small_v(u):
                    if not small_groups(u):
                        return
                    act.wait_ge(vb_ready, level(vb_ready, it, small_nth(u) - 1))
                    for k, g in enumerate(SMALL[layer(u)]):
                        act.dma_start(
                            VR[:, k, :], dram_vs[g, it * 2 + u % 2].rearrange("(o n) c -> o n c", o=1)
                            .to_broadcast([H, 4, C])).then_inc(vr_in, 16)

                def loads_and_stores(s):
                    if s in (0, 1) or s == UNITS and not at_end:
                        p = s % 2
                        act.wait_ge(kv_ready, level(kv_ready, it, piece_index(s + 1, 0)))
                        load_ctx("ctx1", p, it * 2 + (2 if s == UNITS else 0) + p)
                    if s in (3, 4) and not at_end:
                        act.wait_ge(x_ready, level(x_ready, it, s - 2))
                        load_x(s - 3, it * 2 + s - 1)
                    if s in (6, 7) and not at_end:
                        act.wait_ge(kv_ready, level(kv_ready, it, piece_index(s + 1, 0)))
                        load_ctx("ctx0", s - 6, it * 2 + s - 4)
                    if s == UNITS:
                        store(0)

                def store(p):
                    act.wait_ge(x_ready, level(x_ready, it, UNITS - 1 + p))
                    act.dma_start(out_t[it * 2 + p, 0:256, :].rearrange("(k p) q -> p k q", p=128),
                                  XT[p][:, 0:2, :]).then_inc(stored[p], 16)
                    act.dma_start(out_t[it * 2 + p, 256:C, :], XT[p][0:64, 2, :]).then_inc(stored[p], 16)

                for s in slots:
                    if s == 0:
                        loads_and_stores(s)
                    for kind, u, n in plan(s, at_end):
                        if kind == "p":
                            kv_piece(u, n)
                        elif kind == "k":
                            k_second(u, n)
                        elif kind == "Q":
                            queries(u)
                        elif kind == "v":
                            load_small_v(u)
                            loads_and_stores(s)
                        elif kind == "b":
                            exponentials(u, n)
                        elif kind == "M":
                            maxima(u)
                        elif kind == "m":
                            small_exp(u)
                        elif kind == "t":
                            small_t(u)
                        elif kind == "H" and layer(u) == 3:
                            act.wait_ge(sq_ready, level(sq_ready, it, 2 * (u - 6) + 2))
                            nc.scalar.activation(QN[:, 0, :], QN[:, 0, :], ACT.Sqrt).then_inc(sq_done, 1)
                            small_exp(u)
                        elif kind == "T":
                            if layer(u) == 3:
                                small_t(u)
                            act.wait_ge(otf_ready, level(otf_ready, it, u + 1))
                            copy(OTF[:, :, :].rearrange("p t q -> p (t q)"), MI[:, 0:NT * SQ]).then_inc(otf_copied, 1)
                    if s == UNITS:
                        store(1)

            run_slots(0, [-1, 0], False)
            with act.Fori(0, PAIRS - 1) as it:
                run_slots(it, range(1, UNITS + 1), False)
            run_slots(PAIRS - 1, range(1, UNITS + 1), True)

        @block.vector
        def _(dve):
            v = nc.vector
            steps = [0]

            def setup(instruction):
                steps[0] += 1
                instruction.then_inc(setup_step, 1)
                dve.wait_ge(setup_step, steps[0])

            for bank_ in ALL_BANKS:
                setup(v.memset(bank_[:, :], 0.0))
            for buf in [MX[:, :], QC[:, :, :], QR[:, :], KC[0][:, :, :], KC[1][:, :, :], KC[2][:, :, :], OTF[:, :, :],
                        KSM[:, 0, :, :, :, :], KSM[:, 1, :, :, :, :], KSM[:, 2, :, :, :, :]] \
                    + [VA[k][:, :, :, :] for k in range(3)] + [VT[k][:, :, :] for k in range(2)]:
                setup(v.memset(buf, 0.0))
            for k in range(3):
                setup(v.memset(VA[k][:, :, :, ONE_COL:ONE_COL + 1], 1.0))
            for k in range(2):
                setup(v.memset(VT[k][:, :, ONE_COL:ONE_COL + 1], 1.0))
            setup(v.memset(NSEL[:, :], 0.0))
            setup(v.memset(NSEL[:, N_COL:N_COL + 1], 1.0))
            setup(v.memset(ONES[:, :], 1.0))
            v.memset(SM[:, :, :, :], 0.0).then_inc(zeroed, 1)
            dve.wait_ge(small_in, 16 * (1 + len(WS_NAMES)))
            for k in range(NCK):
                ip = CS[:, k, QUAD[4], :]
                ins_ = v.tensor_tensor(SQI[:, k, :], ip, ip, ALU.mult)
                if k < NCK - 1:
                    setup(ins_)
            ins_.then_inc(ip_sq, 1)
            dve.wait_ge(const_in, 16 * CONSTS)
            v.tensor_copy(SEG[:, :], SEG32).then_inc(seg_ready, 1)
            edges = [(0, 0, ALU.is_le), (1, 1, ALU.is_le), (2, 0, ALU.is_ge), (3, 1, ALU.is_ge)]
            for k, (edge, axis, op) in enumerate(edges):
                setup(v.tensor_scalar(IN[:, k, :, :], BB[:, :, :, edge], GXY[:, axis:axis + 1], None, op))
            for k in range(1, 4):
                setup(v.tensor_tensor(IN[:, 0, :, :], IN[:, 0, :, :], IN[:, k, :, :], ALU.mult))
            setup(v.tensor_scalar(MSK[:, :, 1, :], IN[:, 0, :, :], -NEG, NEG, ALU.mult, ALU.add))
            setup(v.tensor_reduce(ANY[:, :], IN[:, 0, :, :], AX.X, ALU.max))
            setup(v.tensor_scalar(MSK[:, :, 0, :], ANY[:, :].rearrange("p (b o) -> p b o", o=1).to_broadcast([SQ, B, 4]),
                                  NEG, None, ALU.mult))
            dve.wait_ge(ks_ready, 1)
            flat = [KSM[:, part, :, :, :, :].rearrange("p g t b n -> p (g t b n)") for part in range(3)]
            src = MI[:, 0:5 * NT * 32]
            setup(v.tensor_copy(flat[0], src))
            setup(v.tensor_tensor(KSR[:, :], src, flat[0], ALU.subtract))
            setup(v.tensor_copy(flat[1], KSR[:, :]))
            v.tensor_tensor(flat[2], KSR[:, :], flat[1], ALU.subtract).then_inc(ks_copy, 1)
            dve.wait_ge(ip_ready, 1)
            flat_ipi = IPI[:, :, :].rearrange("p b n -> p (b n)")
            v.tensor_reduce(flat_ipi, ALL_BANKS[5][0:SQ, 0:NCK * 32].rearrange("p (k n) -> p n k", k=NCK),
                            AX.X, ALU.add).then_inc(ip_summed, 1)
            dve.wait_ge(ip_sqrt, 1)
            setup(v.tensor_scalar(flat_ipi, flat_ipi, EPS, None, ALU.max))
            setup(v.reciprocal(flat_ipi, flat_ipi))
            assert steps[0] == SETUP_STEPS, steps[0]

            for sig in [k_rest, g_ready, z_ready, q_rest, q3_ready, s_used, m2_ready, ot_used, sx_ready, ps_ready,
                        sq_ready, o_ready, x_ready, dve_step]:
                dve.sem_inc(sig, 1)
            def run_slots(it, slots, at_end):
                steps[0] = 0 if slots[0] < 0 else DVE_AHEAD

                def step(instruction):
                    steps[0] += 1
                    instruction.then_inc(dve_step, 1)
                    dve.wait_ge(dve_step, level(dve_step, it, steps[0]))

                def kv_piece(u, p):
                    l, par = layer(u), u % 2
                    kind, i = PIECES[l][p]
                    src = KVB[BANK[u, kind, i]]
                    if kind == "K":
                        cn, m = CH[i][1], MAIN[l]
                        dve.wait_ge(k1_ready, level(k1_ready, it, 3 * u + i + 1))
                        dve.wait_ge(k3_ready, level(k3_ready, it, 3 * (u - 1) + i + 1))
                        v.tensor_tensor(KR[i][0:cn, 0:m], src[0:cn, 0:m], KC[i][0:cn, 0, 0:m],
                                                  ALU.subtract).then_inc(k_rest, 1)
                    elif kind == "G":
                        dve.wait_ge(kv_ready, level(kv_ready, it, piece_index(u, p) + 1))
                        r, wd = rows_of(3, i), min(128 * i + 128, MAIN[3])
                        dve.wait_ge(pv_done, level(pv_done, it, 0))
                        if i:
                            step(v.tensor_scalar_mul(GM[par][0:r, i, 0:128 * i], src[0:r, 0:128 * i], 2.0))
                        v.tensor_copy(GM[par][0:r, i, 128 * i:wd], src[0:r, 128 * i:wd]).then_inc(g_ready, 1)

                def queries(u):
                    dve.wait_ge(q1_ready, level(q1_ready, it, u + 1))
                    v.tensor_tensor(QR[:, :], MI[:, 0:NT * SQ], QC[:, 0, :], ALU.subtract).then_inc(q_rest, 1)
                    dve.wait_ge(q2_ready, level(q2_ready, it, u + 1))
                    v.tensor_tensor(QC[:, 2, :], QR[:, :], QC[:, 1, :], ALU.subtract).then_inc(q3_ready, 1)

                def max_of(u, h):
                    l = layer(u)
                    if h == 0:
                        dve.wait_ge(m_ready, level(m_ready, it, u))
                    n = u * H + h
                    dve.wait_ge(s_ready, level(s_ready, it, n + 1))
                    src = SB_[n % 2]
                    if small_groups(u):
                        m = small_groups(u)
                        dst = SM3[u % 2][:, :, h, :] if l == 3 else SM[:, :, h, :]
                        v.tensor_copy(dst, src[0:SQ, MAIN[l]:MAIN[l] + 4 * m].rearrange("p (g n) -> p g n", g=m))
                    for s, (t0, t1) in enumerate(SEGS[l]):
                        last = v.tensor_reduce(MX[:, s * H + h:s * H + h + 1], src[0:SQ, t0:t1], AX.X, ALU.max,
                                               negate=True)
                    last.then_inc(s_used, 1)

                def small_softmax(u, scores_):
                    l, k = layer(u), small_groups(u)
                    if l == 1:
                        def view(buf):
                            return buf[:, 0:k, :, :].rearrange("p g h n -> p h g n")
                        m = H
                        axis = AX.XY

                        def wide(vec):
                            return vec[:, 0:H].rearrange("p (o h i) -> p o h i", o=1, i=1).to_broadcast([SQ, k, H, 4])
                        full = lambda buf: buf[:, 0:k, :, :]
                    else:
                        m = k * H
                        axis = AX.X

                        def view(buf):
                            return buf[:, 0:k, :, :].rearrange("p g h n -> p (g h) n")

                        def wide(vec):
                            return vec[:, 0:m].rearrange("p (h i) -> p h i", i=1).to_broadcast([SQ, m, 4])
                        full = view
                    step(v.tensor_reduce(SX[:, 0:m], view(scores_), axis, ALU.max))
                    v.tensor_tensor(full(SE), full(scores_), wide(SX), ALU.subtract).then_inc(sx_ready, 1)
                    dve.wait_ge(se_ready, level(se_ready, it, small_nth(u)))
                    step(v.tensor_reduce(SS[:, 0:m], view(SE), axis, ALU.add))
                    step(v.reciprocal(SR[:, 0:m], SS[:, 0:m]))
                    if l == 3:
                        v.scalar_tensor_tensor(full(SP_), full(SE), SPM[:, 0:1], wide(SR),
                                               ALU.mult, ALU.mult).then_inc(ps_ready, 1)
                    else:
                        v.tensor_tensor(full(SP_), full(SE), wide(SR), ALU.mult).then_inc(ps_ready, 1)

                def maxima(u):
                    l = layer(u)
                    ns = len(SEGS[l])
                    dve.wait_ge(m1_ready, level(m1_ready, it, u + 1))
                    v.tensor_tensor(MP[0:ns * H, 1, :], MI[0:ns * H, 0:SQ], MP[0:ns * H, 0, :],
                                                ALU.subtract).then_inc(m2_ready, 1)

                def small_front(u):
                    l = layer(u)
                    if l < 2:
                        dve.wait_ge(s_used, level(s_used, it, (u + 1) * H))
                        dve.wait_ge(pst_ready, level(pst_ready, it, small_nth(u) - 1))
                        if l == 1:
                            for g in range(2):
                                step(v.scalar_tensor_tensor(
                                    SM[:, g, :, :], SM[:, g, :, :], SCALE,
                                    MSK[:, it * 2 + u % 2, g, :].rearrange("p (o n) -> p o n", o=1)
                                    .to_broadcast([SQ, H, 4]), ALU.mult, ALU.add))
                        small_softmax(u, SM)

                def times_probs(u, k):
                    g, i = k // NT, k % NT
                    par, gn = u % 2, u * GROUPS + g
                    n = par * GROUPS * NT + k
                    r = rows_of(3, i)
                    dve.wait_ge(gp_ready, level(gp_ready, it, n + 1))
                    if i == 1:
                        dve.wait_ge(pv_done, level(pv_done, it, gn))
                    else:
                        dve.wait_ge(zt_used, level(zt_used, it, 2 * (par * GROUPS + g) + i // 2))
                    v.tensor_tensor(ZT[n % 2][0:r, :], KVB[BANK[u, "Y", k]][0:r, 0:4 * SQ],
                                    PT[gn % 2][0:r, i, :], ALU.mult).then_inc(z_ready, 1)

                def copy_out(u, g):
                    ns = len(SEGS[layer(u)])
                    dve.wait_ge(pv_done, level(pv_done, it, u * GROUPS + g + 1))
                    if g == 0:
                        dve.wait_ge(o2_ready, level(o2_ready, it, u))
                    v.tensor_copy(OTS[:, g, 0:ns, :],
                                  OT[:, 0:ns * SQ].rearrange("p (s q) -> p s q", s=ns)).then_inc(ot_used, 1)

                def parts(s, lo, hi):
                    return [([ST[0], OT][s][0:SQ, 0:512].rearrange("p (h c) -> p h c", c=32)[:, :, lo:hi], 0, 16),
                            (ST[1][0:SQ, s * 128:s * 128 + 128].rearrange("p (h c) -> p h c", c=32)[:, :, lo:hi], 16, H)]

                def final(u):
                    l, par = layer(u), u % 2
                    ns = len(SEGS[l])
                    dve.wait_ge(o2_ready, level(o2_ready, it, u + 1))
                    dve.wait_ge(otf_ready, level(otf_ready, it, u))
                    for s in range(ns):
                        for src_, h0, h1 in parts(s, ONE_COL, ONE_COL + 1):
                            step(v.reciprocal(ZR[:, s, h0:h1].rearrange("p (h o) -> p h o", o=1), src_))
                    for s in range(ns):
                        dst = [OS, O2][s]
                        for src_, h0, h1 in parts(s, 0, D):
                            ins_ = v.tensor_tensor(dst[:, h0 * D:h1 * D].rearrange("p (h c) -> p h c", c=D), src_,
                                                   ZR[:, s, h0:h1].rearrange("p (h o) -> p h o", o=1)
                                                   .to_broadcast([SQ, h1 - h0, D]), ALU.mult)
                            if h0 == 0 or s < ns - 1 or ns == 2 or l == 3:
                                step(ins_)
                    if l == 3:
                        for src_, h0, h1 in parts(0, N_COL, N_COL + 1):
                            v.tensor_scalar(QN[:, 0, h0:h1].rearrange("p (h o) -> p h o", o=1), src_, 0.0,
                                                        None, ALU.max).then_inc(sq_ready, 1)
                        dve.wait_ge(sq_done, level(sq_done, it, par + 1))
                        for src_, h0, h1 in parts(0, ONE_COL, ONE_COL + 1):
                            step(v.scalar_tensor_tensor(QN[:, 1, h0:h1].rearrange("p (h o) -> p h o", o=1), src_, EPS,
                                                        QN[:, 0, h0:h1].rearrange("p (h o) -> p h o", o=1),
                                                        ALU.mult, ALU.max))
                        step(v.reciprocal(QN[:, 2, :], QN[:, 1, :]))
                        for src_, h0, h1 in parts(0, R_COL, R_COL + 4):
                            ins_ = v.tensor_tensor(QS[:, h0:h1, :], src_, QN[:, 2, h0:h1].rearrange("p (h o) -> p h o", o=1)
                                                   .to_broadcast([SQ, h1 - h0, 4]), ALU.mult)
                            if h0 == 0:
                                step(ins_)
                        ins_.then_inc(o_ready, 1)
                        dve.wait_ge(o_ready, level(o_ready, it, u + 1))
                        step(v.scalar_tensor_tensor(QS[:, :, :], QS[:, :, :], SEM_SCALE,
                                                    IPI[:, it * 2 + u % 2, :].rearrange("p (o n) -> p o n", o=1)
                                                    .to_broadcast([SQ, H, 4]), ALU.mult, ALU.mult))
                        step(v.scalar_tensor_tensor(QS[:, :, :], SM3[u % 2][:, 0, :, :], SCALE, QS[:, :, :],
                                                    ALU.mult, ALU.add))
                        dve.wait_ge(pst_ready, level(pst_ready, it, small_nth(u) - 1))
                        small_softmax(u, QS[:, :, :].rearrange("p (g h) n -> p g h n", g=1))
                    elif ns == 2:
                        v.tensor_tensor(OS[:, :], OS[:, :], O2[:, :], ALU.add).then_inc(o_ready, 1)
                    else:
                        ins_.then_inc(o_ready, 1)

                def result(u):
                    l, par = layer(u), u % 2
                    dve.wait_ge(y_ready, level(y_ready, it, u + 1))
                    if l == 0:
                        dve.wait_ge(stored[par], level(stored[par], it, 0))
                    for t, (c0, cn) in enumerate(CH):
                        ins_ = v.scalar_tensor_tensor(XT[par][0:cn, t, :], MI[0:cn, t * SQ:(t + 1) * SQ],
                                                      BIAS[0:cn, l, t:t + 1], sources(u)[0:cn, t, :],
                                                      ALU.add, ALU.add)
                    ins_.then_inc(x_ready, 1)

                for s in slots:
                    for kind, u, n in plan(s, at_end):
                        if kind == "s":
                            max_of(u, n)
                        elif kind == "p":
                            kv_piece(u, n)
                        elif kind == "Q":
                            queries(u)
                        elif kind == "z":
                            times_probs(u, n)
                        elif kind == "o":
                            copy_out(u, n)
                        elif kind == "M":
                            maxima(u)
                        elif kind == "m":
                            small_front(u)
                        elif kind == "H":
                            final(u)
                        elif kind == "R":
                            result(u)

                assert at_end or steps[0] == DVE_AHEAD + (DVE_STEPS if slots[0] > 0 else 0), steps[0]

            run_slots(0, [-1, 0], False)
            with dve.Fori(0, PAIRS - 1) as it:
                run_slots(it, range(1, UNITS + 1), False)
            run_slots(PAIRS - 1, range(1, UNITS + 1), True)

        @block.gpsimd
        def _(pool):
            g_ = nc.gpsimd
            pool.wait_ge(ks_copy, 1)
            pool.wait_ge(const_in, 16 * CONSTS)

            for sig in [k3_ready, ones_ready, vb_ready]:
                pool.sem_inc(sig, 1)
            def run_slots(it, slots, at_end):
                def kv_piece(u, p):
                    l, par = layer(u), u % 2
                    kind, i = PIECES[l][p]
                    if kind == "K":
                        cn, m = CH[i][1], MAIN[l]
                        pool.wait_ge(st_ready, level(st_ready, it, (u - 1 if u >= UNITS else u - 2) * GROUPS * NT))
                        pool.wait_ge(k2_ready, level(k2_ready, it, 3 * u + i + 1))
                        last = g_.tensor_tensor(KC[i][0:cn, 2, 0:m], KR[i][0:cn, 0:m], KC[i][0:cn, 1, 0:m],
                                                ALU.subtract)
                        for k, grp in enumerate(SMALL[l]):
                            last = g_.tensor_copy(KC[i][:, :, m + 4 * k:m + 4 * k + 4],
                                                  KSM[:, :, grp, i, it * 2 + u // UNITS * 2 + par, :])
                        last.then_inc(k3_ready, 1)
                    elif kind == "V" and i == 0:
                        pool.wait_ge(pv_done, level(pv_done, it, (u - 1 if u >= UNITS else u - 2) * GROUPS))
                        col = 1 if len(SEGS[l]) == 2 else 0
                        marks = IPM[:, col:col + 1].rearrange("p (o i) -> p o i", o=1).to_broadcast([128, H, 1])
                        g_.tensor_tensor(VA[buf(u)][:, 0, :, ONE_COL:ONE_COL + 1], marks, marks,
                                         ALU.mult).then_inc(ones_ready, 1)

                def mask_small_v(u):
                    if small_groups(u):
                        pool.wait_ge(vr_in, level(vr_in, it, 16 * over_units(groups_of_units, u + 1)))
                        pool.wait_ge(otf_ready, level(otf_ready, it, u))
                        for k in range(small_groups(u)):
                            last = g_.tensor_tensor(VB[:, k, :], VR[:, k, :], HM[:, :], ALU.mult)
                        last.then_inc(vb_ready, 1)

                for s in slots:
                    for kind, u, n in plan(s, at_end):
                        if kind == "p":
                            kv_piece(u, n)
                        elif kind == "v":
                            mask_small_v(u)

            run_slots(0, [-1, 0], False)
            with pool.Fori(0, PAIRS - 1) as it:
                run_slots(it, range(1, UNITS + 1), False)
            run_slots(PAIRS - 1, range(1, UNITS + 1), True)

CONSTS = 8
SETUP_STEPS = 49
DVE_STEPS = 84
DVE_AHEAD = 3


def kernel(**inputs):
    import numpy as np
    import concourse.bacc as bacc
    from concourse.bass_utils import run_bass_kernel_spmd

    def arr(name):
        return np.asarray(inputs[name])

    ctx = arr("ctx_2048").transpose(0, 2, 1)
    order0 = list(range(TXT)) + list(range(TXT + 8, T)) + list(range(TXT, TXT + 8))
    small = list(range(TXT, TXT + 8)) + list(range(T - 8, T))
    data = {
        "x_t": arr("x").transpose(0, 2, 1),
        "ctx0": ctx[:, :, order0],
        "ctx1": ctx,
        "ctx_small": ctx[:, :, small].reshape(B, CC, 4, 4).transpose(1, 2, 0, 3).reshape(CC, 4, 4 * B),
        "boxes": arr("fside_Bx4x4_0"),
        "spatial": arr("fside_S_0").reshape(SQ, 1),
    }
    names = {
        "L0_q": "L0_xattn_to_q_w", "L0_k": "L0_xattn_to_k_w", "L0_v": "L0_xattn_to_v_w",
        "L0_kip": "L0_xattn_to_k_ip_w", "L0_vip": "L0_xattn_to_v_ip_w", "L0_o": "L0_xattn_to_out_w",
        "S0_k": "L0_xattn_to_k_object_w", "S0_v": "L0_xattn_to_v_object_w",
        "S1_k": "L0_xattn_to_k_others_w", "S1_v": "L0_xattn_to_v_others_w",
        "L1_q": "L1_xattn_w_q", "L1_k": "L1_xattn_w_k", "L1_v": "L1_xattn_w_v", "L1_o": "L1_xattn_w_out",
        "S2_k": "L1_xattn_w_k_ip", "S2_v": "L1_xattn_w_v_ip",
        "L3_q": "L3_xattn_W_q", "L3_k": "L3_xattn_W_k", "L3_v": "L3_xattn_W_v", "L3_o": "L3_xattn_W_out",
        "S4_k": "L3_xattn_W_k_ip", "S4_v": "L3_xattn_W_v_ip",
    }
    for short, name in names.items():
        data[short] = arr(name)
    heads = [range(0, 16, 2), range(1, 16, 2), range(16, H)]
    by_channel = [D * h + c for tile in heads for c in range(D) for h in tile]
    names2 = {"L2_q": "Wq", "L2_k": "Wk", "L2_v": "Wv", "L2_kip": "Wk_ip", "L2_vip": "Wv_ip", "L2_o": "Wo"}
    for short, name in names2.items():
        data[short] = arr("L2_xattn_" + name).T
    for short in data:
        if short.endswith(("_q", "_k", "_kip")):
            data[short] = data[short][:, by_channel]
    biases = np.zeros((4, NT * 128), np.float32)
    for l, name in enumerate(["L0_xattn_to_out_b", "L1_xattn_b_out", "L2_xattn_bo", "L3_xattn_b_out"]):
        biases[l, :C] = arr(name)
    data["biases"] = biases.reshape(4, NT, 128).transpose(2, 0, 1)
    f = np.float32
    gh, gw = 8, 14
    data["ident"] = np.eye(128, dtype=f)
    data["head_mask"] = (np.arange(80)[:, None] // 4 == np.arange(C)[None, :] // D).astype(f)
    q = np.arange(SQ)
    data["grid"] = np.stack([(q % gw).astype(f) / f(gw - 1), (q // gw).astype(f) / f(gh - 1)], 1).astype(f)
    text = (np.arange(T) < TXT).astype(f)
    data["segments"] = np.stack([text, text, 1 - text, 1 - text])
    data["image_rows"] = np.stack([np.ones(128, f), (np.arange(128) >= TXT).astype(f)], 1)

    nc = bacc.Bacc("TRN2", target_bir_lowering=False, num_devices=1, dynamic_dma_scratch_size=512)
    arrays, ins = {}, {}
    for name, a in data.items():
        a = np.ascontiguousarray(a)
        arrays["in_" + name] = a
        ins[name] = nc.dram_tensor("in_" + name, a.shape, mybir.dt.from_np(a.dtype), kind="ExternalInput").ap()
    out_t = nc.dram_tensor("out_t", (B, C, SQ), F32, kind="ExternalOutput").ap()
    build(nc, ins, out_t)
    r = run_bass_kernel_spmd(nc, [arrays], core_ids=[0])
    return np.ascontiguousarray(r.results[0]["out_t"].transpose(0, 2, 1))
```
